# Optimizing a Trainium2 kernel written in Bass

```python
import numpy as np
import jax
import jax.numpy as jnp

def _softmax(x, axis=-1):
    return jax.nn.softmax(x, axis=axis)

def _gelu(x):
    return jax.nn.gelu(x, approximate=True)

def _silu(x):
    return jax.nn.silu(x)

def _sigmoid(x):
    return jax.nn.sigmoid(x)

def _layernorm(x, axis=-1, eps=1e-05):
    m = jnp.mean(x, axis=axis, keepdims=True)
    v = jnp.var(x, axis=axis, keepdims=True)
    return (x - m) / jnp.sqrt(v + eps)

def _scatter_add(tgt, idx, src, axis=0):
    return tgt.at[idx].add(src)

def _segment_sum(src, seg, n):
    return jax.ops.segment_sum(src, seg, n)
kernel_name = 'mk_gps_d1_gnn_r8_43d6e8'

def setup_inputs(seed: int=0):
    np.random.seed(seed)
    _w = jnp.asarray

    def _rec_inputs():
        import jax
        import jax.numpy as jnp
        _gk = jax.random.key(seed)
        x = -0.0002949 + 1 * jax.random.normal(jax.random.fold_in(_gk, 1), (1250, 512), jnp.float32)
        src = jax.random.randint(jax.random.fold_in(_gk, 2), (20000,), 0, 1250, jnp.int32)
        dst = jax.random.randint(jax.random.fold_in(_gk, 3), (20000,), 0, 1250, jnp.int32)
        _o = jnp.argsort(dst, stable=True)
        src = src[_o]
        dst = dst[_o]
        node_vec1 = jax.random.uniform(jax.random.fold_in(_gk, 12), (1250, 1), jnp.float32, 0.0, 0.999957)
        return (x, src, dst, node_vec1)
    x, src, dst, node_vec1 = _rec_inputs()

    def _L0_gnn_setup():
        import jax, jax.numpy as jnp
        import numpy as np
        N_NODES = 40962
        LATENT_DIM = 512
        N_EDGES = 81924
        NUM_BLOCKS = 4
        NUM_HEADS = 4
        NUM_FREQ = 32
        BASE_PERIOD = 16
        NOISE_EMB_DIM = 16
        EPS = 1e-05

        def _cond_layer_norm(x, cond, sw, sb, bw, bb):
            mu = jnp.mean(x, axis=-1, keepdims=True)
            var = jnp.var(x, axis=-1, keepdims=True)
            xn = (x - mu) * jax.lax.rsqrt(var + EPS)
            scale = cond @ sw + sb
            bias = cond @ bw + bb
            return xn * (1.0 + scale) + bias

        def _sparse_attention(x, src, dst, wq, bq, wk, bk, wv, bv, wo, bo):
            N, D = x.shape
            H, Dh = (NUM_HEADS, D // NUM_HEADS)
            q = (x @ wq + bq).reshape(N, H, Dh) * Dh ** (-0.5)
            k = (x @ wk + bk).reshape(N, H, Dh)
            v = (x @ wv + bv).reshape(N, H, Dh)
            scores = jnp.einsum('ehd,ehd->eh', q[src], k[dst])
            smax = jax.ops.segment_max(scores, src, num_segments=N)
            ex = jnp.exp(scores - smax[src])
            denom = jax.ops.segment_sum(ex, src, num_segments=N)
            attn = ex / denom[src]
            out = jax.ops.segment_sum(attn[:, :, None] * v[dst], src, num_segments=N)
            return out.reshape(N, D) @ wo + bo

        def _forward(x, edge_index, noise_levels, f_w1, f_b1, f_w2, f_b2, s1_w, s1_b, b1_w, b1_b, wq, bq, wk, bk, wv, bv, wo, bo, s2_w, s2_b, b2_w, b2_b, m_w1, m_b1, m_w2, m_b2):
            src, dst = (edge_index[0], edge_index[1])
            freqs = jnp.arange(1, NUM_FREQ + 1, dtype=x.dtype) * (2.0 * np.pi / BASE_PERIOD)
            ph = noise_levels * freqs
            emb = jnp.concatenate([jnp.sin(ph), jnp.cos(ph)], axis=-1)
            cond = jax.nn.silu(emb @ f_w1 + f_b1) @ f_w2 + f_b2
            for i in range(NUM_BLOCKS):
                y = _cond_layer_norm(x, cond, s1_w[i], s1_b[i], b1_w[i], b1_b[i])
                y = _sparse_attention(y, src, dst, wq[i], bq[i], wk[i], bk[i], wv[i], bv[i], wo[i], bo[i])
                x = x + y
                y = _cond_layer_norm(x, cond, s2_w[i], s2_b[i], b2_w[i], b2_b[i])
                y = jax.nn.relu(y @ m_w1[i] + m_b1[i]) @ m_w2[i] + m_b2[i]
                x = x + y
            return x
        key = jax.random.key(seed)
        ks = jax.random.split(key, 20)

        def w(k, shape, s=0.02):
            return jax.random.normal(k, shape, dtype=jnp.float32) * s
        D, B, C = (LATENT_DIM, NUM_BLOCKS, NOISE_EMB_DIM)
        z = lambda *s: jnp.zeros(s, jnp.float32)
        return {'latent_mesh_nodes': jax.random.normal(ks[0], (N_NODES, D), dtype=jnp.float32), 'edge_index': jax.random.randint(ks[1], (2, N_EDGES), 0, N_NODES, dtype=jnp.int32), 'noise_levels': jax.random.uniform(ks[2], (N_NODES, 1), dtype=jnp.float32), 'f_w1': w(ks[3], (2 * NUM_FREQ, C)), 'f_b1': z(C), 'f_w2': w(ks[4], (C, C)), 'f_b2': z(C), 's1_w': w(ks[5], (B, C, D)), 's1_b': z(B, D), 'b1_w': w(ks[6], (B, C, D)), 'b1_b': z(B, D), 'wq': w(ks[7], (B, D, D)), 'bq': z(B, D), 'wk': w(ks[8], (B, D, D)), 'bk': z(B, D), 'wv': w(ks[9], (B, D, D)), 'bv': z(B, D), 'wo': w(ks[10], (B, D, D)), 'bo': z(B, D), 's2_w': w(ks[11], (B, C, D)), 's2_b': z(B, D), 'b2_w': w(ks[12], (B, C, D)), 'b2_b': z(B, D), 'm_w1': w(ks[13], (B, D, D)), 'm_b1': z(B, D), 'm_w2': w(ks[14], (B, D, D)), 'm_b2': z(B, D)}
    _L0_gnn_all = _L0_gnn_setup()
    _L0_gnn_in = {k: v for k, v in _L0_gnn_all.items() if k in ('f_w1', 'f_b1', 'f_w2', 'f_b2', 's1_w', 's1_b', 'b1_w', 'b1_b', 'wq', 'bq', 'wk', 'bk', 'wv', 'bv', 'wo', 'bo', 's2_w', 's2_b', 'b2_w', 'b2_b', 'm_w1', 'm_b1', 'm_w2', 'm_b2')}
    del _L0_gnn_all

    def _L0_mix_setup():
        import jax, jax.numpy as jnp
        import numpy as np
        DIM = 512
        HEADS = 8
        DIM_HEAD = 64
        INNER = HEADS * DIM_HEAD
        EPS = 1e-05

        def _per_head_layernorm(t, gamma, beta):
            mu = jnp.mean(t, axis=-1, keepdims=True)
            var = jnp.mean(jnp.square(t - mu), axis=-1, keepdims=True)
            t_hat = (t - mu) * jax.lax.rsqrt(var + EPS)
            return t_hat * gamma[None, :, None, :] + beta[None, :, None, :]
        key = jax.random.key(seed)
        ks = jax.random.split(key, 6)
        x = jax.random.normal(ks[0], (4, 1024, DIM), dtype=jnp.float32)
        std_qkv = 0.0001 * np.sqrt(2.0 / (3 * INNER + DIM))
        W_qkv = jax.random.normal(ks[1], (3 * INNER, DIM), dtype=jnp.float32) * std_qkv
        gamma_K = jnp.ones((HEADS, DIM_HEAD), dtype=jnp.float32)
        beta_K = jnp.zeros((HEADS, DIM_HEAD), dtype=jnp.float32)
        gamma_V = jnp.ones((HEADS, DIM_HEAD), dtype=jnp.float32)
        beta_V = jnp.zeros((HEADS, DIM_HEAD), dtype=jnp.float32)
        std_out = np.sqrt(1.0 / INNER)
        W_out = jax.random.uniform(ks[2], (DIM, INNER), dtype=jnp.float32, minval=-std_out, maxval=std_out)
        b_out = jax.random.uniform(ks[3], (DIM,), dtype=jnp.float32, minval=-std_out, maxval=std_out)
        return {'x': x, 'W_qkv': W_qkv, 'gamma_K': gamma_K, 'beta_K': beta_K, 'gamma_V': gamma_V, 'beta_V': beta_V, 'W_out': W_out, 'b_out': b_out}
    _L0_mix_all = _L0_mix_setup()
    _L0_mix_in = {k: v for k, v in _L0_mix_all.items() if k in ('W_qkv', 'gamma_K', 'beta_K', 'gamma_V', 'beta_V', 'W_out', 'b_out')}
    del _L0_mix_all

    def _L0_ffn_setup():
        import jax, jax.numpy as jnp
        import numpy as np
        B, T, D = (4, 1024, 512)
        E, F, CAP = (8, 256, 512)
        key = jax.random.key(seed)
        ks = jax.random.split(key, 6)
        s = 0.02
        return {'x': jax.random.normal(ks[0], (B, T, D), dtype=jnp.float32), 'Wr': jax.random.normal(ks[1], (D, E), dtype=jnp.float32) * s, 'W1': jax.random.normal(ks[2], (E, D, F), dtype=jnp.float32) * s, 'b1': jax.random.normal(ks[3], (E, F), dtype=jnp.float32) * s, 'W2': jax.random.normal(ks[4], (E, F, D), dtype=jnp.float32) * s, 'b2': jax.random.normal(ks[5], (E, D), dtype=jnp.float32) * s}
    _L0_ffn_all = _L0_ffn_setup()
    _L0_ffn_in = {k: v for k, v in _L0_ffn_all.items() if k in ('Wr', 'W1', 'b1', 'W2', 'b2')}
    del _L0_ffn_all
    return {'x': x, 'src': src, 'dst': dst, 'node_vec1': node_vec1, 'L0_gnn_f_w1': _L0_gnn_in['f_w1'], 'L0_gnn_f_b1': _L0_gnn_in['f_b1'], 'L0_gnn_f_w2': _L0_gnn_in['f_w2'], 'L0_gnn_f_b2': _L0_gnn_in['f_b2'], 'L0_gnn_s1_w': _L0_gnn_in['s1_w'], 'L0_gnn_s1_b': _L0_gnn_in['s1_b'], 'L0_gnn_b1_w': _L0_gnn_in['b1_w'], 'L0_gnn_b1_b': _L0_gnn_in['b1_b'], 'L0_gnn_wq': _L0_gnn_in['wq'], 'L0_gnn_bq': _L0_gnn_in['bq'], 'L0_gnn_wk': _L0_gnn_in['wk'], 'L0_gnn_bk': _L0_gnn_in['bk'], 'L0_gnn_wv': _L0_gnn_in['wv'], 'L0_gnn_bv': _L0_gnn_in['bv'], 'L0_gnn_wo': _L0_gnn_in['wo'], 'L0_gnn_bo': _L0_gnn_in['bo'], 'L0_gnn_s2_w': _L0_gnn_in['s2_w'], 'L0_gnn_s2_b': _L0_gnn_in['s2_b'], 'L0_gnn_b2_w': _L0_gnn_in['b2_w'], 'L0_gnn_b2_b': _L0_gnn_in['b2_b'], 'L0_gnn_m_w1': _L0_gnn_in['m_w1'], 'L0_gnn_m_b1': _L0_gnn_in['m_b1'], 'L0_gnn_m_w2': _L0_gnn_in['m_w2'], 'L0_gnn_m_b2': _L0_gnn_in['m_b2'], 'L0_mix_W_qkv': _L0_mix_in['W_qkv'], 'L0_mix_gamma_K': _L0_mix_in['gamma_K'], 'L0_mix_beta_K': _L0_mix_in['beta_K'], 'L0_mix_gamma_V': _L0_mix_in['gamma_V'], 'L0_mix_beta_V': _L0_mix_in['beta_V'], 'L0_mix_W_out': _L0_mix_in['W_out'], 'L0_mix_b_out': _L0_mix_in['b_out'], 'L0_ffn_Wr': _L0_ffn_in['Wr'], 'L0_ffn_W1': _L0_ffn_in['W1'], 'L0_ffn_b1': _L0_ffn_in['b1'], 'L0_ffn_W2': _L0_ffn_in['W2'], 'L0_ffn_b2': _L0_ffn_in['b2']}

def reference(x, src, dst, node_vec1, L0_gnn_f_w1, L0_gnn_f_b1, L0_gnn_f_w2, L0_gnn_f_b2, L0_gnn_s1_w, L0_gnn_s1_b, L0_gnn_b1_w, L0_gnn_b1_b, L0_gnn_wq, L0_gnn_bq, L0_gnn_wk, L0_gnn_bk, L0_gnn_wv, L0_gnn_bv, L0_gnn_wo, L0_gnn_bo, L0_gnn_s2_w, L0_gnn_s2_b, L0_gnn_b2_w, L0_gnn_b2_b, L0_gnn_m_w1, L0_gnn_m_b1, L0_gnn_m_w2, L0_gnn_m_b2, L0_mix_W_qkv, L0_mix_gamma_K, L0_mix_beta_K, L0_mix_gamma_V, L0_mix_beta_V, L0_mix_W_out, L0_mix_b_out, L0_ffn_Wr, L0_ffn_W1, L0_ffn_b1, L0_ffn_W2, L0_ffn_b2):
    import jax
    import jax.numpy as jnp

    def _L0_gnn_ref(latent_mesh_nodes, edge_index, noise_levels, f_w1, f_b1, f_w2, f_b2, s1_w, s1_b, b1_w, b1_b, wq, bq, wk, bk, wv, bv, wo, bo, s2_w, s2_b, b2_w, b2_b, m_w1, m_b1, m_w2, m_b2):
        import jax, jax.numpy as jnp
        import numpy as np
        N_NODES = 40962
        LATENT_DIM = 512
        N_EDGES = 81924
        NUM_BLOCKS = 4
        NUM_HEADS = 4
        NUM_FREQ = 32
        BASE_PERIOD = 16
        NOISE_EMB_DIM = 16
        EPS = 1e-05

        def _cond_layer_norm(x, cond, sw, sb, bw, bb):
            mu = jnp.mean(x, axis=-1, keepdims=True)
            var = jnp.var(x, axis=-1, keepdims=True)
            xn = (x - mu) * jax.lax.rsqrt(var + EPS)
            scale = cond @ sw + sb
            bias = cond @ bw + bb
            return xn * (1.0 + scale) + bias

        def _sparse_attention(x, src, dst, wq, bq, wk, bk, wv, bv, wo, bo):
            N, D = x.shape
            H, Dh = (NUM_HEADS, D // NUM_HEADS)
            q = (x @ wq + bq).reshape(N, H, Dh) * Dh ** (-0.5)
            k = (x @ wk + bk).reshape(N, H, Dh)
            v = (x @ wv + bv).reshape(N, H, Dh)
            scores = jnp.einsum('ehd,ehd->eh', q[src], k[dst])
            smax = jax.ops.segment_max(scores, src, num_segments=N)
            ex = jnp.exp(scores - smax[src])
            denom = jax.ops.segment_sum(ex, src, num_segments=N)
            attn = ex / denom[src]
            out = jax.ops.segment_sum(attn[:, :, None] * v[dst], src, num_segments=N)
            return out.reshape(N, D) @ wo + bo

        def _forward(x, edge_index, noise_levels, f_w1, f_b1, f_w2, f_b2, s1_w, s1_b, b1_w, b1_b, wq, bq, wk, bk, wv, bv, wo, bo, s2_w, s2_b, b2_w, b2_b, m_w1, m_b1, m_w2, m_b2):
            src, dst = (edge_index[0], edge_index[1])
            freqs = jnp.arange(1, NUM_FREQ + 1, dtype=x.dtype) * (2.0 * np.pi / BASE_PERIOD)
            ph = noise_levels * freqs
            emb = jnp.concatenate([jnp.sin(ph), jnp.cos(ph)], axis=-1)
            cond = jax.nn.silu(emb @ f_w1 + f_b1) @ f_w2 + f_b2
            for i in range(NUM_BLOCKS):
                y = _cond_layer_norm(x, cond, s1_w[i], s1_b[i], b1_w[i], b1_b[i])
                y = _sparse_attention(y, src, dst, wq[i], bq[i], wk[i], bk[i], wv[i], bv[i], wo[i], bo[i])
                x = x + y
                y = _cond_layer_norm(x, cond, s2_w[i], s2_b[i], b2_w[i], b2_b[i])
                y = jax.nn.relu(y @ m_w1[i] + m_b1[i]) @ m_w2[i] + m_b2[i]
                x = x + y
            return x
        return _forward(latent_mesh_nodes, edge_index, noise_levels, f_w1, f_b1, f_w2, f_b2, s1_w, s1_b, b1_w, b1_b, wq, bq, wk, bk, wv, bv, wo, bo, s2_w, s2_b, b2_w, b2_b, m_w1, m_b1, m_w2, m_b2)

    def _L0_mix_ref(x, W_qkv, gamma_K, beta_K, gamma_V, beta_V, W_out, b_out):
        import jax, jax.numpy as jnp
        import numpy as np
        DIM = 512
        HEADS = 8
        DIM_HEAD = 64
        INNER = HEADS * DIM_HEAD
        EPS = 1e-05

        def _per_head_layernorm(t, gamma, beta):
            mu = jnp.mean(t, axis=-1, keepdims=True)
            var = jnp.mean(jnp.square(t - mu), axis=-1, keepdims=True)
            t_hat = (t - mu) * jax.lax.rsqrt(var + EPS)
            return t_hat * gamma[None, :, None, :] + beta[None, :, None, :]
        b, n, _ = x.shape
        qkv = jnp.einsum('bnd,ed->bne', x, W_qkv)
        q, k, v = jnp.split(qkv, 3, axis=-1)

        def to_heads(t):
            return t.reshape(b, n, HEADS, DIM_HEAD).transpose(0, 2, 1, 3)
        q, k, v = (to_heads(q), to_heads(k), to_heads(v))
        k = _per_head_layernorm(k, gamma_K, beta_K)
        v = _per_head_layernorm(v, gamma_V, beta_V)
        p_attn = jnp.einsum('bhnk,bhnv->bhkv', k, v) / n
        out = jnp.einsum('bhnk,bhkv->bhnv', q, p_attn)
        out = out.transpose(0, 2, 1, 3).reshape(b, n, INNER)
        return jnp.einsum('bne,de->bnd', out, W_out) + b_out

    def _L0_ffn_ref(x, Wr, W1, b1, W2, b2):
        import jax, jax.numpy as jnp
        import numpy as np
        B, T, D = (4, 1024, 512)
        E, F, CAP = (8, 256, 512)
        Bb, Tt, Dd = x.shape
        N = Bb * Tt
        C = min(CAP, N)
        x_flat = x.reshape(N, Dd)
        logits = x_flat @ Wr
        probs = jax.nn.softmax(logits, axis=0)
        vals, idx = jax.lax.top_k(probs.T, C)
        selected = x_flat[idx]
        h = jax.nn.gelu(jnp.einsum('ecd,edf->ecf', selected, W1) + b1[:, None, :], approximate=False)
        out_e = jnp.einsum('ecf,efd->ecd', h, W2) + b2[:, None, :]
        weighted = vals[..., None] * out_e
        output = jnp.zeros_like(x_flat).at[idx.reshape(-1)].add(weighted.reshape(-1, Dd))
        return output.reshape(Bb, Tt, Dd)
    edge_index = jnp.stack([src, dst])
    xn = _layernorm(x, axis=-1)
    x = x + _L0_gnn_ref(xn, edge_index, node_vec1, L0_gnn_f_w1, L0_gnn_f_b1, L0_gnn_f_w2, L0_gnn_f_b2, L0_gnn_s1_w, L0_gnn_s1_b, L0_gnn_b1_w, L0_gnn_b1_b, L0_gnn_wq, L0_gnn_bq, L0_gnn_wk, L0_gnn_bk, L0_gnn_wv, L0_gnn_bv, L0_gnn_wo, L0_gnn_bo, L0_gnn_s2_w, L0_gnn_s2_b, L0_gnn_b2_w, L0_gnn_b2_b, L0_gnn_m_w1, L0_gnn_m_b1, L0_gnn_m_w2, L0_gnn_m_b2) + _L0_mix_ref(xn[None], L0_mix_W_qkv, L0_mix_gamma_K, L0_mix_beta_K, L0_mix_gamma_V, L0_mix_beta_V, L0_mix_W_out, L0_mix_b_out)[0]
    x = x + _L0_ffn_ref(_layernorm(x, axis=-1)[None], L0_ffn_Wr, L0_ffn_W1, L0_ffn_b1, L0_ffn_W2, L0_ffn_b2)[0]
    return x

_drawn_inputs = setup_inputs


def setup_inputs(seed=0):
    import zlib

    import numpy as np

    out = dict(_drawn_inputs(seed))
    spreads = {'L0_gnn_f_b1': (0.0, 0.8),
     'L0_gnn_f_b2': (0.0, 0.8),
     'L0_gnn_s1_b': (0.0, 0.8),
     'L0_gnn_b1_b': (0.0, 0.39),
     'L0_gnn_bq': (0.0, 0.8),
     'L0_gnn_bk': (0.0, 2.0),
     'L0_gnn_bv': (0.0, 0.401),
     'L0_gnn_bo': (0.0, 0.1),
     'L0_gnn_s2_b': (0.0, 0.571),
     'L0_gnn_b2_b': (0.0, 0.565),
     'L0_gnn_m_b1': (0.0, 0.529),
     'L0_gnn_m_b2': (0.0, 0.1),
     'L0_mix_gamma_K': (1.0, 0.6),
     'L0_mix_beta_K': (0.0, 2.0),
     'L0_mix_gamma_V': (1.0, 0.6),
     'L0_mix_beta_V': (0.0, 2.0)}
    factors = {'node_vec1': 8.0,
     'L0_gnn_f_w1': 8.0,
     'L0_gnn_f_w2': 8.0,
     'L0_gnn_s1_w': 8.0,
     'L0_gnn_b1_w': 8.0,
     'L0_gnn_wq': 5.442,
     'L0_gnn_wk': 5.313,
     'L0_gnn_s2_w': 8.0,
     'L0_gnn_b2_w': 8.0,
     'L0_mix_W_qkv': 63.227,
     'L0_mix_W_out': 58.949,
     'L0_mix_b_out': 14.744,
     'L0_ffn_Wr': 22.631,
     'L0_ffn_W1': 25.381,
     'L0_ffn_b1': 200.0,
     'L0_ffn_W2': 8.0,
     'L0_ffn_b2': 200.0}
    for name, (base, spread) in spreads.items():
        noise = np.random.default_rng([zlib.crc32(name.encode()), seed]).standard_normal(out[name].shape)
        drawn = base * np.exp(spread * noise) if base else spread * noise
        out[name] = jnp.asarray(drawn.astype(out[name].dtype))
    for name, factor in factors.items():
        out[name] = (out[name] * factor).astype(out[name].dtype)
    return out
```

```python
from contextlib import ExitStack

import numpy as np

import concourse.bass as bass
from concourse import mybir

F32 = mybir.dt.float32
F32R = mybir.dt.float32r
BF16 = mybir.dt.bfloat16
I32 = mybir.dt.int32
U32 = mybir.dt.uint32
ALU = mybir.AluOpType
ACT = mybir.ActivationFunctionType
AX = mybir.AxisListType

N = 1250
D = 512
EDGES = 20000
BLOCKS = 4
HEADS = 4
DH = D // HEADS
TP = 125
NT = N // TP
KD = D // 128
CHUNKS = [(0, 500), (500, 500), (1000, 250)]
SW = 418
NPAD = 3 * SW
PAIRS = NT // 2
ET = EDGES // TP
TABLES = 2
TABLE = N * NPAD
EC = 40
COND = 16
MH, MD = 8, 64
EXPERTS, FF, CAP = 8, 256, 512
EPS = 1e-5
MASKED = -1e30
SCALE = float(DH) ** -0.5
TURN = 2.0 * np.pi
TURN_PARTS = [6.28125, 0.0019340515136718750, TURN - 6.28125 - 0.0019340515136718750]
ROUNDER = 1.5 * 2.0 ** 23
PI_BELOW = 3.1415925


def host_arrays(a):
    f = np.float32

    def kpn(w):
        return np.ascontiguousarray(w.reshape(KD, 128, -1).transpose(1, 0, 2).reshape(128, -1))

    g = {k[7:]: v for k, v in a.items() if k.startswith("L0_gnn_")}
    o = {"x": a["x"], "src": a["src"].reshape(80, 250), "dst": a["dst"].reshape(80, 250),
         "noise": a["node_vec1"].reshape(1, N)}
    o["ident"] = np.eye(128, dtype=f)
    freq = np.arange(1, 33, dtype=f) * f(2.0 * np.pi / 16)
    o["freq"] = np.concatenate([freq, freq]).reshape(64, 1)
    o["quarter"] = np.repeat(np.array([[0, 0], [0.25, np.pi / 2]], f), 32, axis=0)
    o["earlier"] = np.tril(np.ones((TP, TP), f), -1)
    o["trash"] = (TABLE + np.arange(TP)).astype(f).reshape(TP, 1)
    blk = np.zeros((128, 128), f)
    blk[:64, :64] = blk[64:, 64:] = 1.0 / N
    o["headmask"] = blk
    o["f_w1"], o["f_b1"] = g["f_w1"], g["f_b1"].reshape(COND, 1)
    w2, b2 = np.zeros((COND, 96), f), np.zeros((96, 1), f)
    for r in (0, 32, 64):
        w2[:, r:r + COND], b2[r:r + COND, 0] = g["f_w2"], g["f_b2"]
        b2[r + COND] = 1.0
    o["f_w2"], o["f_b2"] = w2, b2

    def affine(cols):
        m = np.zeros((96, 3 * D), f)
        for n, (w, b) in enumerate(cols):
            for r in (0, 32, 64):
                if w is not None:
                    m[r:r + COND, n * D:(n + 1) * D] = w
                if b is not None:
                    m[r + COND, n * D:(n + 1) * D] = b
        return m

    o["aff1"] = np.stack([affine([(g["s1_w"][n % 4], g["s1_b"][n % 4]), (g["b1_w"][n % 4], g["b1_b"][n % 4]),
                                  (None, g["m_b2"][n - 1] if n else None)]) for n in range(BLOCKS + 1)])
    o["aff2"] = np.stack([affine([(g["s2_w"][n], g["s2_b"][n]), (g["b2_w"][n], g["b2_b"][n]),
                                  (None, g["bo"][n])]) for n in range(BLOCKS)])
    qkv = np.stack([g["wq"], g["wk"], g["wv"]], 1).reshape(BLOCKS, 3, KD, 128, HEADS, DH)
    qkv = qkv.transpose(0, 4, 3, 1, 2, 5).reshape(BLOCKS * HEADS, 128, 3 * KD * DH)
    o["wqkv"] = np.ascontiguousarray(np.concatenate([qkv, qkv[:1]]))
    bias = np.stack([g["bq"], g["bk"], g["bv"], g["m_b1"]], 1).reshape(BLOCKS, 4, 4, 128)
    o["bias"] = np.ascontiguousarray(bias.transpose(0, 3, 1, 2).reshape(BLOCKS, 128, 16))
    o["wo"] = np.stack([kpn(w) for w in g["wo"]])
    o["w1"] = np.stack([kpn(w) for w in g["m_w1"]])
    o["w2"] = np.stack([kpn(w) for w in g["m_w2"]])
    wqkv = a["L0_mix_W_qkv"]
    o["mix_wk"], o["mix_wv"] = kpn(wqkv[D:2 * D].T), kpn(wqkv[2 * D:].T)
    o["mix_wq"] = kpn(wqkv[:D])
    o["mix_wo"] = kpn(a["L0_mix_W_out"].T)
    o["mix_bo"] = a["L0_mix_b_out"].reshape(1, D)
    o["mix_gk"], o["mix_bk"] = a["L0_mix_gamma_K"].reshape(1, D), a["L0_mix_beta_K"].reshape(1, D)
    o["mix_gv"] = a["L0_mix_gamma_V"].reshape(4, 128).T
    o["mix_bv"] = a["L0_mix_beta_V"].reshape(4, 128).T
    wr = np.zeros((D, 128), f)
    wr[:, :EXPERTS] = a["L0_ffn_Wr"]
    o["ffn_wr"] = kpn(wr)
    o["ffn_w1"] = np.stack([kpn(w) for w in a["L0_ffn_W1"]])
    o["ffn_w2"] = np.ascontiguousarray(
        a["L0_ffn_W2"].reshape(EXPERTS, 2, 128, D).transpose(0, 2, 1, 3).reshape(EXPERTS, 128, 2 * D))
    o["ffn_b1"] = a["L0_ffn_b1"].reshape(EXPERTS, 2, 128).transpose(2, 0, 1).reshape(128, 16)
    o["ffn_b2"] = a["L0_ffn_b2"]
    return {k: np.ascontiguousarray(v) for k, v in o.items()}


def groups_of(n):
    return [range(b, min(b + 4, n)) for b in range(0, n, 4)]


def build(nc, I, out):
    ctx = ExitStack()
    uniq = [0]

    def at(name, shape, dt, addr):
        uniq[0] += 1
        with ExitStack() as s:
            if addr:
                s.enter_context(nc.sbuf_tensor(f"below{uniq[0]}", [128, addr // 4], F32))
            return s.enter_context(nc.sbuf_tensor(name, shape, dt))

    with ctx:
        names = {}

        def sem(name):
            names[name] = ctx.enter_context(nc.semaphore(name))
            return names[name]

        L = at("L", [TP, NT, NPAD], F32, 0)
        ident = at("ident_s", [128, 128], F32, 50176)
        ones = at("ones", [128, 128], F32, 50688)
        condS = at("condS", [96, N], F32R, 51200)
        yT_hi = at("yT_hi", [128, KD, N], F32R, 56224)
        yT_lo = at("yT_lo", [128, KD, N], F32R, 76224)
        diag = at("diag", [TP, 4, TP], F32, 96224)
        rb = at("rb", [128, 250], F32, 98240)
        small = at("small", [128, 256], F32, 99264)
        stage = at("stage", [128, 1536], F32, 100288)
        R = 106432
        mv = small[0:TP, 0:2 * NT].rearrange("p (t s) -> p t s", s=2)
        ve = small[0:TP, 20:30]
        r0 = small[0:TP, 30:40]
        rt = small[0:TP, 40:50]
        rstd = small[0:TP, 50:60]
        st6 = small[0:TP, 60:72].rearrange("p (b s) -> p b s", b=2)
        halves = small[0:TP, 72:82]
        rowmax = small[0:TP, 82:92]
        negm = small[0:TP, 92:102]
        den = small[0:TP, 102:112]
        rden = small[0:TP, 112:122]
        dmax = small[0:TP, 122:132]
        lbias = small[:, 132:148]
        fsmall = small[0:64, 148:152]
        fb = small[0:96, 152:154]
        qT_hi = at("qT_hi", [128, N], F32R, R)
        qT_lo = at("qT_lo", [128, N], F32R, R + 5024)
        kT_hi = at("kT_hi", [128, NPAD], F32R, R + 10048)
        kT_lo = at("kT_lo", [128, NPAD], F32R, R + 15072)
        v_hi = at("v_hi", [TP, NT, DH], F32R, R + 20096)
        v_lo = at("v_lo", [TP, NT, DH], F32R, R + 25216)
        Pb = at("Pb", [128, 3, 1256], F32, R + 30336)
        vT = Pb[:, 2, 0:N]
        PT = at("PT", [TP, 2, NT, 250], F32R, R + 45408)
        PT_hi, PT_lo = PT[:, 0], PT[:, 1]
        oT = at("oT", [128, HEADS, N], F32, R + 65408)
        wA_hi = at("wA_hi", [128, 3, KD, DH], F32R, R + 85632)
        wA_lo = at("wA_lo", [128, 3, KD, DH], F32R, R + 91776)
        wo = at("wo_s", [128, KD, D], F32, R)
        aff2_hi = at("aff2_hi", [96, 3 * D], F32R, R + 8192)
        w1_hi = at("w1_hi", [128, KD, D], F32R, R + 20096)
        w1_lo = at("w1_lo", [128, KD, D], F32R, R + 28288)
        xh = at("xh", [TP, D], F32, R + 16384)
        y1 = at("y1", [TP, 2, D], F32, R + 36480)
        bS = at("bS", [TP, 2, D], F32, R + 40576)
        g = at("g", [TP, NT, D], F32, R + 44928)
        hT_hi = at("hT_hi", [128, KD, 500], F32R, R)
        hT_lo = at("hT_lo", [128, KD, 500], F32R, R + 65408)
        w2_hi = at("w2_hi", [128, KD, D], F32R, R + 73408)
        w2_lo = at("w2_lo", [128, KD, D], F32R, R + 8192)
        fT = at("fT", [128, 2, 500], F32, R + 81600)
        aff1_hi = at("aff1_hi", [96, 3 * D], F32R, R + 97920)
        keyB = at("keyB", [TP, 2, EC, TP], F32, 0)
        eq = at("eq", [TP, EC, TP], BF16, 40000)
        zrow = at("zrow", [TP, NPAD], F32, R + 32768)
        keyR = at("keyR", [80, 250], F32, R + 97920)
        srcR = at("srcR", [80, 2, 250], I32, R + 98944)
        keyC = at("keyC", [TP, 80, 2], F32, R + 100960)
        bef = at("bef", [TP, ET], F32, R + 101600)
        trash = at("trash_s", [TP, 1], F32, R + 102240)
        earlier = at("earlier_s", [TP, TP], F32, R + 102272)
        idxU = at("idxU", [TP, ET], U32, R + 104064)
        cnt = at("cnt", [TP, ET], F32, R + 104704)
        embT = at("embT", [64, N], F32, R + 69504)
        embK = at("embK", [64, N], F32, R + 74528)
        embI = at("embI", [64, N], I32, R + 79552)
        hid = at("hid", [COND, N], F32, R + 84576)
        condF = at("condF", [96, N], F32, R + 89600)
        fw1 = at("fw1", [64, COND], F32, R + 94624)
        fw2 = at("fw2", [COND, 96], F32, R + 94688)
        lt = at("lt", [TP, 3, 1256], F32, R)
        wk_hi = at("wk_hi", [128, KD, D], F32R, R)
        wk_lo = at("wk_lo", [128, KD, D], F32R, R + 8192)
        wv_hi = at("wv_hi", [128, KD, D], F32R, R + 16384)
        wv_lo = at("wv_lo", [128, KD, D], F32R, R + 24576)
        kvh = at("kvh", [TP, 2, 2, D], F32, R + 32768)
        kvq = at("kvq", [TP, 2, D], F32, R + 65408)
        kvc = at("kvc", [TP, 2, D], F32, R + 93120)
        mix_wo = at("mix_wo_s", [128, KD, D], F32, R + 69504)
        mix_wq = at("mix_wq_s", [128, KD, D], F32, R + 77696)
        mbo = at("mbo", [TP, D], F32, R + 85888)
        hmask = at("hmask", [128, 128], F32, R + 87936)
        mrow = at("mrow", [128, 2, D], F32, R + 88448)
        mcol = at("mcol", [128, 4, 4], F32, R + 92544)
        ms8 = at("ms8", [TP, 2, 5, MH], F32, R + 92608)
        pvk = at("pvk", [128, KD, 128], F32, R)
        pvu = at("pvu", [128, KD, 128], F32, R + 2048)
        pvw = at("pvw", [128, KD, D], F32, R + 4096)
        we_hi = at("we_hi", [128, KD, D], F32R, R + 16384)
        we_lo = at("we_lo", [128, KD, D], F32R, R + 24576)
        xr = at("xr", [TP, 2, D], F32, R + 65408)
        prB = at("prB", [TP, EXPERTS, N], F32, 0)
        prC = at("prC", [TP, NT, EXPERTS], F32, 40000)
        rank = at("rank", [TP, EXPERTS, NT, 3], F32, 40320)
        gate = at("gate", [TP, EXPERTS, NT], F32, 41280)
        gateT = at("gateT", [EXPERTS, N], F32, 41600)
        junk = at("junk", [TP, N], BF16, 46624)
        early2 = at("early2", [TP, TP], F32, 49152)
        eW2_lo = at("eW2_lo", [128, 2, D], F32R, 51200)
        xm = at("xm_s", [TP, 2, D], F32, R)
        fb2 = at("fb2", [EXPERTS, D], F32, R + 4096)
        fstat = at("fstat", [128, 32], F32, R + 6144)
        logT = at("logT", [EXPERTS, N], F32, R + 8192)
        prT = at("prT", [EXPERTS, N], F32, R + 13216)
        hE_hi = at("hE_hi", [128, 2, 2, N], F32R, R + 18240)
        wr_hi = at("wr_hi", [128, KD, 128], F32R, R + 38240)
        wr_lo = at("wr_lo", [128, KD, 128], F32R, R + 40288)
        hE_lo = at("hE_lo", [128, 2, 2, N], F32R, R + 65408)
        hF = at("hF", [128, 2, 500], F32, R + 85408)
        eW1_hi = at("eW1_hi", [128, KD, FF], F32R, R + 89408)
        eW1_lo = at("eW1_lo", [128, KD, FF], F32R, R + 93504)
        eW2_hi = at("eW2_hi", [128, 2, D], F32R, R + 97600)

        pS = ctx.enter_context(nc.psum_tensor("pS", [128, 3, 512], F32))
        pT = ctx.enter_context(nc.psum_tensor("pT", [128, 3, 512], F32))
        pO = ctx.enter_context(nc.psum_tensor("pO", [128, 512], F32))
        pJ = ctx.enter_context(nc.psum_tensor("pJ", [128, 512], F32))
        pOJ = [pJ, pO]

        tabs = [nc.dram_tensor(f"counts{k}", [TABLE + TP, 1], F32).ap() for k in range(TABLES)]
        keys_d = nc.dram_tensor("keys", [80, 250], F32).ap()
        g_d = nc.dram_tensor("g_spill", [N, D], F32).ap()
        xm_d = nc.dram_tensor("x_plus_mix", [N, D], F32).ap()
        pr_d = nc.dram_tensor("probs", [EXPERTS, N], F32).ap()

        ld_x, ld_edge, ld_cond, ld_ident, ld_mix, ld_mixw = [sem(n) for n in (
            "ld_x", "ld_edge", "ld_cond", "ld_ident", "ld_mix", "ld_mixw")]
        zeroed, keys_out = sem("tables_zeroed"), sem("keys_out")
        keyb_in = [sem(f"keyb_in{k}") for k in range(2)]
        stage_in, split_done = sem("stage_in"), sem("split_done")
        counted = [sem(f"counted{k}") for k in range(TABLES)]
        const_set, dchain, pchain = sem("const_set"), sem("dve_chain"), sem("pool_chain")
        key_rows, key_turn, key_cols, edge_idx = [sem(n) for n in (
            "key_rows", "key_turned", "key_cols", "edge_idx")]
        emb_arg, emb_sin, hid_mm, hid_act, cond_mm, cond_act, cond_done = [sem(n) for n in (
            "emb_arg", "emb_sin", "hid_mm", "hid_act", "cond_mm", "cond_act", "cond_done")]
        x_ve, x_pow, x_norm, x_turn, x_hi, x_lo = [sem(n) for n in (
            "x_ve", "x_pow", "x_norm", "x_turned", "x_hi", "x_lo")]
        kv_mm, kv_cent, kv_sq, kv_var, kv_std, kv_norm, kv_acc = [sem(n) for n in (
            "kv_mm", "kv_centred", "kv_squares", "kv_var", "kv_std", "kv_norm", "kv_acc")]
        pv_ready, pw_mm, pw_out, we_mm, we_h, we_l = [sem(n) for n in (
            "pv_ready", "pw_mm", "pw_out", "we_mm", "we_hi_done", "we_lo_done")]
        mix_mm, mix_add = sem("mix_mm"), sem("mix_add")
        xr_in = [sem(f"xr_in{k}") for k in range(2)]
        xm_out = [sem(f"xm_out{k}") for k in range(2)]
        lt_in = [[sem(f"lt_in{p}{k}") for k in range(TABLES)] for p in range(2)]
        l_max, l_ln, l_done = sem("l_max"), sem("l_ln"), sem("l_done")
        first_of_block = len(names)
        bstage_in, bsplit = sem("block_stage_in"), sem("block_split")
        bias_in, wo_in, g_out = sem("bias_in"), sem("wo_in"), sem("g_out")
        g_in = [sem("g_in0"), sem("g_in1")]
        qk_mm, qk_hi, qk_lo, v_mm, v_act = [sem(n) for n in ("qk_mm", "qk_hi", "qk_lo", "v_mm", "v_act")]
        scores, row_max, neg_max, exp_done, den_inv, diag_done = [sem(n) for n in (
            "scores", "row_max", "neg_max", "exp_done", "den_inverse", "diag_done")]
        turned, turn_hi, turn_lo = sem("turned"), sem("turn_hi"), sem("turn_lo")
        pv_mm, rb_copied, o_done = sem("pv_mm"), sem("rb_copied"), sem("o_done")
        proj, g_add, var_done, pow_done, aff_mm, bias_copied = [sem(n) for n in (
            "proj", "g_added", "var_done", "pow_done", "affine_mm", "bias_copied")]
        y_scaled, y_done, y_turn, y_hi, y_lo = [sem(n) for n in (
            "y_scaled", "y_done", "y_turned", "y_hi", "y_lo")]
        m1_mm, m1_hi, m1_lo = sem("m1_mm"), sem("m1_hi"), sem("m1_lo")
        lchain = sem("dve_block_chain")
        qchain = sem("pool_block_chain")
        cleared = list(names.values())[first_of_block:]
        block_done, block_seen, block_go = sem("block_done"), sem("block_seen"), sem("block_go")
        f_in = [sem("f_in0"), sem("f_in1")]
        f_add, f_ve, f_pow, f_norm, f_turn, f_hi, f_lo = [sem(n) for n in (
            "f_added", "f_ve", "f_pow", "f_norm", "f_turned", "f_hi", "f_lo")]
        f_ld, f_stage, f_split, f_log, f_logc, f_nmax, f_exp, f_prob = [sem(n) for n in (
            "f_ld", "f_stage_in", "f_split", "f_logits", "f_logits_out", "f_negmax", "f_exp", "f_prob")]
        f_store, f_prb, f_pturn, f_prc = [sem(n) for n in ("f_probs_out", "f_probs_in", "f_pturn", "f_prc")]
        f_m1, f_h, f_hlo, f_m2, f_acc, f_gate, f_gturn, f_gt, f_b2, f_fin, f_out = [sem(n) for n in (
            "f_m1", "f_h", "f_hlo", "f_m2", "f_acc", "f_gate", "f_gturn", "f_gateT", "f_b2", "f_fin", "f_out")]

        class Chain:

            def __init__(self, eng, s):
                self.eng, self.sem, self.n = eng, s, 0

            def link(self, ins):
                self.n += 1
                ins.then_inc(self.sem, 1)
                self.eng.wait_ge(self.sem, self.n)

        block = ctx.enter_context(nc.Block())

        def at_tile(ap, t):
            return ap[:, TP * t:TP * (t + 1)]

        mlp_order = []
        for c, (c0, cn) in enumerate(CHUNKS):
            mlp_order += [("m1", 4 * c + m) for m in range(4)]
            mlp_order += [("step", t) for t in range(c0 // TP, (c0 + cn) // TP)]
        mlp_order += [("step", NT), ("step", NT + 1)]
        uses = [("proj", t) for t in range(NT)]
        uses += [("m1", i) if k == "m1" else ("proj", NT + i) for k, i in mlp_order if k == "m1" or i < NT]
        use_of = {u: n for n, u in enumerate(uses)}
        (H1, AFF1, H2, H3, AFF2, W1A, W1B, W2A, W2B, NQ, NK, NV) = range(12)
        head_piece = {1: H1, 2: H2, 3: H3}

        @block.sync
        def _(sp):
            def stage_load(src, n, s_in, s_split):
                if n:
                    sp.wait_ge(s_split, n)
                sp.dma_start(stage[0:src.shape[0], 0:src.shape[1]], src).then_inc(s_in, 16)

            sp.dma_start(srcR[:, 0, :], I["src"]).then_inc(ld_edge, 16)
            sp.dma_start(srcR[:, 1, :], I["dst"]).then_inc(ld_edge, 16)
            sp.dma_start(trash[:], I["trash"]).then_inc(ld_edge, 16)
            sp.dma_start(earlier[:], I["earlier"]).then_inc(ld_edge, 16)
            sp.dma_start(ident[:], I["ident"]).then_inc(ld_ident, 16)
            sp.dma_start(g[:], I["x"].rearrange("(t p) d -> p t d", p=TP)).then_inc(ld_x, 16)
            sp.dma_start(embT[:], I["noise"].to_broadcast((64, N))).then_inc(ld_cond, 16)
            sp.dma_start(fsmall[:, 0:1], I["freq"]).then_inc(ld_cond, 16)
            sp.dma_start(fsmall[:, 1:3], I["quarter"]).then_inc(ld_cond, 16)
            sp.dma_start(fsmall[0:COND, 3:4], I["f_b1"]).then_inc(ld_cond, 16)
            sp.dma_start(fb[:, 0:1], I["f_b2"]).then_inc(ld_cond, 16)
            sp.dma_start(fw1[:], I["f_w1"]).then_inc(ld_cond, 16)
            sp.dma_start(fw2[:], I["f_w2"]).then_inc(ld_cond, 16)
            sp.wait_ge(key_rows, 1)
            sp.dma_start(keys_d, keyR[:]).then_inc(keys_out, 16)
            sp.wait_ge(keys_out, 16)
            flat = keys_d.rearrange("a b -> (a b)")

            def key_load(c):
                if c >= 2:
                    sp.wait_ge(edge_idx, c - 1)
                src = flat[c * EC * TP:(c + 1) * EC * TP].unsqueeze(0).to_broadcast((TP, EC * TP))
                sp.dma_start(keyB[:, c % 2].rearrange("p t j -> p (t j)"), src).then_inc(keyb_in[c % 2], 16)

            key_load(0)
            mixw = [I["mix_wk"][:, 0:1024], I["mix_wk"][:, 1024:], I["mix_wv"][:, 0:1024], I["mix_wv"][:, 1024:]]
            pieces = mixw + [I["aff1"][0], I["wqkv"][0]]
            stage_load(pieces[0], 0, stage_in, split_done)
            key_load(1)
            sp.wait_ge(const_set, 3)
            for tab in tabs:
                body = tab[0:TABLE, :].rearrange("(t p c) o -> p t (c o)", t=NT, p=TP)
                sp.dma_start(body, zrow[:].unsqueeze(1).to_broadcast((TP, NT, NPAD))).then_inc(zeroed, 16)
                sp.dma_start(tab[TABLE:, :].rearrange("p o -> o p"), zrow[0:1, 0:TP]).then_inc(zeroed, 16)
            stage_load(pieces[1], 1, stage_in, split_done)
            key_load(2)
            stage_load(pieces[2], 2, stage_in, split_done)
            key_load(3)
            stage_load(pieces[3], 3, stage_in, split_done)
            sp.wait_ge(cond_done, 2)
            sp.dma_start(mix_wo[:].rearrange("p k n -> p (k n)"), I["mix_wo"]).then_inc(ld_mix, 16)
            sp.dma_start(mix_wq[:].rearrange("p k n -> p (k n)"), I["mix_wq"]).then_inc(ld_mix, 16)
            sp.dma_start(mbo[:], I["mix_bo"].to_broadcast((TP, D))).then_inc(ld_mix, 16)
            sp.dma_start(hmask[:], I["headmask"]).then_inc(ld_mix, 16)
            sp.dma_start(mrow[:, 0, :], I["mix_gk"].to_broadcast((128, D))).then_inc(ld_mix, 16)
            sp.dma_start(mrow[:, 1, :], I["mix_bk"].to_broadcast((128, D))).then_inc(ld_mix, 16)
            sp.dma_start(mcol[:, 0, :], I["mix_gv"]).then_inc(ld_mix, 16)
            sp.dma_start(mcol[:, 1, :], I["mix_bv"]).then_inc(ld_mix, 16)
            sp.wait_ge(kv_acc, NT)
            for t in range(NT + 2):
                if t >= 2:
                    sp.wait_ge(mix_add, t - 1)
                    sp.dma_start(xm_d[TP * (t - 2):TP * (t - 1), :], xr[:, t % 2, :]).then_inc(xm_out[t % 2], 16)
                if t < NT:
                    if t >= 2:
                        sp.wait_ge(xm_out[t % 2], 16 * (t // 2))
                    sp.dma_start(xr[:, t % 2, :], I["x"][TP * t:TP * (t + 1), :]).then_inc(xr_in[t % 2], 16)
            stage_load(pieces[4], 4, stage_in, split_done)
            sp.wait_ge(x_norm, NT)
            sp.dma_start(g_d.rearrange("(t p) d -> p t d", p=TP), g[:]).then_inc(ld_mixw, 16)
            for k in range(TABLES):
                sp.wait_ge(counted[k], 16 * (ET // TABLES))
            for t in range(NT):
                if t >= 1:
                    sp.wait_ge(l_done, t)
                for k in range(TABLES):
                    rows = tabs[k][0:TABLE, :].rearrange("(t p c) o -> t p (c o)", t=NT, p=TP)[t]
                    dst = L[:, t, :] if k == 0 else lt[:, k - 1, 0:NPAD]
                    sp.dma_start(dst, rows).then_inc(lt_in[t % 2][k], 16)
            stage_load(pieces[5], 5, stage_in, split_done)
            sp.wait_ge(ld_mixw, 16)
            for k in range(2):
                sp.wait_ge(xm_out[k], 16 * (NT // 2))

            def between(n):
                sp.wait_ge(block_done, 4 * n)
                for s in cleared:
                    sp.sem_clear(s)
                sp.sem_inc(block_go, 1)

            between(1)
            with sp.Fori(0, BLOCKS) as l:
                def one(name, n=1, off=0):
                    return I[name][bass.ds(n * l + off, 1)].rearrange("a p f -> (a p) f")

                sp.dma_start(lbias[:], one("bias")).then_inc(bias_in, 16)
                stage_load(one("wqkv", HEADS, 1), H1, bstage_in, bsplit)
                stage_load(one("aff1", 1, 1), AFF1, bstage_in, bsplit)
                stage_load(one("wqkv", HEADS, 2), H2, bstage_in, bsplit)
                stage_load(one("wqkv", HEADS, 3), H3, bstage_in, bsplit)
                stage_load(one("aff2"), AFF2, bstage_in, bsplit)
                sp.wait_ge(scores, NT * HEADS)
                sp.dma_start(wo[:].rearrange("p k n -> p (k n)"), one("wo")).then_inc(wo_in, 16)
                stage_load(one("w1")[:, 0:1024], W1A, bstage_in, bsplit)
                sp.wait_ge(pv_mm, PAIRS * HEADS)
                gv = g_d.rearrange("(t p) d -> p t d", p=TP)
                sp.dma_start(g[:, 0:2, :], gv[:, 0:2, :]).then_inc(g_in[0], 16)
                sp.dma_start(g[:, 2:NT, :], gv[:, 2:NT, :]).then_inc(g_in[1], 16)
                stage_load(one("w1")[:, 1024:], W1B, bstage_in, bsplit)
                stage_load(one("w2")[:, 0:1024], W2A, bstage_in, bsplit)
                stage_load(one("w2")[:, 1024:], W2B, bstage_in, bsplit)
                nxt = one("wqkv", HEADS, 4)
                for t in range(NT):
                    if t in (0, 4, 6):
                        j = (0, 4, 6).index(t)
                        stage_load(nxt[:, 512 * j:512 * (j + 1)], NQ + j, bstage_in, bsplit)
                    sp.wait_ge(g_add, NT + t + 1)
                    sp.dma_start(g_d[TP * t:TP * (t + 1), :], g[:, t, :]).then_inc(g_out, 16)
                sp.wait_ge(block_done, 4 * l + 8)
                sp.sem_inc(block_seen, 1)
                sp.wait_ge(g_out, 16 * NT)
                for s in cleared:
                    sp.sem_clear(s)
                sp.sem_inc(block_go, 1)
            sp.dma_start(fb2[:], I["ffn_b2"]).then_inc(f_ld, 16)
            sp.dma_start(fstat[:, 0:16], I["ffn_b1"]).then_inc(f_ld, 16)
            sp.dma_start(early2[:], I["earlier"]).then_inc(f_ld, 16)
            for t in range(NT):
                if t >= 2:
                    sp.wait_ge(f_add, t - 1)
                sp.dma_start(xm[:, t % 2, :], xm_d[TP * t:TP * (t + 1), :]).then_inc(f_in[t % 2], 16)
            fpieces = [I["ffn_wr"]]
            for e in range(EXPERTS):
                fpieces += [I["ffn_w1"][e], I["ffn_w2"][e]]
            for n in range(3):
                stage_load(fpieces[n], n, f_stage, f_split)
            sp.wait_ge(f_prob, 1)
            sp.dma_start(pr_d, prT[:]).then_inc(f_store, 16)
            sp.wait_ge(f_store, 16)
            sp.dma_start(prB[:].rearrange("p e n -> p (e n)"),
                         pr_d.rearrange("e n -> (e n)").unsqueeze(0).to_broadcast((TP, EXPERTS * N))
                         ).then_inc(f_prb, 16)
            for n in range(3, len(fpieces)):
                stage_load(fpieces[n], n, f_stage, f_split)
            for t in range(NT):
                sp.wait_ge(f_fin, t + 1)
                sp.dma_start(out[TP * t:TP * (t + 1), :], g[:, t, :]).then_inc(f_out, 16)
            sp.wait_ge(f_out, 16 * NT)

        @block.gpsimd
        def _(pool):
            ch = outer = Chain(pool, pchain)

            def split(hi, lo, n, s_in, s_done, cols, rows=128):
                pool.wait_ge(s_in, 16 * (n + 1))
                src = stage[0:rows, 0:cols]
                ch.link(pool.tensor_copy(hi, src))
                pool.tensor_tensor(lo, src, hi.bitcast(F32), ALU.subtract).then_inc(s_done, 1)

            def split_affine(dst, n, s_in, s_done):
                pool.wait_ge(s_in, 16 * (n + 1))
                ch.link(pool.tensor_copy(dst[:], stage[0:96, :]))
                low = dst[64:96, :]
                pool.tensor_tensor(low, stage[64:96, :], low.bitcast(F32), ALU.subtract).then_inc(s_done, 1)
                pool.wait_ge(s_done, n + 1)

            def flat(ap, a, b):
                return ap[:].rearrange("p k n -> p (k n)")[:, a:b]

            def rsqrt(dst, src, n, s_in, n_in, s_out):
                pool.wait_ge(s_in, n_in)
                pool.tensor_tensor(dst, src, halves[:, 0:n], ALU.pow).then_inc(s_out, 1)

            def ln_step(base, s):
                if s < NT:
                    rsqrt(r0[:, s:s + 1], ve[:, s:s + 1], 1, var_done, base + s + 1, pow_done)
                if 1 <= s <= NT:
                    t = s - 1
                    pool.wait_ge(y_scaled, base + t + 1)
                    pool.wait_ge(bias_copied, base + t + 1)
                    pool.tensor_tensor(y1[:, t % 2, :], y1[:, t % 2, :], bS[:, t % 2, :], ALU.add
                                       ).then_inc(y_done, 1)

            pool.wait_ge(const_set, 1)
            rsqrt(r0, ve, NT, x_ve, 1, x_pow)
            split(flat(wk_hi, 0, 1024), flat(wk_lo, 0, 1024), 0, stage_in, split_done, 1024)
            split(flat(wk_hi, 1024, 2048), flat(wk_lo, 1024, 2048), 1, stage_in, split_done, 1024)
            split(flat(wv_hi, 0, 1024), flat(wv_lo, 0, 1024), 2, stage_in, split_done, 1024)
            split(flat(wv_hi, 1024, 2048), flat(wv_lo, 1024, 2048), 3, stage_in, split_done, 1024)
            pool.wait_ge(zeroed, 32 * TABLES)
            for T in range(ET):
                if T % EC == 0:
                    pool.wait_ge(edge_idx, T // EC + 1)
                k = T % TABLES
                if T >= TABLES:
                    pool.wait_ge(counted[k], 16 * (T // TABLES))
                pool.indirect_dma_start(tabs[k], bass.IndirectOffsetOnAxis(ap=idxU[:, T:T + 1], axis=0),
                                        cnt[:, T:T + 1], None, compute_op=ALU.add,
                                        bounds_check=TABLE + TP - 1).then_inc(counted[k], 16)
            for k in range(TABLES):
                pool.wait_ge(counted[k], 16 * (ET // TABLES))
            split_affine(aff1_hi, 4, stage_in, split_done)
            for s in range(NT + 2):
                ln_step(0, s)
            pool.wait_ge(mix_add, NT)
            wA = lambda ap, a, b: ap[:].rearrange("p w k n -> p (w k n)")[:, a:b]
            split(wA(wA_hi, 0, 1536), wA(wA_lo, 0, 1536), 5, stage_in, split_done, 1536)
            pool.drain().then_inc(block_done, 1)
            pool.wait_ge(block_go, 1)
            with pool.Fori(0, BLOCKS) as l:
                ch = Chain(pool, qchain)
                for h in (1, 2, 3):
                    pool.wait_ge(v_mm, 3 * h)
                    split(wA(wA_hi, 0, 1536), wA(wA_lo, 0, 1536), head_piece[h], bstage_in, bsplit, 1536)
                    if h == 1:
                        split_affine(aff1_hi, AFF1, bstage_in, bsplit)
                pool.wait_ge(scores, NT * HEADS)
                split_affine(aff2_hi, AFF2, bstage_in, bsplit)
                pool.wait_ge(pv_mm, PAIRS * HEADS)
                split(flat(w1_hi, 0, 1024), flat(w1_lo, 0, 1024), W1A, bstage_in, bsplit, 1024)
                for s in range(NT + 2):
                    ln_step(0, s)
                    if s == 2:
                        split(flat(w1_hi, 1024, 2048), flat(w1_lo, 1024, 2048), W1B, bstage_in, bsplit, 1024)
                pool.wait_ge(proj, NT)
                pool.wait_ge(aff_mm, NT)
                split(flat(w2_hi, 0, 1024), flat(w2_lo, 0, 1024), W2A, bstage_in, bsplit, 1024)
                split(flat(w2_hi, 1024, 2048), flat(w2_lo, 1024, 2048), W2B, bstage_in, bsplit, 1024)
                for s in range(NT + 2):
                    ln_step(NT, s)
                    if s in (3, 5, 7):
                        j = (3, 5, 7).index(s)
                        split(wA(wA_hi, 512 * j, 512 * (j + 1)), wA(wA_lo, 512 * j, 512 * (j + 1)),
                              NQ + j, bstage_in, bsplit, 512)
                pool.drain().then_inc(block_done, 1)
                pool.wait_ge(block_go, l + 2)
            ch = outer
            rsqrt(r0, ve, NT, f_ve, 1, f_pow)
            split(wr_hi[:].rearrange("p k n -> p (k n)"), wr_lo[:].rearrange("p k n -> p (k n)"),
                  0, f_stage, f_split, 512)
            for e in range(EXPERTS):
                if e:
                    pool.wait_ge(f_m1, 6 * e)
                split(flat(eW1_hi, 0, 1024), flat(eW1_lo, 0, 1024), 1 + 2 * e, f_stage, f_split, 1024)
                if e:
                    pool.wait_ge(f_m2, NT * e)
                split(flat(eW2_hi, 0, 1024), flat(eW2_lo, 0, 1024), 2 + 2 * e, f_stage, f_split, 1024)

        @block.tensor
        def _(pe):
            def mm3(dst, lhs, rhs, first, last):
                (lh, ll), (rh, rl) = lhs, rhs
                pe.matmul(dst, lh, rh, start=first, stop=False)
                pe.matmul(dst, lh, rl, start=False, stop=False)
                return pe.matmul(dst, ll, rh, start=False, stop=last)

            def turn(dst, src, n):
                for k in range(KD):
                    mm = pe.transpose(dst[:, n * k:n * (k + 1)], src[:, 128 * k:128 * (k + 1)], ident[0:n, 0:n])
                return mm

            def y_tile(k, t):
                return at_tile(yT_hi[:, k, :], t), at_tile(yT_lo[:, k, :], t)

            def affine(aff, G, t):
                if G:
                    pe.wait_ge(y_scaled, G)
                    pe.wait_ge(bias_copied, G)
                pe.matmul(pS[0:TP, 0, :], at_tile(condS, t), aff[:, 0:D], start=True, stop=True)
                pe.matmul(pS[0:TP, 1, :], at_tile(condS, t), aff[:, D:2 * D], start=True, stop=True
                          ).then_inc(aff_mm, 1)

            def ln_turn(G, t):
                pe.wait_ge(y_done, G + 1)
                if G >= 3:
                    pe.wait_ge(y_lo, G - 2)
                turn(pT[:, G % 3, :], y1[:, t % 2, :], TP).then_inc(y_turn, 1)

            pe.wait_ge(ld_ident, 16)
            pe.wait_ge(key_rows, 1)
            for b in range(2):
                pe.transpose(pOJ[b][0:TP, 0:80], keyR[:, TP * b:TP * (b + 1)], ident[0:80, 0:80]).then_inc(key_turn, 1)
            pe.wait_ge(ld_cond, 16 * 7)
            pe.wait_ge(emb_sin, 1)
            for c, (c0, cn) in enumerate(CHUNKS):
                pe.matmul(pS[0:COND, c, 0:cn], fw1[:], embT[:, c0:c0 + cn], start=True, stop=True).then_inc(hid_mm, 1)
            for c, (c0, cn) in enumerate(CHUNKS):
                pe.wait_ge(hid_act, c + 1)
                pe.matmul(pT[0:96, c, 0:cn], fw2[:], hid[:, c0:c0 + cn], start=True, stop=True).then_inc(cond_mm, 1)
            pe.wait_ge(cond_act, 3)
            for t in range(NT):
                pe.wait_ge(x_norm, t + 1)
                if t >= 3:
                    pe.wait_ge(x_lo, t - 2)
                turn(pT[:, t % 3, :], g[:, t, :], TP).then_inc(x_turn, 1)
            pe.wait_ge(split_done, 4)
            pe.wait_ge(key_cols, 2)
            pe.wait_ge(const_set, 2)

            def kv_products(t):
                pe.wait_ge(kv_norm, t + 1)
                k, v = kvh[:, t % 2, 0, :], kvh[:, t % 2, 1, :]
                for p in range(4):
                    cols = slice(128 * p, 128 * (p + 1))
                    pe.matmul(pT[:, 0, cols], v[:, cols], k[:, cols], start=(t == 0 and p == 0),
                              stop=(t == NT - 1), skip_group_check=True)
                    pe.matmul(pT[:, 1, p:p + 1], v[:, cols], ones[0:TP, 0:1], start=(t == 0 and p == 0),
                              stop=(t == NT - 1), skip_group_check=True)
                pe.matmul(pT[:, 2, :], ones[0:TP, :], k, start=(t == 0), stop=(t == NT - 1)).then_inc(kv_acc, 1)

            for t in range(NT):
                pe.wait_ge(x_lo, t + 1)
                if t >= 2:
                    pe.wait_ge(kv_cent, t - 1)
                for k in range(KD):
                    mm3(pS[0:TP, t % 2, :], y_tile(k, t), (wk_hi[:, k, :], wk_lo[:, k, :]), k == 0, k == KD - 1)
                for k in range(KD):
                    mm = mm3(pOJ[t % 2][0:TP, :], y_tile(k, t), (wv_hi[:, k, :], wv_lo[:, k, :]), k == 0, k == KD - 1)
                mm.then_inc(kv_mm, 1)
                if t == 0:
                    pe.wait_ge(x_lo, NT)
                if t:
                    kv_products(t - 1)
            kv_products(NT - 1)
            banks4 = [pS[:, 0, :], pS[:, 1, :], pS[:, 2, :], pJ[:, :]]
            pe.wait_ge(ld_mix, 16 * 8)
            pe.wait_ge(pv_ready, 1)
            for p in range(4):
                pe.matmul(banks4[p], pvk[:, p, :], mix_wo[:, p, :], start=True, stop=True).then_inc(pw_mm, 1)
            for m in range(4):
                pe.wait_ge(pw_out, 4)
                for p in range(4):
                    mm = pe.matmul(banks4[m], mix_wq[:, p, 128 * m:128 * (m + 1)], pvw[:, p, :],
                                   start=(p == 0), stop=(p == 3))
                mm.then_inc(we_mm, 1)
            pe.wait_ge(we_l, 4)
            for t in range(NT):
                if t >= 2:
                    pe.wait_ge(mix_add, t - 1)
                for k in range(KD):
                    mm = mm3(pOJ[t % 2][0:TP, :], y_tile(k, t), (we_hi[:, k, :], we_lo[:, k, :]), k == 0, k == KD - 1)
                mm.then_inc(mix_mm, 1)
            pe.wait_ge(cond_done, 2)
            pe.wait_ge(split_done, 5)
            for s in range(NT + 2):
                if 1 <= s <= NT:
                    affine(aff1_hi, s - 1, s - 1)
                if s >= 2:
                    ln_turn(s - 2, s - 2)
            pe.drain().then_inc(block_done, 1)
            pe.wait_ge(block_go, 1)

            with pe.Fori(0, BLOCKS) as l:
                def qk_group(h, n):
                    w, c = divmod(n, 3)
                    c0, cn = CHUNKS[c]
                    if w == 1:
                        pe.wait_ge(qk_lo, 6 * h + c + 1)
                    elif h and c == 0:
                        pe.wait_ge(bsplit, head_piece[h] + 1)
                        pe.wait_ge(row_max, NT * h)
                    for k in range(KD):
                        mm = mm3(pS[:, c, 0:cn], (wA_hi[:, w, k, :], wA_lo[:, w, k, :]),
                                 (yT_hi[:, k, c0:c0 + cn], yT_lo[:, k, c0:c0 + cn]), k == 0, k == KD - 1)
                    mm.then_inc(qk_mm, 1)

                def v_group(h, c):
                    c0, cn = CHUNKS[c]
                    if c == 1 and h:
                        pe.wait_ge(o_done, PAIRS * h)
                    if c == 2 or h:
                        pe.wait_ge(v_act, 3 * h + (1 if c == 2 else 0))
                    for k in range(KD):
                        mm = mm3(pOJ[c % 2][:, 0:cn], (wA_hi[:, 2, k, :], wA_lo[:, 2, k, :]),
                                 (yT_hi[:, k, c0:c0 + cn], yT_lo[:, k, c0:c0 + cn]), k == 0, k == KD - 1)
                    mm.then_inc(v_mm, 1)

                def score(h, i):
                    if i == 0:
                        pe.wait_ge(qk_lo, 6 * h + 6)
                    else:
                        pe.wait_ge(row_max, NT * h + i)
                    for c in range(3):
                        cols = slice(SW * c, SW * (c + 1))
                        mm = mm3(pS[0:TP, c, 0:SW], (at_tile(qT_hi, i), at_tile(qT_lo, i)),
                                 (kT_hi[:, cols], kT_lo[:, cols]), True, True)
                    mm.then_inc(scores, 1)

                def turn_v(h):
                    pe.wait_ge(v_act, 3 * h + 3)
                    for j, ts in enumerate(groups_of(NT)):
                        if h:
                            pe.wait_ge(turn_lo, 33 * h + j - 2)
                        for t in ts:
                            mm = pe.transpose(pT[0:TP, j, 128 * (t % 4):128 * (t % 4 + 1)],
                                              at_tile(vT, t), ident[:, :])
                        mm.then_inc(turned, 1)

                def turn_p(h, i):
                    pe.wait_ge(exp_done, NT * h + i + 1)
                    for j, bs in enumerate(groups_of(NT)):
                        G = 33 * h + 3 + 3 * i + j
                        pe.wait_ge(turn_lo, G - 2)
                        for b in bs:
                            mm = pe.transpose(pT[0:TP, j, TP * (b % 4):TP * (b % 4 + 1)],
                                              at_tile(Pb[0:TP, i % 3, :], b), ident[0:TP, 0:TP])
                        mm.then_inc(turned, 1)

                def pv(h, p):
                    pe.wait_ge(turn_lo, 33 * h + 9 + 6 * p)
                    if p:
                        pe.wait_ge(o_done, PAIRS * h + p)
                    else:
                        pe.wait_ge(v_act, 3 * h + 2)
                    for b in range(NT):
                        mm3(pO[:, 0:250], (v_hi[:, b, :], v_lo[:, b, :]), (PT_hi[:, b, :], PT_lo[:, b, :]),
                            b == 0, b == NT - 1)
                    pe.wait_ge(diag_done, NT * h + 2 * p + 2)
                    for u in range(2):
                        mm = pe.matmul(pO[:, 250 + TP * u:250 + TP * (u + 1)], ones[0:TP, :],
                                       diag[:, (2 * p + u) % 4, :], start=True, stop=True)
                    mm.then_inc(pv_mm, 1)

                for c in range(3):
                    qk_group(0, c)
                for h in range(HEADS):
                    for c in range(3):
                        qk_group(h, 3 + c)
                    v_group(h, 0)
                    score(h, 0)
                    v_group(h, 1)
                    v_group(h, 2)
                    score(h, 1)
                    turn_v(h)
                    for i in range(2, NT):
                        score(h, i)
                        if i >= 4 and i % 2 == 0:
                            pv(h, i // 2 - 2)
                        turn_p(h, i - 2)
                    nxt = [lambda c=c: qk_group(h + 1, c) for c in range(3)] if h + 1 < HEADS else [lambda: None] * 3
                    nxt[0]()
                    pv(h, 3)
                    turn_p(h, 8)
                    nxt[1]()
                    turn_p(h, 9)
                    nxt[2]()
                    pv(h, 4)

                def bank(use):
                    n = use_of[use]
                    if n >= 2:
                        kind, i = uses[n - 2]
                        pe.wait_ge(m1_hi if kind == "m1" else g_add, i + 1)
                    return pOJ[n % 2]

                def out_proj(t):
                    if t == 0:
                        pe.wait_ge(o_done, PAIRS * HEADS)
                        pe.wait_ge(wo_in, 16)
                        pe.wait_ge(bsplit, AFF2 + 1)
                    dst = bank(("proj", t))[0:TP, :]
                    pe.matmul(dst, at_tile(condS, t), aff2_hi[:, 2 * D:], start=True, stop=False)
                    for k in range(KD):
                        mm = pe.matmul(dst, at_tile(oT[:, k, :], t), wo[:, k, :], start=False, stop=(k == KD - 1))
                    mm.then_inc(proj, 1)

                def mlp_out(t):
                    c = [i for i, (c0, cn) in enumerate(CHUNKS) if c0 <= TP * t < c0 + cn][0]
                    t0 = TP * t - CHUNKS[c][0]
                    if t == 0:
                        pe.wait_ge(bsplit, W2B + 1)
                    pe.wait_ge(m1_lo, 4 * (c + 1))
                    dst = bank(("proj", NT + t))[0:TP, :]
                    pe.matmul(dst, at_tile(condS, t), aff1_hi[:, 2 * D:], start=True, stop=False)
                    for k in range(KD):
                        mm = mm3(dst, (hT_hi[:, k, t0:t0 + TP], hT_lo[:, k, t0:t0 + TP]),
                                 (w2_hi[:, k, :], w2_lo[:, k, :]), False, k == KD - 1)
                    mm.then_inc(proj, 1)

                def mlp_in(i):
                    c, m = divmod(i, 4)
                    c0, cn = CHUNKS[c]
                    if i == 0:
                        pe.wait_ge(bsplit, W1B + 1)
                    pe.wait_ge(y_lo, (c0 + cn) // TP)
                    dst = bank(("m1", i))[:, 0:cn]
                    cols = slice(128 * m, 128 * (m + 1))
                    for k in range(KD):
                        mm = mm3(dst, (w1_hi[:, k, cols], w1_lo[:, k, cols]),
                                 (yT_hi[:, k, c0:c0 + cn], yT_lo[:, k, c0:c0 + cn]), k == 0, k == KD - 1)
                    mm.then_inc(m1_mm, 1)

                for s in range(NT + 2):
                    if s < NT:
                        out_proj(s)
                    if 1 <= s <= NT:
                        affine(aff2_hi, s - 1, s - 1)
                    if s >= 2:
                        ln_turn(s - 2, s - 2)
                for kind, i in mlp_order:
                    if kind == "m1":
                        mlp_in(i)
                        continue
                    if i < NT:
                        mlp_out(i)
                    if 1 <= i <= NT:
                        affine(aff1_hi, NT + i - 1, i - 1)
                    if i >= 2:
                        ln_turn(NT + i - 2, i - 2)
                pe.drain().then_inc(block_done, 1)
                pe.wait_ge(block_go, l + 2)

            for t in range(NT):
                pe.wait_ge(f_norm, t + 1)
                if t >= 3:
                    pe.wait_ge(f_lo, t - 2)
                turn(pT[:, t % 3, :], xm[:, t % 2, :], TP).then_inc(f_turn, 1)
            pe.wait_ge(f_split, 1)
            pe.wait_ge(f_lo, NT)
            for c, (c0, cn) in enumerate(CHUNKS):
                for k in range(KD):
                    mm = mm3(pS[:, c, 0:cn], (wr_hi[:, k, :], wr_lo[:, k, :]),
                             (yT_hi[:, k, c0:c0 + cn], yT_lo[:, k, c0:c0 + cn]), k == 0, k == KD - 1)
                mm.then_inc(f_log, 1)

            def expert_in(e):
                pe.wait_ge(f_split, 2 + 2 * e)
                for i in range(6):
                    m, c = divmod(i, 3)
                    c0, cn = CHUNKS[c]
                    n = 6 * e + i
                    if n < 3:
                        pe.wait_ge(f_logc, c + 1)
                    else:
                        pe.wait_ge(f_h, n - 2)
                    cols = slice(128 * m, 128 * (m + 1))
                    for k in range(KD):
                        mm = mm3(pS[:, c, 0:cn], (eW1_hi[:, k, cols], eW1_lo[:, k, cols]),
                                 (yT_hi[:, k, c0:c0 + cn], yT_lo[:, k, c0:c0 + cn]), k == 0, k == KD - 1)
                    mm.then_inc(f_m1, 1)

            def expert_out(e):
                pe.wait_ge(f_hlo, 6 * e + 6)
                pe.wait_ge(f_split, 3 + 2 * e)
                for t in range(NT):
                    n = NT * e + t
                    if n >= 2:
                        pe.wait_ge(f_acc, n - 1)
                    for k in range(2):
                        mm = mm3(pOJ[t % 2][0:TP, :],
                                 (at_tile(hE_hi[:, e % 2, k, :], t), at_tile(hE_lo[:, e % 2, k, :], t)),
                                 (eW2_hi[:, k, :], eW2_lo[:, k, :]), k == 0, k == 1)
                    mm.then_inc(f_m2, 1)

            expert_in(0)
            pe.wait_ge(f_prob, 1)
            for t in range(NT):
                mm = pe.transpose(pT[0:TP, 0, 8 * t:8 * (t + 1)], at_tile(prT, t), ident[0:8, 0:8])
            mm.then_inc(f_pturn, 1)
            for e in range(EXPERTS):
                if e + 1 < EXPERTS:
                    expert_in(e + 1)
                expert_out(e)
            pe.wait_ge(f_gate, EXPERTS)
            for t in range(NT):
                mm = pe.transpose(pS[0:EXPERTS, t // 4, TP * (t % 4):TP * (t % 4 + 1)], gate[:, :, t], ident[0:TP, 0:TP])
            mm.then_inc(f_gturn, 1)
            pe.wait_ge(f_gt, 1)
            pe.wait_ge(f_ld, 48)
            pe.wait_ge(f_acc, NT * EXPERTS)
            for t in range(NT):
                if t >= 2:
                    pe.wait_ge(f_fin, t - 1)
                pe.matmul(pOJ[t % 2][0:TP, :], at_tile(gateT, t), fb2[:], start=True, stop=True).then_inc(f_b2, 1)

        @block.scalar
        def _(act):
            A = nc.scalar.activation
            act.wait_ge(emb_arg, 1)
            A(embT[:], embT[:], ACT.Sin).then_inc(emb_sin, 1)
            for c, (c0, cn) in enumerate(CHUNKS):
                act.wait_ge(hid_mm, c + 1)
                A(hid[:, c0:c0 + cn], pS[0:COND, c, 0:cn], ACT.Silu, bias=fsmall[0:COND, 3:4]).then_inc(hid_act, 1)
            for c, (c0, cn) in enumerate(CHUNKS):
                act.wait_ge(cond_mm, c + 1)
                A(condF[:, c0:c0 + cn], pT[0:96, c, 0:cn], ACT.Identity, bias=fb[:, 0:1]).then_inc(cond_act, 1)

            def hi_tile(G, t, s_in, s_out):
                act.wait_ge(s_in, G + 1)
                A(yT_hi[:, :, TP * t:TP * (t + 1)], pT[:, G % 3, 0:4 * TP].rearrange("p (k n) -> p k n", k=KD),
                  ACT.Copy).then_inc(s_out, 1)

            for t in range(NT):
                hi_tile(t, t, x_turn, x_hi)
            for t in range(NT):
                act.wait_ge(kv_cent, t + 1)
                A(kvq[:], kvc[:], ACT.Square).then_inc(kv_sq, 1)
                act.wait_ge(kv_var, t + 1)
                A(ms8[:, :, 2, :], ms8[:, :, 1, :], ACT.Sqrt).then_inc(kv_std, 1)
            for p in range(4):
                act.wait_ge(pw_mm, p + 1)
                A(pvw[:, p, :], (pS[:, p, :] if p < 3 else pJ[:, :]), ACT.Copy).then_inc(pw_out, 1)
            for m in range(4):
                act.wait_ge(we_mm, m + 1)
                A(we_hi[:, m, :], (pS[:, m, :] if m < 3 else pJ[:, :]), ACT.Copy).then_inc(we_h, 1)

            def ln_step(base, s):
                if 1 <= s <= NT:
                    t, G = s - 1, base + s - 1
                    act.wait_ge(aff_mm, G + 1)
                    if G >= 2:
                        act.wait_ge(y_done, G - 1)
                    A(bS[:, t % 2, :], pS[0:TP, 1, :], ACT.Copy).then_inc(bias_copied, 1)
                if s >= 2:
                    hi_tile(base + s - 2, s - 2, y_turn, y_hi)

            for s in range(NT + 2):
                ln_step(0, s)
            for t in range(NT):
                act.wait_ge(l_max, t + 1)
                A(lt[:, 1, 0:NPAD], lt[:, 1, 0:NPAD], ACT.Ln).then_inc(l_ln, 1)
            act.drain().then_inc(block_done, 1)
            act.wait_ge(block_go, 1)

            with act.Fori(0, BLOCKS) as l:
                act.wait_ge(bias_in, 16)

                def qk_out(h, n):
                    w, c = divmod(n, 3)
                    c0, cn = CHUNKS[c]
                    act.wait_ge(qk_mm, 6 * h + n + 1)
                    dst = (qT_hi, kT_hi)[w][:, c0:c0 + cn]
                    A(dst, pS[:, c, 0:cn], ACT.Identity, bias=lbias[:, 4 * w + h:4 * w + h + 1]).then_inc(qk_hi, 1)

                def v_out(h, c):
                    c0, cn = CHUNKS[c]
                    act.wait_ge(v_mm, 3 * h + c + 1)
                    A(vT[:, c0:c0 + cn], pOJ[c % 2][:, 0:cn], ACT.Identity, bias=lbias[:, 8 + h:9 + h]).then_inc(v_act, 1)

                def exp(h, i):
                    act.wait_ge(neg_max, NT * h + i + 1)
                    p = Pb[0:TP, i % 3, 0:N]
                    A(p, p, ACT.Exp, bias=negm[:, i:i + 1], scale=SCALE, accum_out=den[:, i:i + 1]).then_inc(exp_done, 1)

                def v_turned(h):
                    for j, ts in enumerate(groups_of(NT)):
                        act.wait_ge(turned, 33 * h + j + 1)
                        n = len(ts)
                        A(v_hi[:, ts[0]:ts[0] + n, :], pT[0:TP, j, 0:128 * n].rearrange("p (t d) -> p t d", d=128),
                          ACT.Copy).then_inc(turn_hi, 1)

                def p_turned(h, i):
                    for j, bs in enumerate(groups_of(NT)):
                        act.wait_ge(turned, 33 * h + 4 + 3 * i + j)
                        n, u = len(bs), TP * (i % 2)
                        A(PT_hi[:, bs[0]:bs[0] + n, u:u + TP],
                          pT[0:TP, j, 0:TP * n].rearrange("p (b s) -> p b s", s=TP), ACT.Copy).then_inc(turn_hi, 1)

                def rden_out(h, p):
                    act.wait_ge(pv_mm, PAIRS * h + p + 1)
                    if h or p:
                        act.wait_ge(o_done, PAIRS * h + p)
                    A(rb[:], pO[:, 250:500], ACT.Copy).then_inc(rb_copied, 1)

                for c in range(3):
                    qk_out(0, c)
                for h in range(HEADS):
                    for c in range(3):
                        qk_out(h, 3 + c)
                    for c in range(3):
                        v_out(h, c)
                    exp(h, 0)
                    v_turned(h)
                    exp(h, 1)
                    for i in range(2, NT):
                        exp(h, i)
                        if i >= 4 and i % 2 == 0:
                            rden_out(h, i // 2 - 2)
                        p_turned(h, i - 2)
                    more = h + 1 < HEADS
                    if more:
                        qk_out(h + 1, 0)
                    rden_out(h, 3)
                    p_turned(h, 8)
                    if more:
                        qk_out(h + 1, 1)
                    p_turned(h, 9)
                    if more:
                        qk_out(h + 1, 2)
                    rden_out(h, 4)
                for s in range(NT + 2):
                    ln_step(0, s)
                for kind, i in mlp_order:
                    if kind == "m1":
                        c, m = divmod(i, 4)
                        cn = CHUNKS[c][1]
                        src = pOJ[use_of[("m1", i)] % 2][:, 0:cn]
                        act.wait_ge(m1_mm, i + 1)
                        if i >= 2:
                            act.wait_ge(m1_lo, i - 1)
                        A(fT[:, i % 2, 0:cn], src, ACT.Relu, bias=lbias[:, 12 + m:13 + m])
                        A(hT_hi[:, m, 0:cn], src, ACT.Relu, bias=lbias[:, 12 + m:13 + m]).then_inc(m1_hi, 1)
                    else:
                        ln_step(NT, i)
                act.drain().then_inc(block_done, 1)
                act.wait_ge(block_go, l + 2)

            for t in range(NT):
                hi_tile(t, t, f_turn, f_hi)
            for c, (c0, cn) in enumerate(CHUNKS):
                act.wait_ge(f_log, c + 1)
                A(logT[:, c0:c0 + cn], pS[0:EXPERTS, c, 0:cn], ACT.Copy).then_inc(f_logc, 1)
            act.wait_ge(f_nmax, 1)
            A(prT[:], logT[:], ACT.Exp, bias=fstat[0:EXPERTS, 16:17], accum_out=fstat[0:EXPERTS, 17:18]).then_inc(f_exp, 1)
            act.wait_ge(f_ld, 48)

            def expert_act(e):
                for i in range(6):
                    m, c = divmod(i, 3)
                    c0, cn = CHUNKS[c]
                    n = 6 * e + i
                    act.wait_ge(f_m1, n + 1)
                    if n >= 2:
                        act.wait_ge(f_hlo, n - 1)
                    if i == 0 and e >= 2:
                        act.wait_ge(f_m2, NT * (e - 1))
                    b = fstat[:, 2 * e + m:2 * e + m + 1]
                    A(hF[:, n % 2, 0:cn], pS[:, c, 0:cn], ACT.Gelu, bias=b)
                    A(hE_hi[:, e % 2, m, c0:c0 + cn], pS[:, c, 0:cn], ACT.Gelu, bias=b).then_inc(f_h, 1)

            expert_act(0)
            act.wait_ge(f_pturn, 1)
            A(prC[:].rearrange("p t e -> p (t e)"), pT[0:TP, 0, 0:8 * NT], ACT.Copy).then_inc(f_prc, 1)
            for e in range(1, EXPERTS):
                expert_act(e)
            act.wait_ge(f_gturn, 1)
            for c, (c0, cn) in enumerate(CHUNKS):
                ins = A(gateT[:, c0:c0 + cn], pS[0:EXPERTS, c, 0:cn], ACT.Copy)
            ins.then_inc(f_gt, 1)

        @block.vector
        def _(dve):
            ch = outer = Chain(dve, dchain)
            link = ch.link

            def newton(r, r_in, v, tmp):
                link(dve.tensor_tensor(tmp, r_in, r_in, ALU.mult))
                link(dve.tensor_tensor(tmp, tmp, v, ALU.mult))
                link(dve.tensor_scalar(tmp, tmp, -0.5, 1.5, ALU.mult, ALU.add))
                link(dve.tensor_tensor(r, r_in, tmp, ALU.mult))

            def lo_tile(G, t, s_in, s_out):
                dve.wait_ge(s_in, G + 1)
                cols = slice(TP * t, TP * (t + 1))
                dve.tensor_tensor(yT_lo[:, :, cols], pT[:, G % 3, 0:4 * TP].rearrange("p (k n) -> p k n", k=KD),
                                  yT_hi[:, :, cols].bitcast(F32), ALU.subtract).then_inc(s_out, 1)

            dve.memset(halves, -0.5).then_inc(const_set, 1)
            dve.memset(ones[:], 1.0).then_inc(const_set, 1)
            dve.memset(zrow[:], 0.0).then_inc(const_set, 1)
            dve.wait_ge(ld_edge, 64)
            dve.scalar_tensor_tensor(out=keyR[:], in0=srcR[:, 0, :], scalar=float(NPAD), in1=srcR[:, 1, :],
                                     op0=ALU.mult, op1=ALU.add).then_inc(key_rows, 1)
            for b in range(2):
                dve.wait_ge(key_turn, b + 1)
                dve.tensor_copy(keyC[:, :, b], pOJ[b][0:TP, 0:80]).then_inc(key_cols, 1)
            dve.wait_ge(key_cols, 2)
            kc = keyC[:].rearrange("p a b -> p (a b)")

            def edge_chunk(c):
                cols = slice(EC * c, EC * (c + 1))
                dve.wait_ge(keyb_in[c % 2], 16 * (c // 2 + 1))
                link(dve.tensor_tensor(eq[:], keyB[:, c % 2], kc[:, cols].unsqueeze(2).to_broadcast((TP, EC, TP)),
                                       ALU.is_equal))
                link(dve.tensor_reduce(cnt[:, cols], eq[:], AX.X, ALU.add))
                link(dve.tensor_tensor(eq[:], eq[:], earlier[:].unsqueeze(1).to_broadcast((TP, EC, TP)), ALU.mult))
                link(dve.tensor_reduce(bef[:, cols], eq[:], AX.X, ALU.add))
                link(dve.tensor_scalar(bef[:, cols], bef[:, cols], 0.0, None, ALU.is_equal))
                link(dve.scalar_tensor_tensor(out=bef[:, cols], in0=kc[:, cols], scalar=trash[:, 0:1], in1=bef[:, cols],
                                              op0=ALU.subtract, op1=ALU.mult))
                dve.tensor_scalar(idxU[:, cols], bef[:, cols], trash[:, 0:1], None, ALU.add).then_inc(edge_idx, 1)
                dve.wait_ge(edge_idx, c + 1)

            edge_chunk(0)
            dve.wait_ge(ld_cond, 16 * 7)
            link(dve.tensor_scalar(embT[:], embT[:], fsmall[:, 0:1], None, ALU.mult))
            link(dve.tensor_scalar(embK[:], embT[:], 1.0 / TURN, fsmall[:, 1:2], ALU.mult, ALU.add))
            link(dve.tensor_scalar(embK[:], embK[:], ROUNDER, None, ALU.add))
            link(dve.tensor_scalar(embK[:], embK[:], -ROUNDER, None, ALU.add))
            for part in TURN_PARTS:
                link(dve.scalar_tensor_tensor(out=embT[:], in0=embK[:], scalar=-part, in1=embT[:],
                                              op0=ALU.mult, op1=ALU.add))
            link(dve.tensor_scalar(embT[:], embT[:], fsmall[:, 2:3], PI_BELOW, ALU.add, ALU.min))
            dve.tensor_scalar(embT[:], embT[:], -PI_BELOW, None, ALU.max).then_inc(emb_arg, 1)
            dve.wait_ge(ld_x, 16)

            def stats(t, src):
                link(dve.bn_stats(st6[:, t % 2, :], src))
                link(dve.bn_aggr(mv[:, t, :], st6[:, t % 2, :]))

            for t in range(NT):
                stats(t, g[:, t, :])
            dve.tensor_scalar(ve, mv[:, :, 1], EPS, None, ALU.add).then_inc(x_ve, 1)
            dve.wait_ge(cond_act, 3)
            dve.tensor_copy(condS[:], condF[:]).then_inc(cond_done, 1)
            dve.wait_ge(cond_done, 1)
            dve.tensor_tensor(condS[32:64, :], condF[32:64, :], condS[32:64, :].bitcast(F32), ALU.subtract
                              ).then_inc(cond_done, 1)
            dve.wait_ge(x_pow, 1)
            newton(rstd, r0, ve, rt)
            for t in range(NT):
                dve.tensor_scalar(g[:, t, :], g[:, t, :], mv[:, t, 0:1], rstd[:, t:t + 1], ALU.subtract, ALU.mult
                                  ).then_inc(x_norm, 1)
                if t >= 1:
                    lo_tile(t - 1, t - 1, x_hi, x_lo)
            lo_tile(NT - 1, NT - 1, x_hi, x_lo)
            for c in range(1, ET // EC):
                edge_chunk(c)
            dve.wait_ge(zeroed, 32 * TABLES)
            by_head = lambda ap: ap.rearrange("p (h d) -> p h d", h=MH)
            wide = lambda ap: ap.unsqueeze(2).to_broadcast((TP, MH, MD))
            for t in range(NT):
                dve.wait_ge(kv_mm, t + 1)
                src = [pS[0:TP, t % 2, :], pOJ[t % 2][0:TP, :]]
                for w in range(2):
                    link(dve.tensor_reduce(ms8[:, w, 0, :], by_head(src[w]), AX.X, ALU.add))
                link(dve.tensor_scalar(ms8[:, :, 0, :], ms8[:, :, 0, :], 1.0 / MD, None, ALU.mult))
                link(dve.tensor_tensor(by_head(kvc[:, 0, :]), by_head(src[0]), wide(ms8[:, 0, 0, :]), ALU.subtract))
                dve.tensor_tensor(by_head(kvc[:, 1, :]), by_head(src[1]), wide(ms8[:, 1, 0, :]), ALU.subtract
                                  ).then_inc(kv_cent, 1)
                dve.wait_ge(kv_sq, t + 1)
                for w in range(2):
                    link(dve.tensor_reduce(ms8[:, w, 1, :], by_head(kvq[:, w, :]), AX.X, ALU.add))
                dve.tensor_scalar(ms8[:, :, 1, :], ms8[:, :, 1, :], 1.0 / MD, EPS, ALU.mult, ALU.add).then_inc(kv_var, 1)
                dve.wait_ge(kv_std, t + 1)
                link(dve.reciprocal(ms8[:, :, 3, :], ms8[:, :, 2, :]))
                newton(ms8[:, :, 4, :], ms8[:, :, 3, :], ms8[:, :, 1, :], ms8[:, :, 2, :])
                if t >= 2:
                    dve.wait_ge(kv_acc, t - 1)
                link(dve.tensor_tensor(by_head(kvh[:, t % 2, 0, :]), by_head(kvc[:, 0, :]), wide(ms8[:, 0, 4, :]), ALU.mult))
                dve.tensor_tensor(by_head(kvh[:, t % 2, 1, :]), by_head(kvc[:, 1, :]), wide(ms8[:, 1, 4, :]), ALU.mult
                                  ).then_inc(kv_norm, 1)
            dve.wait_ge(ld_mix, 16 * 8)
            dve.wait_ge(kv_acc, NT)
            gk, bk = mrow[:, 0, :], mrow[:, 1, :]
            row = lambda ap: ap[:].rearrange("p k n -> p (k n)")
            for p in range(4):
                link(dve.tensor_scalar(pvk[:, p, :], pT[:, 0, 128 * p:128 * (p + 1)], mcol[:, 0, p:p + 1], None, ALU.mult))
            link(dve.tensor_tensor(row(pvk), row(pvk), gk, ALU.mult))
            link(dve.tensor_tensor(row(pvu), pT[:, 2, :], gk, ALU.mult))
            link(dve.scalar_tensor_tensor(out=row(pvu), in0=bk, scalar=float(N), in1=row(pvu), op0=ALU.mult, op1=ALU.add))
            link(dve.tensor_tensor(mcol[:, 2, :], pT[:, 1, 0:4], mcol[:, 0, :], ALU.mult))
            for p in range(4):
                link(dve.scalar_tensor_tensor(out=pvk[:, p, :], in0=pvu[:, p, :], scalar=mcol[:, 1, p:p + 1],
                                              in1=pvk[:, p, :], op0=ALU.mult, op1=ALU.add))
                link(dve.scalar_tensor_tensor(out=pvk[:, p, :], in0=bk[:, 128 * p:128 * (p + 1)],
                                              scalar=mcol[:, 2, p:p + 1], in1=pvk[:, p, :], op0=ALU.mult, op1=ALU.add))
            dve.tensor_tensor(pvk[:], pvk[:], hmask[:].unsqueeze(1).to_broadcast((128, 4, 128)), ALU.mult
                              ).then_inc(pv_ready, 1)
            for m in range(4):
                dve.wait_ge(we_h, m + 1)
                dve.tensor_tensor(we_lo[:, m, :], (pS[:, m, :] if m < 3 else pJ[:, :]), we_hi[:, m, :].bitcast(F32),
                                  ALU.subtract).then_inc(we_l, 1)
            for t in range(NT):
                dve.wait_ge(xr_in[t % 2], 16 * (t // 2 + 1))
                link(dve.tensor_tensor(xr[:, t % 2, :], xr[:, t % 2, :], mbo[:], ALU.add))
                dve.wait_ge(mix_mm, t + 1)
                dve.tensor_tensor(xr[:, t % 2, :], xr[:, t % 2, :], pOJ[t % 2][0:TP, :], ALU.add).then_inc(mix_add, 1)

            def ln_stats(base, s):
                link(dve.bn_stats(st6[:, s % 2, :], g[:, s, :]))
                link(dve.bn_aggr(mv[:, s, :], st6[:, s % 2, :]))
                dve.tensor_scalar(ve[:, s:s + 1], mv[:, s, 1:2], EPS, None, ALU.add).then_inc(var_done, 1)

            def ln_finish(base, s):
                if 1 <= s <= NT:
                    t, G = s - 1, base + s - 1
                    c = slice(t, t + 1)
                    dve.wait_ge(pow_done, G + 1)
                    newton(rstd[:, c], r0[:, c], ve[:, c], rt[:, c])
                    link(dve.tensor_scalar(xh[:], g[:, t, :], mv[:, t, 0:1], rstd[:, c], ALU.subtract, ALU.mult))
                    dve.wait_ge(aff_mm, G + 1)
                    if G >= 2:
                        dve.wait_ge(y_turn, G - 1)
                    dve.scalar_tensor_tensor(out=y1[:, t % 2, :], in0=pS[0:TP, 0, :], scalar=1.0, in1=xh[:],
                                             op0=ALU.add, op1=ALU.mult).then_inc(y_scaled, 1)
                if s >= 2:
                    lo_tile(base + s - 2, s - 2, y_hi, y_lo)

            for s in range(NT + 2):
                if s < NT:
                    ln_stats(0, s)
                ln_finish(0, s)
            for t in range(NT):
                row_t, tmp, mask = L[:, t, :], lt[:, 1, 0:NPAD], lt[:, 2, 0:NPAD]
                for k in range(TABLES):
                    dve.wait_ge(lt_in[t % 2][k], 16 * (t // 2 + 1))
                for k in range(1, TABLES):
                    link(dve.tensor_tensor(row_t, row_t, lt[:, k - 1, 0:NPAD], ALU.add))
                link(dve.tensor_scalar(mask, row_t, 0.5, MASKED, ALU.is_lt, ALU.mult))
                dve.tensor_scalar(tmp, row_t, 1.0, None, ALU.max).then_inc(l_max, 1)
                dve.wait_ge(l_ln, t + 1)
                dve.scalar_tensor_tensor(out=row_t, in0=tmp, scalar=1.0 / SCALE, in1=mask, op0=ALU.mult, op1=ALU.add
                                         ).then_inc(l_done, 1)
            dve.wait_ge(l_done, NT)
            dve.drain().then_inc(block_done, 1)
            dve.wait_ge(block_go, 1)

            with dve.Fori(0, BLOCKS) as l:
                ch = Chain(dve, lchain)
                link = ch.link
                link(dve.memset(kT_hi[:, N:NPAD].bitcast(F32), 0.0))
                link(dve.memset(kT_lo[:, N:NPAD].bitcast(F32), 0.0))
                dve.wait_ge(bias_in, 16)

                def qk_rest(h, n):
                    w, c = divmod(n, 3)
                    c0, cn = CHUNKS[c]
                    dve.wait_ge(qk_hi, 6 * h + n + 1)
                    hi, lo = ((qT_hi, qT_lo), (kT_hi, kT_lo))[w]
                    dve.scalar_tensor_tensor(out=lo[:, c0:c0 + cn], in0=pS[:, c, 0:cn],
                                             scalar=lbias[:, 4 * w + h:4 * w + h + 1],
                                             in1=hi[:, c0:c0 + cn].bitcast(F32), op0=ALU.add, op1=ALU.subtract
                                             ).then_inc(qk_lo, 1)

                def masked_max(h, i):
                    dve.wait_ge(scores, NT * h + i + 1)
                    if i >= 3:
                        dve.wait_ge(turned, 33 * h + 3 * i - 3)
                    elif i == 2:
                        dve.wait_ge(turned, 33 * h + 3)
                    elif i == 0 and h:
                        dve.wait_ge(turned, 33 * h)
                    dve.tensor_tensor_reduce(
                        out=Pb[0:TP, i % 3, 0:NPAD].rearrange("p (c n) -> p c n", c=3), in0=pS[0:TP, :, 0:SW],
                        in1=L[:, i, :].rearrange("p (c n) -> p c n", c=3), scale=1.0, scalar=2 * MASKED,
                        op0=ALU.add, op1=ALU.max, accum_out=rowmax[:, i:i + 1]).then_inc(row_max, 1)
                    dve.wait_ge(row_max, NT * h + i + 1)
                    dve.tensor_scalar(negm[:, i:i + 1], rowmax[:, i:i + 1], 0.1 * MASKED, -SCALE, ALU.max, ALU.mult
                                      ).then_inc(neg_max, 1)

                def inverse(h, i):
                    dve.wait_ge(exp_done, NT * h + i + 1)
                    link(dve.tensor_scalar(dmax[:, i:i + 1], den[:, i:i + 1], 1e-30, None, ALU.max))
                    link(dve.reciprocal(rden[:, i:i + 1], dmax[:, i:i + 1]))
                    dve.tensor_scalar(diag[:, i % 4, :], ident[0:TP, 0:TP], rden[:, i:i + 1], None, ALU.mult
                                      ).then_inc(diag_done, 1)

                def v_rest(h):
                    for j, ts in enumerate(groups_of(NT)):
                        dve.wait_ge(turn_hi, 33 * h + j + 1)
                        n = len(ts)
                        dve.tensor_tensor(v_lo[:, ts[0]:ts[0] + n, :],
                                          pT[0:TP, j, 0:128 * n].rearrange("p (t d) -> p t d", d=128),
                                          v_hi[:, ts[0]:ts[0] + n, :].bitcast(F32), ALU.subtract).then_inc(turn_lo, 1)

                def p_rest(h, i):
                    for j, bs in enumerate(groups_of(NT)):
                        dve.wait_ge(turn_hi, 33 * h + 4 + 3 * i + j)
                        n, u = len(bs), TP * (i % 2)
                        dst = (slice(None), slice(bs[0], bs[0] + n), slice(u, u + TP))
                        dve.tensor_tensor(PT_lo[dst], pT[0:TP, j, 0:TP * n].rearrange("p (b s) -> p b s", s=TP),
                                          PT_hi[dst].bitcast(F32), ALU.subtract).then_inc(turn_lo, 1)

                def o_out(h, p):
                    dve.wait_ge(rb_copied, PAIRS * h + p + 1)
                    dve.tensor_tensor(oT[:, h, 250 * p:250 * (p + 1)], pO[:, 0:250], rb[:], ALU.mult).then_inc(o_done, 1)

                for c in range(3):
                    qk_rest(0, c)
                for h in range(HEADS):
                    for c in range(3):
                        qk_rest(h, 3 + c)
                    masked_max(h, 0)
                    masked_max(h, 1)
                    v_rest(h)
                    for i in range(2, NT):
                        masked_max(h, i)
                        if i == 2:
                            inverse(h, 0)
                        inverse(h, i - 1)
                        if i >= 4 and i % 2 == 0:
                            o_out(h, i // 2 - 2)
                        p_rest(h, i - 2)
                    more = h + 1 < HEADS
                    inverse(h, 9)
                    if more:
                        qk_rest(h + 1, 0)
                    o_out(h, 3)
                    p_rest(h, 8)
                    if more:
                        qk_rest(h + 1, 1)
                    p_rest(h, 9)
                    if more:
                        qk_rest(h + 1, 2)
                    o_out(h, 4)

                def g_sum(G, s):
                    dve.wait_ge(proj, G + 1)
                    if G == 0:
                        dve.wait_ge(g_in[0], 16)
                    if G == 2:
                        dve.wait_ge(g_in[1], 16)
                    dve.tensor_tensor(g[:, s, :], g[:, s, :], pOJ[use_of[("proj", G)] % 2][0:TP, :], ALU.add
                                      ).then_inc(g_add, 1)
                    dve.wait_ge(g_add, G + 1)

                for s in range(NT + 2):
                    if s < NT:
                        g_sum(s, s)
                        ln_stats(0, s)
                    ln_finish(0, s)
                for kind, i in mlp_order:
                    if kind == "m1":
                        c, m = divmod(i, 4)
                        cn = CHUNKS[c][1]
                        dve.wait_ge(m1_hi, i + 1)
                        dve.tensor_tensor(hT_lo[:, m, 0:cn], fT[:, i % 2, 0:cn], hT_hi[:, m, 0:cn].bitcast(F32),
                                          ALU.subtract).then_inc(m1_lo, 1)
                    else:
                        if i < NT:
                            g_sum(NT + i, i)
                            ln_stats(NT, i)
                        ln_finish(NT, i)
                dve.drain().then_inc(block_done, 1)
                dve.wait_ge(block_go, l + 2)

            ch = outer
            link = ch.link
            for t in range(NT):
                dve.wait_ge(f_in[t % 2], 16 * (t // 2 + 1))
                dve.tensor_tensor(g[:, t, :], g[:, t, :], xm[:, t % 2, :], ALU.add).then_inc(f_add, 1)
                dve.wait_ge(f_add, t + 1)
                stats(t, g[:, t, :])
            dve.tensor_scalar(ve, mv[:, :, 1], EPS, None, ALU.add).then_inc(f_ve, 1)
            dve.wait_ge(f_pow, 1)
            dve.wait_ge(f_ve, 1)
            newton(rstd, r0, ve, rt)
            for t in range(NT):
                if t >= 2:
                    dve.wait_ge(f_turn, t - 1)
                dve.tensor_scalar(xm[:, t % 2, :], g[:, t, :], mv[:, t, 0:1], rstd[:, t:t + 1], ALU.subtract, ALU.mult
                                  ).then_inc(f_norm, 1)
                if t >= 1:
                    lo_tile(t - 1, t - 1, f_hi, f_lo)
            lo_tile(NT - 1, NT - 1, f_hi, f_lo)
            dve.wait_ge(f_ld, 48)
            dve.wait_ge(f_logc, 3)
            link(dve.tensor_reduce(fstat[0:EXPERTS, 18:19], logT[:], AX.X, ALU.max))
            dve.tensor_scalar(fstat[0:EXPERTS, 16:17], fstat[0:EXPERTS, 18:19], -1.0, None, ALU.mult).then_inc(f_nmax, 1)
            dve.wait_ge(f_exp, 1)
            link(dve.reciprocal(fstat[0:EXPERTS, 19:20], fstat[0:EXPERTS, 17:18]))
            dve.tensor_scalar(prT[:], prT[:], fstat[0:EXPERTS, 19:20], None, ALU.mult).then_inc(f_prob, 1)
            link(dve.memset(rank[:], 0.0))

            def expert_rest(e, i):
                m, c = divmod(i, 3)
                c0, cn = CHUNKS[c]
                n = 6 * e + i
                dve.wait_ge(f_h, n + 1)
                dve.tensor_tensor(hE_lo[:, e % 2, m, c0:c0 + cn], hF[:, n % 2, 0:cn],
                                  hE_hi[:, e % 2, m, c0:c0 + cn].bitcast(F32), ALU.subtract).then_inc(f_hlo, 1)

            def ranks(e, t):
                mine = prC[:, t, e:e + 1]
                a, b = TP * t, TP * (t + 1)
                if t:
                    link(dve.tensor_scalar(junk[:, 0:a], prB[:, e, 0:a], mine, 0.0, ALU.is_ge, ALU.add,
                                           accum_out=rank[:, e, t, 0:1]))
                link(dve.tensor_scalar(junk[:, a:N], prB[:, e, a:N], mine, 0.0, ALU.is_gt, ALU.add,
                                       accum_out=rank[:, e, t, 1:2]))
                link(dve.scalar_tensor_tensor(out=junk[:, a:b], in0=prB[:, e, a:b], scalar=mine, in1=early2[:],
                                              op0=ALU.is_equal, op1=ALU.mult, accum_out=rank[:, e, t, 2:3]))

            for i in range(6):
                expert_rest(0, i)
            dve.wait_ge(f_prb, 16)
            dve.wait_ge(f_prc, 1)
            for e in range(EXPERTS):
                for i in range(6):
                    if e + 1 < EXPERTS:
                        expert_rest(e + 1, i)
                    for t in (2 * i, 2 * i + 1):
                        if t < NT:
                            ranks(e, t)
                link(dve.tensor_reduce(gate[:, e, :], rank[:, e, :, :], AX.X, ALU.add))
                dve.scalar_tensor_tensor(out=gate[:, e, :], in0=gate[:, e, :], scalar=float(CAP), in1=prC[:, :, e],
                                         op0=ALU.is_lt, op1=ALU.mult).then_inc(f_gate, 1)
                dve.wait_ge(f_gate, e + 1)
                for t in range(NT):
                    dve.wait_ge(f_m2, NT * e + t + 1)
                    dve.scalar_tensor_tensor(out=g[:, t, :], in0=pOJ[t % 2][0:TP, :], scalar=gate[:, e, t:t + 1],
                                             in1=g[:, t, :], op0=ALU.mult, op1=ALU.add).then_inc(f_acc, 1)
            for t in range(NT):
                dve.wait_ge(f_b2, t + 1)
                dve.wait_ge(f_acc, NT * EXPERTS)
                dve.tensor_tensor(g[:, t, :], g[:, t, :], pOJ[t % 2][0:TP, :], ALU.add).then_inc(f_fin, 1)


def kernel(**inputs):
    import concourse.bacc as _bacc
    from concourse.bass_utils import run_bass_kernel_spmd as _run

    nc = _bacc.Bacc("TRN2", target_bir_lowering=False, num_devices=1)
    arrays, args = {}, {}
    for name, a in host_arrays({k: np.asarray(v) for k, v in inputs.items()}).items():
        arrays[f"in_{name}"] = a
        args[name] = nc.dram_tensor(f"in_{name}", a.shape, mybir.dt.from_np(a.dtype), kind="ExternalInput").ap()
    out = nc.dram_tensor("out_0", (N, D), F32, kind="ExternalOutput").ap()
    build(nc, args, out)
    r = _run(nc, [arrays], core_ids=[0])
    return r.results[0]["out_0"]
```

```python
from contextlib import ExitStack

import numpy as np

import concourse.bass as bass
from concourse import mybir

F32 = mybir.dt.float32
F32R = mybir.dt.float32r
BF16 = mybir.dt.bfloat16
I32 = mybir.dt.int32
U32 = mybir.dt.uint32
ALU = mybir.AluOpType
ACT = mybir.ActivationFunctionType
AX = mybir.AxisListType

N = 1250
D = 512
EDGES = 20000
BLOCKS = 4
HEADS = 4
DH = D // HEADS
TP = 125
NT = N // TP
TW = TP + 1
KD = D // 128
CHUNKS = [(0, 500), (500, 500), (1000, 250)]
SW = 418
NPAD = 3 * SW
PAIRS = NT // 2
ET = EDGES // TP
TABLES = 2
TABLE = N * NPAD
GE = 2 * TP
GROUPS = EDGES // GE
PARTS = [(0, 8), (8, 32), (32, GROUPS)]
COND = 16
MH, MD = 8, 64
EXPERTS, FF, CAP = 8, 256, 512
EPS = 1e-5
MASKED = -1e30
SCALE = float(DH) ** -0.5
TURN = 2.0 * np.pi
TURN_PARTS = [6.28125, 0.0019340515136718750, TURN - 6.28125 - 0.0019340515136718750]
ROUNDER = 1.5 * 2.0 ** 23
PI_BELOW = 3.1415925


def host_arrays(a):
    f = np.float32

    def kpn(w):
        return np.ascontiguousarray(w.reshape(KD, 128, -1).transpose(1, 0, 2).reshape(128, -1))

    g = {k[7:]: v for k, v in a.items() if k.startswith("L0_gnn_")}
    o = {"x": a["x"], "src": a["src"].reshape(80, 250), "dst": a["dst"].reshape(80, 250),
         "noise": a["node_vec1"].reshape(1, N)}
    o["ident"] = np.eye(128, dtype=f)
    freq = np.arange(1, 33, dtype=f) * f(2.0 * np.pi / 16)
    o["freq"] = np.concatenate([freq, freq]).reshape(64, 1)
    o["quarter"] = np.repeat(np.array([[0, 0], [0.25, np.pi / 2]], f), 32, axis=0)
    order = np.where(np.arange(GE)[:, None] < np.arange(GE), f(-256), f(1)).astype(f)
    o["order"] = order.reshape(2, TP, GE).transpose(1, 0, 2)
    o["before"] = np.triu(np.ones((TP, TP), f), 1)
    o["trash"] = (TABLE + np.arange(TP)).astype(f).reshape(TP, 1)
    blk = np.zeros((128, 128), f)
    blk[:64, :64] = blk[64:, 64:] = 1.0 / N
    o["headmask"] = blk
    o["f_w1"], o["f_b1"] = g["f_w1"], g["f_b1"].reshape(COND, 1)
    w2, b2 = np.zeros((COND, 96), f), np.zeros((96, 1), f)
    for r in (0, 32, 64):
        w2[:, r:r + COND], b2[r:r + COND, 0] = g["f_w2"], g["f_b2"]
        b2[r + COND] = 1.0
    o["f_w2"], o["f_b2"] = w2, b2

    def affine(cols):
        m = np.zeros((96, 3 * D), f)
        for n, (w, b) in enumerate(cols):
            for r in (0, 32, 64):
                if w is not None:
                    m[r:r + COND, n * D:(n + 1) * D] = w
                if b is not None:
                    m[r + COND, n * D:(n + 1) * D] = b
        return m

    o["aff1"] = np.stack([affine([(g["s1_w"][n % 4], g["s1_b"][n % 4]), (g["b1_w"][n % 4], g["b1_b"][n % 4]),
                                  (None, g["m_b2"][n - 1] if n else a["L0_mix_b_out"])]) for n in range(BLOCKS + 1)])
    o["aff2"] = np.stack([affine([(g["s2_w"][n], g["s2_b"][n]), (g["b2_w"][n], g["b2_b"][n]),
                                  (None, g["bo"][n])]) for n in range(BLOCKS)])
    qkv = np.stack([g["wq"], g["wk"], g["wv"]], 1).reshape(BLOCKS, 3, KD, 128, HEADS, DH)
    qkv = qkv.transpose(0, 4, 3, 1, 2, 5).reshape(BLOCKS * HEADS, 128, 3 * KD * DH)
    o["wqkv"] = np.ascontiguousarray(np.concatenate([qkv, qkv[:1]]))
    bias = np.stack([g["bq"], g["bk"], g["bv"], g["m_b1"]], 1).reshape(BLOCKS, 4, 4, 128)
    o["bias"] = np.ascontiguousarray(bias.transpose(0, 3, 1, 2).reshape(BLOCKS, 128, 16))
    o["wo"] = np.stack([kpn(w) for w in g["wo"]])
    o["w1"] = np.stack([kpn(w) for w in g["m_w1"]])
    o["w2"] = np.stack([kpn(w) for w in g["m_w2"]])
    wqkv = a["L0_mix_W_qkv"]
    o["mix_wk"], o["mix_wv"] = kpn(wqkv[D:2 * D].T), kpn(wqkv[2 * D:].T)
    o["mix_wq"] = kpn(wqkv[:D])
    o["mix_wo"] = kpn(a["L0_mix_W_out"].T)
    o["mix_gk"], o["mix_bk"] = a["L0_mix_gamma_K"].reshape(1, D), a["L0_mix_beta_K"].reshape(1, D)
    o["mix_gv"] = a["L0_mix_gamma_V"].reshape(4, 128).T
    o["mix_bv"] = a["L0_mix_beta_V"].reshape(4, 128).T
    wr = np.zeros((D, 128), f)
    wr[:, :EXPERTS] = a["L0_ffn_Wr"]
    o["ffn_wr"] = kpn(wr)
    o["ffn_w1"] = np.stack([kpn(w) for w in a["L0_ffn_W1"]])
    o["ffn_w2"] = np.ascontiguousarray(
        a["L0_ffn_W2"].reshape(EXPERTS, 2, 128, D).transpose(0, 2, 1, 3).reshape(EXPERTS, 128, 2 * D))
    o["ffn_b1"] = a["L0_ffn_b1"].reshape(EXPERTS, 2, 128).transpose(2, 0, 1).reshape(128, 16)
    o["ffn_b2"] = a["L0_ffn_b2"]
    return {k: np.ascontiguousarray(v) for k, v in o.items()}


def groups_of(n):
    return [range(b, min(b + 4, n)) for b in range(0, n, 4)]


def build(nc, I, out):
    ctx = ExitStack()
    uniq = [0]

    def at(name, shape, dt, addr):
        uniq[0] += 1
        with ExitStack() as s:
            if addr:
                s.enter_context(nc.sbuf_tensor(f"below{uniq[0]}", [128, addr // 4], F32))
            return s.enter_context(nc.sbuf_tensor(name, shape, dt))

    with ctx:
        names = {}

        def sem(name):
            names[name] = ctx.enter_context(nc.semaphore(name))
            return names[name]

        L = at("L", [TP, NT, NPAD], F32, 0)
        ident = at("ident_s", [128, 128], F32, 50176)
        ones = at("ones", [128, 128], F32, 50688)
        condS = at("condS", [96, N + 2], F32R, 51200)
        yT_hi = at("yT_hi", [128, KD, N], F32R, 56224)
        yT_lo = at("yT_lo", [128, KD, N], F32R, 76224)
        diag = at("diag", [TP, 4, TP], F32, 96224)
        rb = at("rb", [128, 250], F32, 98240)
        small = at("small", [128, 256], F32, 99264)
        stage = at("stage", [128, 1536], F32, 100288)
        R = 106432
        mv = small[0:TP, 0:2 * NT].rearrange("p (t s) -> p t s", s=2)
        ve = small[0:TP, 20:30]
        r0 = small[0:TP, 30:40]
        rt = small[0:TP, 40:50]
        rstd = small[0:TP, 50:60]
        st6 = small[0:TP, 60:72].rearrange("p (b s) -> p b s", b=2)
        halves = small[0:TP, 72:82]
        rowmax = small[0:TP, 82:92]
        negm = small[0:TP, 92:102]
        den = small[0:TP, 102:112]
        rden = small[0:TP, 112:122]
        dmax = small[0:TP, 122:132]
        lbias = small[:, 132:148]
        fsmall = small[0:64, 148:152]
        fb = small[0:96, 152:154]
        wmean = small[:, 154:170]
        tiny = small[0:TP, 170:171]
        qT_hi = at("qT_hi", [128, N], F32R, R)
        qT_lo = at("qT_lo", [128, N], F32R, R + 5024)
        kT_hi = at("kT_hi", [128, NPAD], F32R, R + 10048)
        kT_lo = at("kT_lo", [128, NPAD], F32R, R + 15072)
        v_hi = at("v_hi", [TP, NT, DH], F32R, R + 20096)
        v_lo = at("v_lo", [TP, NT, DH], F32R, R + 25216)
        Pb = at("Pb", [128, 3, 1256], F32, R + 30336)
        vT = Pb[:, 2, 0:N]
        PT = at("PT", [TP, 2, NT, 250], F32R, R + 45408)
        PT_hi, PT_lo = PT[:, 0], PT[:, 1]
        oT = at("oT", [128, HEADS, N], F32, R + 65408)
        wA_hi = at("wA_hi", [128, 3, KD, DH], F32R, R + 85632)
        wA_lo = at("wA_lo", [128, 3, KD, DH], F32R, R + 91776)
        wo = at("wo_s", [128, KD, D], F32, R)
        aff2_hi = at("aff2_hi", [96, 3 * D], F32R, R + 8192)
        w1_hi = at("w1_hi", [128, KD, D], F32R, R + 20096)
        w1_lo = at("w1_lo", [128, KD, D], F32R, R + 28288)
        xh = at("xh", [TP, D], F32, R + 16384)
        y1 = at("y1", [TP, 2, D], F32, R + 36480)
        g = at("g", [TP, NT, D], F32, R + 44928)
        hT_hi = at("hT_hi", [128, 2, KD, 250], F32R, R)
        hT_lo = at("hT_lo", [128, 2, KD, 250], F32R, R + 65408)
        w2_hi = at("w2_hi", [128, KD, D], F32R, R + 73408)
        w2_lo = at("w2_lo", [128, KD, D], F32R, R + 8192)
        w2_raw = at("w2_raw", [128, KD, D], F32, R + 85632)
        fT = at("fT", [128, 2, 250], F32, R + 81600)
        aff1_hi = at("aff1_hi", [96, 3 * D], F32R, R + 97920)
        order = at("order_s", [TP, 2, GE], F32, 0)
        eqW = at("eqW", [TP, 4, 2, GE], BF16, 2048)
        ones_b = at("ones_b", [128, 1], BF16, 6400)
        zrow = at("zrow", [TP, NPAD], F32, 6432)
        keyR = at("keyR", [80, 250], F32, R + 97920)
        srcR = at("srcR", [80, 2, 250], I32, R + 98944)
        keyC = at("keyC", [TP, 80, 2], F32, R + 100960)
        bef = at("bef", [TP, ET], F32, R + 101600)
        trash = at("trash_s", [TP, 1], F32, R + 102240)
        idxU = at("idxU", [TP, ET], U32, R + 104064)
        cnt = at("cnt", [TP, ET], F32, R + 104704)
        embT = at("embT", [64, N], F32, R + 69504)
        embK = at("embK", [64, N], F32, R + 74528)
        embI = at("embI", [64, N], I32, R + 79552)
        hid = at("hid", [COND, N], F32, R + 84576)
        condF = at("condF", [96, N], F32, R + 89600)
        fw1 = at("fw1", [64, COND], F32, R + 94624)
        fw2 = at("fw2", [COND, 96], F32, R + 94688)
        tab2 = at("tab2", [TP, NT, NPAD], F32, R)
        lnc = at("lnc", [TP, 2, NPAD], F32, R + 50176)
        mask = at("mask", [TP, 2, NPAD], F32, R + 60224)
        wk_hi = at("wk_hi", [128, KD, D], F32R, R)
        wk_lo = at("wk_lo", [128, KD, D], F32R, R + 8192)
        wv_hi = at("wv_hi", [128, KD, D], F32R, R + 16384)
        wv_lo = at("wv_lo", [128, KD, D], F32R, R + 24576)
        kvh = at("kvh", [TP, 2, 2, D], F32, R + 32768)
        kvq = at("kvq", [TP, 2, D], F32, R + 65408)
        mix_wo = at("mix_wo_s", [128, KD, D], F32, R + 69504)
        mix_wq = at("mix_wq_s", [128, KD, D], F32, R + 77696)
        hmask = at("hmask", [128, 128], F32, R + 87936)
        mrow = at("mrow", [128, 2, D], F32, R + 88448)
        mcol = at("mcol", [128, 4, 4], F32, R + 92544)
        ms8 = at("ms8", [TP, 2, 5, MH], F32, R + 92608)
        pvk = at("pvk", [128, KD, 128], F32, R)
        pvu = at("pvu", [128, KD, 128], F32, R + 2048)
        pvw = at("pvw", [128, KD, D], F32, R + 4096)
        we_hi = at("we_hi", [128, KD, D], F32R, R + 16384)
        we_lo = at("we_lo", [128, KD, D], F32R, R + 24576)
        xr = at("xr", [TP, 2, D], F32, R + 65408)
        hE2_hi = at("hE2_hi", [128, 2, 2, N], F32R, 0)
        hE2_lo = at("hE2_lo", [128, 2, 2, N], F32R, 20000)
        prC = at("prC", [TP, NT, EXPERTS], F32, 40000)
        above = at("above", [TP, NT, EXPERTS], F32, 40320)
        equal = at("equal", [TP, NT, EXPERTS], F32, 40640)
        place = at("place", [TP, NT, EXPERTS], F32, 40960)
        gate = at("gate", [TP, NT, EXPERTS], F32, 41280)
        gateT = at("gateT", [EXPERTS, N], F32, 41600)
        thrB = at("thrB", [EXPERTS, TP], F32, 46624)
        passed = at("passed", [TP, EXPERTS], F32, 47136)
        before = at("before_s", [TP, TP], F32, 47168)
        junk = at("junk", [EXPERTS, N], BF16, 41600)
        eW2_lo = at("eW2_lo", [128, 2, D], F32R, 51200)
        xm = at("xm_s", [TP, 2, D], F32, R)
        fb2 = at("fb2", [EXPERTS, D], F32, R + 4096)
        fstat = at("fstat", [128, 32], F32, R + 6144)
        logT = at("logT", [EXPERTS, N], F32, R + 8192)
        prT = at("prT", [EXPERTS, N], F32, R + 13216)
        hE_hi = at("hE_hi", [128, 2, 2, N], F32R, R + 18240)
        wr_hi = at("wr_hi", [128, KD, 128], F32R, R + 38240)
        wr_lo = at("wr_lo", [128, KD, 128], F32R, R + 40288)
        hE_lo = at("hE_lo", [128, 2, 2, N], F32R, R + 65408)
        hF = at("hF", [128, 2, 500], F32, R + 85408)
        eW1_hi = at("eW1_hi", [128, KD, FF], F32R, R + 89408)
        eW1_lo = at("eW1_lo", [128, KD, FF], F32R, R + 93504)
        eW2_hi = at("eW2_hi", [128, 2, D], F32R, R + 97600)

        def hidden(e):
            return ((hE_hi, hE_lo), (hE2_hi, hE2_lo))[e % 4 // 2][0][:, e % 2], \
                ((hE_hi, hE_lo), (hE2_hi, hE2_lo))[e % 4 // 2][1][:, e % 2]

        pS = ctx.enter_context(nc.psum_tensor("pS", [128, 3, 512], F32))
        pT = ctx.enter_context(nc.psum_tensor("pT", [128, 3, 512], F32))
        pO = ctx.enter_context(nc.psum_tensor("pO", [128, 512], F32))
        pJ = ctx.enter_context(nc.psum_tensor("pJ", [128, 512], F32))
        pOJ = [pJ, pO]

        tabs = [nc.dram_tensor(f"counts{k}", [TABLE + TP, 1], F32).ap() for k in range(TABLES)]
        keys_d = nc.dram_tensor("keys", [80, 250], F32).ap()
        g_d = nc.dram_tensor("g_spill", [N, D], F32).ap()
        xm_d = nc.dram_tensor("x_plus_mix", [N, D], F32).ap()

        ld_x, ld_edge, ld_cond, ld_ident, ld_mix, ld_mixw = [sem(n) for n in (
            "ld_x", "ld_edge", "ld_cond", "ld_ident", "ld_mix", "ld_mixw")]
        zeroed = [sem(f"zeroed{k}") for k in range(TABLES)]
        zrow_set, key_bc, eq_done, edge_sum = [sem(n) for n in ("zrow_set", "keys_broadcast", "eq_done", "edge_sum")]
        w_cent, w_hi = sem("weights_centred"), sem("weights_hi")
        stage_in, split_done = sem("stage_in"), sem("split_done")
        counted = [sem(f"counted{k}") for k in range(TABLES)]
        const_set, dchain, pchain = sem("const_set"), sem("dve_chain"), sem("pool_chain")
        key_rows, key_turn, key_cols, edge_idx = [sem(n) for n in (
            "key_rows", "key_turned", "key_cols", "edge_idx")]
        emb_arg, emb_sin, hid_mm, hid_act, cond_mm, cond_act, cond_done = [sem(n) for n in (
            "emb_arg", "emb_sin", "hid_mm", "hid_act", "cond_mm", "cond_act", "cond_done")]
        x_ve, x_pow, x_norm, x_turn, x_hi, x_lo = [sem(n) for n in (
            "x_ve", "x_pow", "x_norm", "x_turned", "x_hi", "x_lo")]
        kv_mm, kv_sq, kv_var, kv_std, kv_norm, kv_acc = [sem(n) for n in (
            "kv_mm", "kv_squares", "kv_var", "kv_std", "kv_norm", "kv_acc")]
        pv_ready, pw_mm, pw_out, we_mm, we_h, we_l = [sem(n) for n in (
            "pv_ready", "pw_mm", "pw_out", "we_mm", "we_hi_done", "we_lo_done")]
        mix_mm, mix_add = sem("mix_mm"), sem("mix_add")
        xr_in = [sem(f"xr_in{k}") for k in range(2)]
        xm_out = [sem(f"xm_out{k}") for k in range(2)]
        tab_in = [sem(f"tab_in{k}") for k in range(PAIRS)]
        l_sum, l_ln, l_done = sem("l_sum"), sem("l_ln"), sem("l_done")
        first_of_block = len(names)
        bstage_in, bsplit = sem("block_stage_in"), sem("block_split")
        bias_in, wo_in, g_out = sem("bias_in"), sem("wo_in"), sem("g_out")
        w2_in, w2_hi_done, w2_lo_done = sem("w2_in"), sem("w2_hi_done"), sem("w2_lo_done")
        g_in = [sem("g_in0"), sem("g_in1")]
        qk_mm, qk_hi, qk_lo, v_mm, v_act = [sem(n) for n in ("qk_mm", "qk_hi", "qk_lo", "v_mm", "v_act")]
        scores, row_max, neg_max, exp_done, den_inv, diag_done = [sem(n) for n in (
            "scores", "row_max", "neg_max", "exp_done", "den_inverse", "diag_done")]
        turned, turn_hi, turn_lo = sem("turned"), sem("turn_hi"), sem("turn_lo")
        pv_mm, rb_copied, o_done = sem("pv_mm"), sem("rb_copied"), sem("o_done")
        proj, g_add, var_done, pow_done, aff_mm = [sem(n) for n in (
            "proj", "g_added", "var_done", "pow_done", "affine_mm")]
        y_scaled, y_turn, y_hi, y_lo = [sem(n) for n in ("y_scaled", "y_turned", "y_hi", "y_lo")]
        m1_mm, m1_hi, m1_lo = sem("m1_mm"), sem("m1_hi"), sem("m1_lo")
        lchain = sem("dve_block_chain")
        qchain = sem("pool_block_chain")
        cleared = list(names.values())[first_of_block:]
        block_done, block_seen, block_go = sem("block_done"), sem("block_seen"), sem("block_go")
        f_in = [sem("f_in0"), sem("f_in1")]
        f_add, f_ve, f_pow, f_norm, f_turn, f_hi, f_lo = [sem(n) for n in (
            "f_added", "f_ve", "f_pow", "f_norm", "f_turned", "f_hi", "f_lo")]
        f_ld, f_stage, f_split, f_log, f_logc, f_nmax, f_exp, f_prob = [sem(n) for n in (
            "f_ld", "f_stage_in", "f_split", "f_logits", "f_logits_out", "f_negmax", "f_exp", "f_prob")]
        f_pturn, f_prc, f_search, f_thr, f_thrturn, f_above, f_placed = [sem(n) for n in (
            "f_pturn", "f_prc", "f_search", "f_threshold", "f_threshold_turned", "f_above", "f_placed")]
        f_m1, f_h, f_hlo, f_m2, f_acc, f_gate, f_gturn, f_gt, f_b2, f_fin, f_out = [sem(n) for n in (
            "f_m1", "f_h", "f_hlo", "f_m2", "f_acc", "f_gate", "f_gturn", "f_gateT", "f_b2", "f_fin", "f_out")]

        class Chain:

            def __init__(self, eng, s):
                self.eng, self.sem, self.n = eng, s, 0

            def link(self, ins):
                self.n += 1
                ins.then_inc(self.sem, 1)
                self.eng.wait_ge(self.sem, self.n)

        block = ctx.enter_context(nc.Block())

        def at_tile(ap, t):
            return ap[:, TP * t:TP * (t + 1)]

        mlp_order = [("m1", m) for m in range(4)]
        for t in range(NT):
            mlp_order += [("step", t)]
            mlp_order += [("m1", 4 * (t // 2 + 1) + 2 * (t % 2) + m) for m in range(2) if t // 2 + 1 < PAIRS]
        mlp_order += [("step", NT), ("step", NT + 1)]
        uses = [("proj", t) for t in range(NT)]
        uses += [("m1", i) if k == "m1" else ("proj", NT + i) for k, i in mlp_order if k == "m1" or i < NT]
        use_of = {u: n for n, u in enumerate(uses)}
        (H1, AFF1, H2, H3, AFF2, W1A, W1B, W1C, NQ, NK, NV) = range(11)
        head_piece = {1: H1, 2: H2, 3: H3}

        def turned_tile(G):
            return pT[:, G % 3, 0:KD * TW].rearrange("p (k n) -> p k n", k=KD)[:, :, 0:TP]

        def hidden_rest(eng, e, i):
            m, c = divmod(i, 3)
            c0, cn = CHUNKS[c]
            n = 6 * e + i
            hi, lo = hidden(e)
            eng.wait_ge(f_h, n + 1)
            eng.tensor_tensor(lo[:, m, c0:c0 + cn], hF[:, n % 2, 0:cn], hi[:, m, c0:c0 + cn].bitcast(F32),
                              ALU.subtract).then_inc(f_hlo, 1)

        fpieces = [("r", 0)] + [("1", e) for e in range(4)] + [("2", 0), ("1", 4)]
        for e in range(1, EXPERTS):
            fpieces += [("2", e)] + [("1", e + 4)] * (e + 4 < EXPERTS)
        piece_of = {p: n for n, p in enumerate(fpieces)}

        @block.sync
        def _(sp):
            def stage_load(src, n, s_in, s_split):
                if n:
                    sp.wait_ge(s_split, n)
                sp.dma_start(stage[0:src.shape[0], 0:src.shape[1]], src).then_inc(s_in, 16)

            sp.dma_start(srcR[:, 0, :], I["src"]).then_inc(ld_edge, 16)
            sp.dma_start(srcR[:, 1, :], I["dst"]).then_inc(ld_edge, 16)
            sp.dma_start(ident[:], I["ident"]).then_inc(ld_ident, 16)
            sp.dma_start(order[:], I["order"]).then_inc(ld_edge, 16)
            sp.dma_start(trash[:], I["trash"]).then_inc(ld_edge, 16)

            def zero(k):
                body = tabs[k][0:TABLE, :].rearrange("(t p c) o -> p t (c o)", t=NT, p=TP)
                sp.dma_start(body, zrow[:].unsqueeze(1).to_broadcast((TP, NT, NPAD))).then_inc(zeroed[k], 16)
                sp.dma_start(tabs[k][TABLE:, :].rearrange("p o -> o p"), zrow[0:1, 0:TP]).then_inc(zeroed[k], 16)

            sp.wait_ge(zrow_set, 1)
            zero(0)
            sp.dma_start(embT[:], I["noise"].to_broadcast((64, N))).then_inc(ld_cond, 16)
            sp.dma_start(fsmall[:, 0:1], I["freq"]).then_inc(ld_cond, 16)
            sp.dma_start(fsmall[:, 1:3], I["quarter"]).then_inc(ld_cond, 16)
            sp.dma_start(fsmall[0:COND, 3:4], I["f_b1"]).then_inc(ld_cond, 16)
            sp.dma_start(fb[:, 0:1], I["f_b2"]).then_inc(ld_cond, 16)
            sp.dma_start(fw1[:], I["f_w1"]).then_inc(ld_cond, 16)
            sp.dma_start(fw2[:], I["f_w2"]).then_inc(ld_cond, 16)
            zero(1)
            sp.dma_start(g[:], I["x"].rearrange("(t p) d -> p t d", p=TP)).then_inc(ld_x, 16)
            mixw = [I["mix_wk"][:, 0:1024], I["mix_wk"][:, 1024:], I["mix_wv"][:, 0:1024], I["mix_wv"][:, 1024:]]
            pieces = mixw + [I["aff1"][0], I["wqkv"][0]]
            for n in range(4):
                stage_load(pieces[n], n, stage_in, split_done)
            sp.wait_ge(cond_done, 2)
            sp.dma_start(mix_wo[:].rearrange("p k n -> p (k n)"), I["mix_wo"]).then_inc(ld_mix, 16)
            sp.dma_start(mix_wq[:].rearrange("p k n -> p (k n)"), I["mix_wq"]).then_inc(ld_mix, 16)
            sp.dma_start(hmask[:], I["headmask"]).then_inc(ld_mix, 16)
            sp.dma_start(mrow[:, 0, :], I["mix_gk"].to_broadcast((128, D))).then_inc(ld_mix, 16)
            sp.dma_start(mrow[:, 1, :], I["mix_bk"].to_broadcast((128, D))).then_inc(ld_mix, 16)
            sp.dma_start(mcol[:, 0, :], I["mix_gv"]).then_inc(ld_mix, 16)
            sp.dma_start(mcol[:, 1, :], I["mix_bv"]).then_inc(ld_mix, 16)
            sp.wait_ge(edge_idx, len(PARTS))
            stage_load(pieces[4], 4, stage_in, split_done)
            sp.wait_ge(kv_acc, NT)
            for t in range(NT + 2):
                if t >= 2:
                    sp.wait_ge(mix_add, t - 1)
                    sp.dma_start(xm_d[TP * (t - 2):TP * (t - 1), :], xr[:, t % 2, :]).then_inc(xm_out[t % 2], 16)
                if t < NT:
                    if t >= 2:
                        sp.wait_ge(xm_out[t % 2], 16 * (t // 2))
                    sp.dma_start(xr[:, t % 2, :], I["x"][TP * t:TP * (t + 1), :]).then_inc(xr_in[t % 2], 16)
            sp.dma_start(g_d.rearrange("(t p) d -> p t d", p=TP), g[:]).then_inc(ld_mixw, 16)
            sp.wait_ge(ld_mixw, 16)
            for k in range(TABLES):
                sp.wait_ge(counted[k], 16 * (ET // TABLES))
            sp.wait_ge(y_turn, NT)
            for p in range(PAIRS):
                for k in range(TABLES):
                    rows = tabs[k][0:TABLE, :].rearrange("(t p c) o -> p t (c o)", t=NT, p=TP)[:, 2 * p:2 * p + 2, :]
                    sp.dma_start((L, tab2)[k][:, 2 * p:2 * p + 2, :], rows).then_inc(tab_in[p], 16)
            stage_load(pieces[5], 5, stage_in, split_done)
            for k in range(2):
                sp.wait_ge(xm_out[k], 16 * (NT // 2))

            def between(n):
                sp.wait_ge(block_done, 4 * n)
                for s in cleared:
                    sp.sem_clear(s)
                sp.sem_inc(block_go, 1)

            between(1)
            with sp.Fori(0, BLOCKS) as l:
                def one(name, n=1, off=0):
                    return I[name][bass.ds(n * l + off, 1)].rearrange("a p f -> (a p) f")

                sp.dma_start(lbias[:], one("bias")).then_inc(bias_in, 16)
                stage_load(one("wqkv", HEADS, 1), H1, bstage_in, bsplit)
                stage_load(one("aff1", 1, 1), AFF1, bstage_in, bsplit)
                stage_load(one("wqkv", HEADS, 2), H2, bstage_in, bsplit)
                stage_load(one("wqkv", HEADS, 3), H3, bstage_in, bsplit)
                stage_load(one("aff2"), AFF2, bstage_in, bsplit)
                sp.wait_ge(scores, NT * HEADS)
                sp.dma_start(wo[:].rearrange("p k n -> p (k n)"), one("wo")).then_inc(wo_in, 16)
                sp.dma_start(w2_raw[:].rearrange("p k n -> p (k n)"), one("w2")).then_inc(w2_in, 16)
                stage_load(one("w1")[:, 0:683], W1A, bstage_in, bsplit)
                sp.wait_ge(pv_mm, PAIRS * HEADS)
                gv = g_d.rearrange("(t p) d -> p t d", p=TP)
                sp.dma_start(g[:, 0:2, :], gv[:, 0:2, :]).then_inc(g_in[0], 16)
                sp.dma_start(g[:, 2:NT, :], gv[:, 2:NT, :]).then_inc(g_in[1], 16)
                stage_load(one("w1")[:, 683:1366], W1B, bstage_in, bsplit)
                stage_load(one("w1")[:, 1366:], W1C, bstage_in, bsplit)
                nxt = one("wqkv", HEADS, 4)
                for t in range(NT):
                    if t in (0, 4, 6):
                        j = (0, 4, 6).index(t)
                        stage_load(nxt[:, 512 * j:512 * (j + 1)], NQ + j, bstage_in, bsplit)
                    sp.wait_ge(g_add, NT + t + 1)
                    sp.dma_start(g_d[TP * t:TP * (t + 1), :], g[:, t, :]).then_inc(g_out, 16)
                sp.wait_ge(block_done, 4 * l + 8)
                sp.sem_inc(block_seen, 1)
                sp.wait_ge(g_out, 16 * NT)
                for s in cleared:
                    sp.sem_clear(s)
                sp.sem_inc(block_go, 1)
            sp.dma_start(fb2[:], I["ffn_b2"]).then_inc(f_ld, 16)
            sp.dma_start(fstat[:, 0:16], I["ffn_b1"]).then_inc(f_ld, 16)
            sp.dma_start(before[:], I["before"]).then_inc(f_ld, 16)
            for t in range(NT):
                if t >= 2:
                    sp.wait_ge(f_add, t - 1)
                sp.dma_start(xm[:, t % 2, :], xm_d[TP * t:TP * (t + 1), :]).then_inc(f_in[t % 2], 16)
            for n, (kind, e) in enumerate(fpieces):
                stage_load(I["ffn_wr"] if kind == "r" else I["ffn_w1" if kind == "1" else "ffn_w2"][e],
                           n, f_stage, f_split)
            for t in range(NT):
                sp.wait_ge(f_fin, t + 1)
                sp.dma_start(out[TP * t:TP * (t + 1), :], g[:, t, :]).then_inc(f_out, 16)
            sp.wait_ge(f_out, 16 * NT)

        @block.gpsimd
        def _(pool):
            ch = outer = Chain(pool, pchain)

            def split(hi, lo, n, s_in, s_done, cols, rows=128):
                pool.wait_ge(s_in, 16 * (n + 1))
                src = stage[0:rows, 0:cols]
                ch.link(pool.tensor_copy(hi, src))
                pool.tensor_tensor(lo, src, hi.bitcast(F32), ALU.subtract).then_inc(s_done, 1)

            def split_affine(dst, n, s_in, s_done):
                pool.wait_ge(s_in, 16 * (n + 1))
                ch.link(pool.tensor_copy(dst[:], stage[0:96, :]))
                low = dst[64:96, :]
                pool.tensor_tensor(low, stage[64:96, :], low.bitcast(F32), ALU.subtract).then_inc(s_done, 1)
                pool.wait_ge(s_done, n + 1)

            def flat(ap, a, b):
                return ap[:].rearrange("p k n -> p (k n)")[:, a:b]

            def rsqrt(dst, src, n, s_in, n_in, s_out):
                pool.wait_ge(s_in, n_in)
                pool.tensor_tensor(dst, src, halves[:, 0:n], ALU.pow).then_inc(s_out, 1)

            def ln_pow(base, t):
                rsqrt(r0[:, t:t + 1], ve[:, t:t + 1], 1, var_done, base + t + 1, pow_done)

            def all_counted(groups):
                for k in range(TABLES):
                    pool.wait_ge(counted[k], 32 * ((groups + TABLES - 1 - k) // TABLES))

            for r in range(GROUPS):
                k = r % TABLES
                starts = [a for a, _ in PARTS]
                if r in starts:
                    pool.wait_ge(edge_idx, starts.index(r) + 1)
                if r < TABLES:
                    pool.wait_ge(zeroed[k], 32)
                else:
                    pool.wait_ge(counted[k], 32 * (r // TABLES))
                for T in (2 * r, 2 * r + 1):
                    pool.indirect_dma_start(tabs[k], bass.IndirectOffsetOnAxis(ap=idxU[:, T:T + 1], axis=0),
                                            cnt[:, T:T + 1], None, compute_op=ALU.add,
                                            bounds_check=TABLE + TP - 1).then_inc(counted[k], 16)
                if r == 19:
                    all_counted(r + 1)
                    rsqrt(r0, ve, NT, x_ve, 1, x_pow)
                if r == 55:
                    all_counted(r + 1)
                    rsqrt(r0, ve, NT, var_done, 1, pow_done)
            all_counted(GROUPS)
            pool.wait_ge(mix_add, NT)
            wA = lambda ap, a, b: ap[:].rearrange("p w k n -> p (w k n)")[:, a:b]
            split(wA(wA_hi, 0, 1536), wA(wA_lo, 0, 1536), 5, stage_in, split_done, 1536)
            pool.drain().then_inc(block_done, 1)
            pool.wait_ge(block_go, 1)
            with pool.Fori(0, BLOCKS) as l:
                ch = Chain(pool, qchain)
                for h in (1, 2, 3):
                    pool.wait_ge(v_mm, 3 * h)
                    split(wA(wA_hi, 0, 1536), wA(wA_lo, 0, 1536), head_piece[h], bstage_in, bsplit, 1536)
                    if h == 1:
                        split_affine(aff1_hi, AFF1, bstage_in, bsplit)
                pool.wait_ge(scores, NT * HEADS)
                split_affine(aff2_hi, AFF2, bstage_in, bsplit)
                pool.wait_ge(pv_mm, PAIRS * HEADS)
                split(flat(w1_hi, 0, 683), flat(w1_lo, 0, 683), W1A, bstage_in, bsplit, 683)
                for t in range(NT):
                    ln_pow(0, t)
                    if t in (3, 6):
                        n, a = (W1B, 683) if t == 3 else (W1C, 1366)
                        b = min(a + 683, 2048)
                        split(flat(w1_hi, a, b), flat(w1_lo, a, b), n, bstage_in, bsplit, b - a)
                for t in range(NT):
                    ln_pow(NT, t)
                    if t in (3, 5, 7):
                        j = (3, 5, 7).index(t)
                        split(wA(wA_hi, 512 * j, 512 * (j + 1)), wA(wA_lo, 512 * j, 512 * (j + 1)),
                              NQ + j, bstage_in, bsplit, 512)
                pool.drain().then_inc(block_done, 1)
                pool.wait_ge(block_go, l + 2)
            ch = outer
            rsqrt(r0, ve, NT, f_ve, 1, f_pow)
            split(wr_hi[:].rearrange("p k n -> p (k n)"), wr_lo[:].rearrange("p k n -> p (k n)"),
                  0, f_stage, f_split, 512)

            def split_w1(e):
                if e:
                    pool.wait_ge(f_m1, 6 * e)
                split(flat(eW1_hi, 0, 1024), flat(eW1_lo, 0, 1024), piece_of[("1", e)], f_stage, f_split, 1024)

            def split_w2(e):
                if e:
                    pool.wait_ge(f_m2, NT * e)
                split(flat(eW2_hi, 0, 1024), flat(eW2_lo, 0, 1024), piece_of[("2", e)], f_stage, f_split, 1024)

            for e in range(4):
                split_w1(e)
                for i in range(6):
                    hidden_rest(pool, e, i)
            split_w2(0)
            for e in range(EXPERTS):
                if e + 1 < EXPERTS and e:
                    split_w2(e)
                if e + 4 < EXPERTS:
                    split_w1(e + 4)
            split_w2(EXPERTS - 1)

        @block.tensor
        def _(pe):
            def mm3(dst, lhs, rhs, first, last):
                (lh, ll), (rh, rl) = lhs, rhs
                pe.matmul(dst, lh, rh, start=first, stop=False)
                pe.matmul(dst, lh, rl, start=False, stop=False)
                return pe.matmul(dst, ll, rh, start=False, stop=last)

            def turn(dst, src):
                for k in range(KD):
                    mm = pe.transpose(dst[:, TW * k:TW * k + TP], src[:, 128 * k:128 * (k + 1)], ident[0:TP, 0:TP])
                return mm

            def y_tile(k, t):
                return at_tile(yT_hi[:, k, :], t), at_tile(yT_lo[:, k, :], t)

            def affine(aff, G, t):
                if G >= 2:
                    pe.wait_ge(y_scaled, G - 1)
                pe.matmul(pS[0:TP, G % 2, :], at_tile(condS, t), aff[:, 0:D], start=True, stop=True
                          ).then_inc(aff_mm, 1)

            def ln_turn(aff, G, t):
                pe.wait_ge(y_scaled, G + 1)
                if G >= 3:
                    pe.wait_ge(y_lo, G - 2)
                for k in range(KD):
                    cols = slice(128 * k, 128 * (k + 1))
                    pe.transpose(pT[:, G % 3, TW * k:TW * k + TP], y1[:, t % 2, cols], ident[0:TP, 0:TP])
                    mm = pe.matmul(pT[:, G % 3, TW * k:TW * (k + 1)], aff[:, D + 128 * k:D + 128 * (k + 1)],
                                   condS[:, TP * t:TP * t + TW], start=False, stop=True, skip_group_check=True)
                mm.then_inc(y_turn, 1)

            pe.wait_ge(ld_ident, 16)
            pe.wait_ge(key_rows, 1)
            for b in range(2):
                pe.transpose(pOJ[b][0:TP, 0:80], keyR[:, TP * b:TP * (b + 1)], ident[0:80, 0:80]).then_inc(key_turn, 1)
            pe.wait_ge(key_cols, 2)
            pe.wait_ge(const_set, 3)

            def edge_groups(lo, hi):
                for r in range(lo, hi + 2):
                    if r < hi:
                        if r >= 3:
                            pe.wait_ge(eq_done, r - 2)
                        pe.matmul(pS[0:TP, r % 3, 0:GE], ident[0:GROUPS, r:r + 1].to_broadcast((GROUPS, TP)), keyR[:],
                                  start=True, stop=True).then_inc(key_bc, 1)
                    if r - 2 >= lo:
                        q = r - 2
                        pe.wait_ge(eq_done, q + 1)
                        for c in range(2):
                            for b in range(2):
                                mm = pe.matmul(pO[0:TP, 2 * q + c:2 * q + c + 1], eqW[:, q % 4, b, TP * c:TP * (c + 1)],
                                               ones_b[0:TP, :], start=(b == 0), stop=(b == 1))
                        mm.then_inc(edge_sum, 1)

            edge_groups(*PARTS[0])
            pe.wait_ge(ld_cond, 16 * 7)
            pe.wait_ge(emb_sin, 1)
            for c, (c0, cn) in enumerate(CHUNKS):
                pe.matmul(pT[0:COND, c, 0:cn], fw1[:], embT[:, c0:c0 + cn], start=True, stop=True).then_inc(hid_mm, 1)
            edge_groups(*PARTS[1])
            for c, (c0, cn) in enumerate(CHUNKS):
                pe.wait_ge(hid_act, c + 1)
                pe.matmul(pT[0:96, c, 0:cn], fw2[:], hid[:, c0:c0 + cn], start=True, stop=True).then_inc(cond_mm, 1)
            edge_groups(*PARTS[2])
            pe.wait_ge(cond_act, 3)
            for t in range(NT):
                pe.wait_ge(x_norm, t + 1)
                if t >= 3:
                    pe.wait_ge(x_lo, t - 2)
                turn(pT[:, t % 3, :], g[:, t, :]).then_inc(x_turn, 1)
            pe.wait_ge(split_done, 4)
            pe.wait_ge(edge_idx, len(PARTS))

            def kv_products(t):
                pe.wait_ge(kv_norm, t + 1)
                k, v = kvh[:, t % 2, 0, :], kvh[:, t % 2, 1, :]
                for p in range(4):
                    cols = slice(128 * p, 128 * (p + 1))
                    pe.matmul(pT[:, 0, cols], v[:, cols], k[:, cols], start=(t == 0 and p == 0),
                              stop=(t == NT - 1), skip_group_check=True)
                    pe.matmul(pT[:, 1, p:p + 1], v[:, cols], ones[0:TP, 0:1], start=(t == 0 and p == 0),
                              stop=(t == NT - 1), skip_group_check=True)
                pe.matmul(pT[:, 2, :], ones[0:TP, :], k, start=(t == 0), stop=(t == NT - 1)).then_inc(kv_acc, 1)

            for t in range(NT):
                pe.wait_ge(x_lo, t + 1)
                if t >= 2:
                    pe.wait_ge(kv_norm, t - 1)
                for k in range(KD):
                    mm3(pS[0:TP, t % 2, :], y_tile(k, t), (wk_hi[:, k, :], wk_lo[:, k, :]), k == 0, k == KD - 1)
                for k in range(KD):
                    mm = mm3(pOJ[t % 2][0:TP, :], y_tile(k, t), (wv_hi[:, k, :], wv_lo[:, k, :]), k == 0, k == KD - 1)
                mm.then_inc(kv_mm, 1)
                if t == 0:
                    pe.wait_ge(x_lo, NT)
                if t:
                    kv_products(t - 1)
            kv_products(NT - 1)
            banks4 = [pS[:, 0, :], pS[:, 1, :], pS[:, 2, :], pJ[:, :]]
            pe.wait_ge(ld_mix, 16 * 7)
            pe.wait_ge(pv_ready, 1)
            for p in range(4):
                pe.matmul(banks4[p], pvk[:, p, :], mix_wo[:, p, :], start=True, stop=True).then_inc(pw_mm, 1)
            for m in range(4):
                pe.wait_ge(pw_out, 4)
                for p in range(4):
                    mm = pe.matmul(banks4[m], mix_wq[:, p, 128 * m:128 * (m + 1)], pvw[:, p, :],
                                   start=(p == 0), stop=(p == 3))
                mm.then_inc(we_mm, 1)
            pe.wait_ge(we_l, 4)
            pe.wait_ge(cond_done, 2)
            pe.wait_ge(split_done, 5)
            for t in range(NT):
                if t >= 2:
                    pe.wait_ge(mix_add, t - 1)
                dst = pOJ[t % 2][0:TP, :]
                pe.matmul(dst, at_tile(condS, t), aff1_hi[:, 2 * D:], start=True, stop=False)
                for k in range(KD):
                    mm = mm3(dst, y_tile(k, t), (we_hi[:, k, :], we_lo[:, k, :]), False, k == KD - 1)
                mm.then_inc(mix_mm, 1)
            for s in range(NT + 2):
                if 1 <= s <= NT:
                    affine(aff1_hi, s - 1, s - 1)
                if s >= 2:
                    ln_turn(aff1_hi, s - 2, s - 2)
            pe.drain().then_inc(block_done, 1)
            pe.wait_ge(block_go, 1)

            with pe.Fori(0, BLOCKS) as l:
                def qk_group(h, n):
                    w, c = divmod(n, 3)
                    c0, cn = CHUNKS[c]
                    if w == 1:
                        pe.wait_ge(qk_lo, 6 * h + c + 1)
                    elif h and c == 0:
                        pe.wait_ge(bsplit, head_piece[h] + 1)
                        pe.wait_ge(row_max, NT * h)
                    for k in range(KD):
                        mm = mm3(pS[:, c, 0:cn], (wA_hi[:, w, k, :], wA_lo[:, w, k, :]),
                                 (yT_hi[:, k, c0:c0 + cn], yT_lo[:, k, c0:c0 + cn]), k == 0, k == KD - 1)
                    mm.then_inc(qk_mm, 1)

                def v_group(h, c):
                    c0, cn = CHUNKS[c]
                    if c == 1 and h:
                        pe.wait_ge(o_done, PAIRS * h)
                    if c == 2 or h:
                        pe.wait_ge(v_act, 3 * h + (1 if c == 2 else 0))
                    for k in range(KD):
                        mm = mm3(pOJ[c % 2][:, 0:cn], (wA_hi[:, 2, k, :], wA_lo[:, 2, k, :]),
                                 (yT_hi[:, k, c0:c0 + cn], yT_lo[:, k, c0:c0 + cn]), k == 0, k == KD - 1)
                    mm.then_inc(v_mm, 1)

                def score(h, i):
                    if i == 0:
                        pe.wait_ge(qk_lo, 6 * h + 6)
                    else:
                        pe.wait_ge(row_max, NT * h + i)
                    for c in range(3):
                        cols = slice(SW * c, SW * (c + 1))
                        mm = mm3(pS[0:TP, c, 0:SW], (at_tile(qT_hi, i), at_tile(qT_lo, i)),
                                 (kT_hi[:, cols], kT_lo[:, cols]), True, True)
                    mm.then_inc(scores, 1)

                def turn_v(h):
                    pe.wait_ge(v_act, 3 * h + 3)
                    for j, ts in enumerate(groups_of(NT)):
                        if h:
                            pe.wait_ge(turn_lo, 33 * h + j - 2)
                        for t in ts:
                            mm = pe.transpose(pT[0:TP, j, 128 * (t % 4):128 * (t % 4 + 1)],
                                              at_tile(vT, t), ident[:, :])
                        mm.then_inc(turned, 1)

                def turn_p(h, i):
                    pe.wait_ge(exp_done, NT * h + i + 1)
                    for j, bs in enumerate(groups_of(NT)):
                        G = 33 * h + 3 + 3 * i + j
                        pe.wait_ge(turn_lo, G - 2)
                        for b in bs:
                            mm = pe.transpose(pT[0:TP, j, TP * (b % 4):TP * (b % 4 + 1)],
                                              at_tile(Pb[0:TP, i % 3, :], b), ident[0:TP, 0:TP])
                        mm.then_inc(turned, 1)

                def pv(h, p):
                    if p:
                        pe.wait_ge(o_done, PAIRS * h + p)
                    else:
                        pe.wait_ge(v_act, 3 * h + 2)
                    for b in range(NT):
                        if b % 4 == 0:
                            pe.wait_ge(turn_lo, 33 * h + 7 + 6 * p + b // 4)
                        mm3(pO[:, 0:250], (v_hi[:, b, :], v_lo[:, b, :]), (PT_hi[:, b, :], PT_lo[:, b, :]),
                            b == 0, b == NT - 1)
                    pe.wait_ge(diag_done, NT * h + 2 * p + 2)
                    for u in range(2):
                        mm = pe.matmul(pO[:, 250 + TP * u:250 + TP * (u + 1)], ones[0:TP, :],
                                       diag[:, (2 * p + u) % 4, :], start=True, stop=True)
                    mm.then_inc(pv_mm, 1)

                for c in range(3):
                    qk_group(0, c)
                for h in range(HEADS):
                    for c in range(3):
                        qk_group(h, 3 + c)
                    v_group(h, 0)
                    score(h, 0)
                    v_group(h, 1)
                    v_group(h, 2)
                    score(h, 1)
                    turn_v(h)
                    for i in range(2, NT):
                        score(h, i)
                        if i >= 4 and i % 2 == 0:
                            pv(h, i // 2 - 2)
                        turn_p(h, i - 2)
                    nxt = [lambda c=c: qk_group(h + 1, c) for c in range(3)] if h + 1 < HEADS else [lambda: None] * 3
                    nxt[0]()
                    pv(h, 3)
                    turn_p(h, 8)
                    nxt[1]()
                    turn_p(h, 9)
                    nxt[2]()
                    pv(h, 4)

                def bank(use):
                    n = use_of[use]
                    if n >= 2:
                        kind, i = uses[n - 2]
                        pe.wait_ge(m1_hi if kind == "m1" else g_add, i + 1)
                    return pOJ[n % 2]

                def out_proj(t):
                    if t == 0:
                        pe.wait_ge(o_done, PAIRS * HEADS)
                        pe.wait_ge(wo_in, 16)
                        pe.wait_ge(bsplit, AFF2 + 1)
                    dst = bank(("proj", t))[0:TP, :]
                    pe.matmul(dst, at_tile(condS, t), aff2_hi[:, 2 * D:], start=True, stop=False)
                    for k in range(KD):
                        mm = pe.matmul(dst, at_tile(oT[:, k, :], t), wo[:, k, :], start=False, stop=(k == KD - 1))
                    mm.then_inc(proj, 1)

                def mlp_out(t):
                    c, u = divmod(t, 2)
                    if t == 0:
                        pe.wait_ge(w2_lo_done, 1)
                    pe.wait_ge(m1_lo, 4 * (c + 1))
                    dst = bank(("proj", NT + t))[0:TP, :]
                    pe.matmul(dst, at_tile(condS, t), aff1_hi[:, 2 * D:], start=True, stop=False)
                    for k in range(KD):
                        mm = mm3(dst, (at_tile(hT_hi[:, c % 2, k, :], u), at_tile(hT_lo[:, c % 2, k, :], u)),
                                 (w2_hi[:, k, :], w2_lo[:, k, :]), False, k == KD - 1)
                    mm.then_inc(proj, 1)

                def mlp_in(i):
                    c, m = divmod(i, 4)
                    if i == 0:
                        pe.wait_ge(bsplit, W1C + 1)
                    pe.wait_ge(y_lo, 2 * c + 2)
                    dst = bank(("m1", i))[:, 0:250]
                    cols, nodes = slice(128 * m, 128 * (m + 1)), slice(250 * c, 250 * (c + 1))
                    for k in range(KD):
                        mm = mm3(dst, (w1_hi[:, k, cols], w1_lo[:, k, cols]),
                                 (yT_hi[:, k, nodes], yT_lo[:, k, nodes]), k == 0, k == KD - 1)
                    mm.then_inc(m1_mm, 1)

                for s in range(NT + 2):
                    if s < NT:
                        out_proj(s)
                    if 1 <= s <= NT:
                        affine(aff2_hi, s - 1, s - 1)
                    if s >= 2:
                        ln_turn(aff2_hi, s - 2, s - 2)
                for kind, i in mlp_order:
                    if kind == "m1":
                        mlp_in(i)
                        continue
                    if i < NT:
                        mlp_out(i)
                    if 1 <= i <= NT:
                        affine(aff1_hi, NT + i - 1, i - 1)
                    if i >= 2:
                        ln_turn(aff1_hi, NT + i - 2, i - 2)
                pe.drain().then_inc(block_done, 1)
                pe.wait_ge(block_go, l + 2)

            for t in range(NT):
                pe.wait_ge(f_norm, t + 1)
                if t >= 3:
                    pe.wait_ge(f_lo, t - 2)
                turn(pT[:, t % 3, :], xm[:, t % 2, :]).then_inc(f_turn, 1)
            pe.wait_ge(f_split, 1)
            pe.wait_ge(f_lo, NT)
            for c, (c0, cn) in enumerate(CHUNKS):
                for k in range(KD):
                    mm = mm3(pS[:, c, 0:cn], (wr_hi[:, k, :], wr_lo[:, k, :]),
                             (yT_hi[:, k, c0:c0 + cn], yT_lo[:, k, c0:c0 + cn]), k == 0, k == KD - 1)
                mm.then_inc(f_log, 1)

            def expert_in(e):
                pe.wait_ge(f_split, piece_of[("1", e)] + 1)
                for i in range(6):
                    m, c = divmod(i, 3)
                    c0, cn = CHUNKS[c]
                    n = 6 * e + i
                    if n < 3:
                        pe.wait_ge(f_logc, c + 1)
                    else:
                        pe.wait_ge(f_h, n - 2)
                    cols = slice(128 * m, 128 * (m + 1))
                    for k in range(KD):
                        mm = mm3(pS[:, c, 0:cn], (eW1_hi[:, k, cols], eW1_lo[:, k, cols]),
                                 (yT_hi[:, k, c0:c0 + cn], yT_lo[:, k, c0:c0 + cn]), k == 0, k == KD - 1)
                    mm.then_inc(f_m1, 1)

            def expert_out(e):
                pe.wait_ge(f_hlo, 6 * e + 6)
                pe.wait_ge(f_split, piece_of[("2", e)] + 1)
                hi, lo = hidden(e)
                for t in range(NT):
                    n = NT * e + t
                    if n >= 2:
                        pe.wait_ge(f_acc, n - 1)
                    for k in range(2):
                        mm = mm3(pOJ[t % 2][0:TP, :],
                                 (at_tile(hi[:, k, :], t), at_tile(lo[:, k, :], t)),
                                 (eW2_hi[:, k, :], eW2_lo[:, k, :]), k == 0, k == 1)
                    mm.then_inc(f_m2, 1)

            expert_in(0)
            pe.wait_ge(f_prob, 1)
            for t in range(NT):
                mm = pe.transpose(pT[0:TP, 0, 8 * t:8 * (t + 1)], at_tile(prT, t), ident[0:8, 0:8])
            mm.then_inc(f_pturn, 1)
            for e in (1, 2, 3):
                expert_in(e)
            pe.wait_ge(f_thr, 1)
            pe.transpose(pT[0:TP, 1, 0:EXPERTS], thrB[:], ident[0:EXPERTS, 0:EXPERTS]).then_inc(f_thrturn, 1)
            pe.wait_ge(f_above, 1)
            pe.wait_ge(f_ld, 48)
            total = pT[0:TP, 0, 0:EXPERTS]
            for t in range(NT):
                pe.matmul(total, ones[0:TP, 0:TP], above[:, t, :], start=(t == 0), stop=(t == NT - 1))
            pe.matmul(pT[0:TP, 2, 0:8 * NT], before[:], equal[:].rearrange("p t e -> p (t e)"), start=True, stop=False,
                      skip_group_check=True)
            for t in range(NT - 1):
                mm = pe.matmul(pT[0:TP, 2, 8 * (t + 1):8 * NT], ones[0:TP, 0:TP],
                               equal[:, t, :].unsqueeze(1).to_broadcast((TP, NT - 1 - t, EXPERTS)),
                               start=False, stop=(t == NT - 2), skip_group_check=True)
            mm.then_inc(f_placed, 1)
            for e in range(EXPERTS):
                expert_out(e)
                if e + 4 < EXPERTS:
                    expert_in(e + 4)
            pe.wait_ge(f_gate, 1)
            for t in range(NT):
                mm = pe.transpose(pS[0:EXPERTS, t // 4, TP * (t % 4):TP * (t % 4 + 1)], gate[:, t, :], ident[0:TP, 0:TP])
            mm.then_inc(f_gturn, 1)
            pe.wait_ge(f_gt, 1)
            pe.wait_ge(f_ld, 48)
            pe.wait_ge(f_acc, NT * EXPERTS)
            for t in range(NT):
                if t >= 2:
                    pe.wait_ge(f_fin, t - 1)
                pe.matmul(pOJ[t % 2][0:TP, :], at_tile(gateT, t), fb2[:], start=True, stop=True).then_inc(f_b2, 1)

        @block.scalar
        def _(act):
            A = nc.scalar.activation
            act.wait_ge(emb_arg, 1)
            A(embT[:], embT[:], ACT.Sin).then_inc(emb_sin, 1)
            for c, (c0, cn) in enumerate(CHUNKS):
                act.wait_ge(hid_mm, c + 1)
                A(hid[:, c0:c0 + cn], pT[0:COND, c, 0:cn], ACT.Silu, bias=fsmall[0:COND, 3:4]).then_inc(hid_act, 1)
            for c, (c0, cn) in enumerate(CHUNKS):
                act.wait_ge(cond_mm, c + 1)
                A(condF[:, c0:c0 + cn], pT[0:96, c, 0:cn], ACT.Identity, bias=fb[:, 0:1]).then_inc(cond_act, 1)

            def hi_tile(G, t, s_in, s_out):
                act.wait_ge(s_in, G + 1)
                A(yT_hi[:, :, TP * t:TP * (t + 1)], turned_tile(G), ACT.Copy).then_inc(s_out, 1)

            for n in range(4):
                act.wait_ge(w_cent, n + 1)
                dst = (wk_hi, wv_hi)[n // 2][:].rearrange("p k n -> p (k n)")[:, 1024 * (n % 2):1024 * (n % 2 + 1)]
                A(dst, stage[:, 0:1024], ACT.Copy).then_inc(w_hi, 1)
            for t in range(NT):
                hi_tile(t, t, x_turn, x_hi)
            act.wait_ge(stage_in, 16 * 5)
            A(aff1_hi[:], stage[0:96, :], ACT.Copy).then_inc(w_hi, 1)
            for t in range(NT):
                act.wait_ge(kv_mm, t + 1)
                if t:
                    act.wait_ge(kv_var, t)
                A(kvq[:, 0, :], pS[0:TP, t % 2, :], ACT.Square)
                A(kvq[:, 1, :], pOJ[t % 2][0:TP, :], ACT.Square).then_inc(kv_sq, 1)
                act.wait_ge(kv_var, t + 1)
                A(ms8[:, :, 2, :], ms8[:, :, 1, :], ACT.Sqrt).then_inc(kv_std, 1)
            for p in range(4):
                act.wait_ge(pw_mm, p + 1)
                A(pvw[:, p, :], (pS[:, p, :] if p < 3 else pJ[:, :]), ACT.Copy).then_inc(pw_out, 1)
            for m in range(4):
                act.wait_ge(we_mm, m + 1)
                A(we_hi[:, m, :], (pS[:, m, :] if m < 3 else pJ[:, :]), ACT.Copy).then_inc(we_h, 1)

            for t in range(NT):
                hi_tile(t, t, y_turn, y_hi)
            for t in range(NT):
                act.wait_ge(l_sum, t + 1)
                if t >= 2:
                    act.wait_ge(l_done, t - 1)
                A(lnc[:, t % 2, :], L[:, t, :], ACT.Ln, bias=tiny).then_inc(l_ln, 1)
            act.drain().then_inc(block_done, 1)
            act.wait_ge(block_go, 1)

            with act.Fori(0, BLOCKS) as l:
                act.wait_ge(bias_in, 16)

                def qk_out(h, n):
                    w, c = divmod(n, 3)
                    c0, cn = CHUNKS[c]
                    act.wait_ge(qk_mm, 6 * h + n + 1)
                    dst = (qT_hi, kT_hi)[w][:, c0:c0 + cn]
                    A(dst, pS[:, c, 0:cn], ACT.Identity, bias=lbias[:, 4 * w + h:4 * w + h + 1]).then_inc(qk_hi, 1)

                def v_out(h, c):
                    c0, cn = CHUNKS[c]
                    act.wait_ge(v_mm, 3 * h + c + 1)
                    A(vT[:, c0:c0 + cn], pOJ[c % 2][:, 0:cn], ACT.Identity, bias=lbias[:, 8 + h:9 + h]).then_inc(v_act, 1)

                def exp(h, i):
                    act.wait_ge(neg_max, NT * h + i + 1)
                    p = Pb[0:TP, i % 3, 0:N]
                    A(p, p, ACT.Exp, bias=negm[:, i:i + 1], scale=SCALE, accum_out=den[:, i:i + 1]).then_inc(exp_done, 1)

                def v_turned(h):
                    for j, ts in enumerate(groups_of(NT)):
                        act.wait_ge(turned, 33 * h + j + 1)
                        n = len(ts)
                        A(v_hi[:, ts[0]:ts[0] + n, :], pT[0:TP, j, 0:128 * n].rearrange("p (t d) -> p t d", d=128),
                          ACT.Copy).then_inc(turn_hi, 1)

                def p_turned(h, i):
                    for j, bs in enumerate(groups_of(NT)):
                        act.wait_ge(turned, 33 * h + 4 + 3 * i + j)
                        n, u = len(bs), TP * (i % 2)
                        A(PT_hi[:, bs[0]:bs[0] + n, u:u + TP],
                          pT[0:TP, j, 0:TP * n].rearrange("p (b s) -> p b s", s=TP), ACT.Copy).then_inc(turn_hi, 1)

                def rden_out(h, p):
                    act.wait_ge(pv_mm, PAIRS * h + p + 1)
                    if h or p:
                        act.wait_ge(o_done, PAIRS * h + p)
                    A(rb[:], pO[:, 250:500], ACT.Copy).then_inc(rb_copied, 1)

                for c in range(3):
                    qk_out(0, c)
                for h in range(HEADS):
                    for c in range(3):
                        qk_out(h, 3 + c)
                    for c in range(3):
                        v_out(h, c)
                    exp(h, 0)
                    v_turned(h)
                    exp(h, 1)
                    for i in range(2, NT):
                        exp(h, i)
                        if i >= 4 and i % 2 == 0:
                            rden_out(h, i // 2 - 2)
                        p_turned(h, i - 2)
                    more = h + 1 < HEADS
                    if more:
                        qk_out(h + 1, 0)
                    rden_out(h, 3)
                    p_turned(h, 8)
                    if more:
                        qk_out(h + 1, 1)
                    p_turned(h, 9)
                    if more:
                        qk_out(h + 1, 2)
                    rden_out(h, 4)
                for t in range(NT):
                    hi_tile(t, t, y_turn, y_hi)
                act.wait_ge(w2_in, 16)
                act.wait_ge(proj, NT)
                A(w2_hi[:], w2_raw[:], ACT.Copy).then_inc(w2_hi_done, 1)
                for kind, i in mlp_order:
                    if kind == "m1":
                        c, m = divmod(i, 4)
                        src = pOJ[use_of[("m1", i)] % 2][:, 0:250]
                        act.wait_ge(m1_mm, i + 1)
                        if i >= 2:
                            act.wait_ge(m1_lo, i - 1)
                        if c >= 2 and m == 0:
                            act.wait_ge(proj, NT + 2 * (c - 1))
                        A(fT[:, i % 2, :], src, ACT.Relu, bias=lbias[:, 12 + m:13 + m])
                        A(hT_hi[:, c % 2, m, :], src, ACT.Relu, bias=lbias[:, 12 + m:13 + m]).then_inc(m1_hi, 1)
                    elif i >= 2:
                        hi_tile(NT + i - 2, i - 2, y_turn, y_hi)
                act.drain().then_inc(block_done, 1)
                act.wait_ge(block_go, l + 2)

            for t in range(NT):
                hi_tile(t, t, f_turn, f_hi)
            for c, (c0, cn) in enumerate(CHUNKS):
                act.wait_ge(f_log, c + 1)
                A(logT[:, c0:c0 + cn], pS[0:EXPERTS, c, 0:cn], ACT.Copy).then_inc(f_logc, 1)
            act.wait_ge(f_nmax, 1)
            A(prT[:], logT[:], ACT.Exp, bias=fstat[0:EXPERTS, 16:17], accum_out=fstat[0:EXPERTS, 17:18]).then_inc(f_exp, 1)
            act.wait_ge(f_ld, 48)

            def expert_act(e):
                for i in range(6):
                    m, c = divmod(i, 3)
                    c0, cn = CHUNKS[c]
                    n = 6 * e + i
                    act.wait_ge(f_m1, n + 1)
                    if n >= 2:
                        act.wait_ge(f_hlo, n - 1)
                    if i == 0 and e >= 4:
                        act.wait_ge(f_m2, NT * (e - 3))
                    b = fstat[:, 2 * e + m:2 * e + m + 1]
                    A(hF[:, n % 2, 0:cn], pS[:, c, 0:cn], ACT.Gelu, bias=b)
                    A(hidden(e)[0][:, m, c0:c0 + cn], pS[:, c, 0:cn], ACT.Gelu, bias=b).then_inc(f_h, 1)

            expert_act(0)
            act.wait_ge(f_pturn, 1)
            A(prC[:].rearrange("p t e -> p (t e)"), pT[0:TP, 0, 0:8 * NT], ACT.Copy).then_inc(f_prc, 1)
            for e in range(1, EXPERTS):
                expert_act(e)
            act.wait_ge(f_gturn, 1)
            for c, (c0, cn) in enumerate(CHUNKS):
                ins = A(gateT[:, c0:c0 + cn], pS[0:EXPERTS, c, 0:cn], ACT.Copy)
            ins.then_inc(f_gt, 1)

        @block.vector
        def _(dve):
            ch = outer = Chain(dve, dchain)
            link = ch.link

            def newton(r, r_in, v, tmp):
                link(dve.tensor_tensor(tmp, r_in, r_in, ALU.mult))
                link(dve.tensor_tensor(tmp, tmp, v, ALU.mult))
                link(dve.tensor_scalar(tmp, tmp, -0.5, 1.5, ALU.mult, ALU.add))
                link(dve.tensor_tensor(r, r_in, tmp, ALU.mult))

            def lo_tile(G, t, s_in, s_out):
                dve.wait_ge(s_in, G + 1)
                cols = slice(TP * t, TP * (t + 1))
                dve.tensor_tensor(yT_lo[:, :, cols], turned_tile(G), yT_hi[:, :, cols].bitcast(F32), ALU.subtract).then_inc(s_out, 1)

            dve.memset(zrow[:], 0.0).then_inc(zrow_set, 1)
            dve.memset(halves, -0.5).then_inc(const_set, 1)
            dve.memset(ones[:], 1.0).then_inc(const_set, 1)
            dve.memset(ones_b[:], 1.0).then_inc(const_set, 1)
            dve.memset(tiny, 1e-30).then_inc(const_set, 1)
            dve.wait_ge(ld_edge, 64)
            dve.scalar_tensor_tensor(out=keyR[:], in0=srcR[:, 0, :], scalar=float(NPAD), in1=srcR[:, 1, :],
                                     op0=ALU.mult, op1=ALU.add).then_inc(key_rows, 1)
            for b in range(2):
                dve.wait_ge(key_turn, b + 1)
                dve.tensor_copy(keyC[:, :, b], pOJ[b][0:TP, 0:80]).then_inc(key_cols, 1)
            dve.wait_ge(key_cols, 2)
            kc = keyC[:].rearrange("p a b -> p (a b)")

            def edge_groups(lo, hi):
                for r in range(lo, hi):
                    dve.wait_ge(key_bc, r + 1)
                    if r >= 4:
                        dve.wait_ge(edge_sum, r - 3)
                    for b in range(2):
                        ins = dve.scalar_tensor_tensor(out=eqW[:, r % 4, b, :], in0=pS[0:TP, r % 3, 0:GE],
                                                       scalar=keyC[:, r, b:b + 1], in1=order[:, b, :],
                                                       op0=ALU.is_equal, op1=ALU.mult)
                    ins.then_inc(eq_done, 1)
                cols = slice(2 * lo, 2 * hi)
                dve.wait_ge(edge_sum, hi)
                link(dve.tensor_scalar(bef[:, cols], pO[0:TP, cols], 0.0, None, ALU.is_gt))
                link(dve.tensor_copy(cnt[:, cols], pO[0:TP, cols]))
                link(dve.scalar_tensor_tensor(out=bef[:, cols], in0=kc[:, cols], scalar=trash[:, 0:1], in1=bef[:, cols],
                                              op0=ALU.subtract, op1=ALU.mult))
                dve.tensor_scalar(idxU[:, cols], bef[:, cols], trash[:, 0:1], None, ALU.add).then_inc(edge_idx, 1)

            edge_groups(*PARTS[0])
            dve.wait_ge(ld_cond, 16 * 7)
            link(dve.tensor_scalar(embT[:], embT[:], fsmall[:, 0:1], None, ALU.mult))
            link(dve.tensor_scalar(embK[:], embT[:], 1.0 / TURN, fsmall[:, 1:2], ALU.mult, ALU.add))
            link(dve.tensor_scalar(embK[:], embK[:], ROUNDER, None, ALU.add))
            link(dve.tensor_scalar(embK[:], embK[:], -ROUNDER, None, ALU.add))
            for part in TURN_PARTS:
                link(dve.scalar_tensor_tensor(out=embT[:], in0=embK[:], scalar=-part, in1=embT[:],
                                              op0=ALU.mult, op1=ALU.add))
            link(dve.tensor_scalar(embT[:], embT[:], fsmall[:, 2:3], PI_BELOW, ALU.add, ALU.min))
            dve.tensor_scalar(embT[:], embT[:], -PI_BELOW, None, ALU.max).then_inc(emb_arg, 1)
            edge_groups(*PARTS[1])
            dve.wait_ge(ld_x, 16)

            def stats(t, src):
                link(dve.bn_stats(st6[:, t % 2, :], src))
                link(dve.bn_aggr(mv[:, t, :], st6[:, t % 2, :]))

            for t in range(NT):
                stats(t, g[:, t, :])
            dve.tensor_scalar(ve, mv[:, :, 1], EPS, None, ALU.add).then_inc(x_ve, 1)
            dve.wait_ge(cond_act, 3)
            link(dve.memset(condS[:, N:].bitcast(F32), 0.0))
            dve.tensor_copy(condS[:, 0:N], condF[:]).then_inc(cond_done, 1)
            dve.wait_ge(cond_done, 1)
            dve.tensor_tensor(condS[32:64, 0:N], condF[32:64, :], condS[32:64, 0:N].bitcast(F32), ALU.subtract
                              ).then_inc(cond_done, 1)
            edge_groups(*PARTS[2])
            for n in range(4):
                part = stage[:, 0:1024].rearrange("p (h d) -> p h d", d=MD)
                dve.wait_ge(stage_in, 16 * (n + 1))
                link(dve.tensor_reduce(wmean, part, AX.X, ALU.add))
                link(dve.tensor_scalar(wmean, wmean, 1.0 / MD, None, ALU.mult))
                dve.tensor_tensor(part, part, wmean.unsqueeze(2).to_broadcast((128, 16, MD)), ALU.subtract
                                  ).then_inc(w_cent, 1)
                dve.wait_ge(w_hi, n + 1)
                cols = slice(1024 * (n % 2), 1024 * (n % 2 + 1))
                hi, lo = [ap[:].rearrange("p k n -> p (k n)")[:, cols] for ap in ((wk_hi, wk_lo), (wv_hi, wv_lo))[n // 2]]
                dve.tensor_tensor(lo, stage[:, 0:1024], hi.bitcast(F32), ALU.subtract).then_inc(split_done, 1)
            dve.wait_ge(x_pow, 1)
            newton(rstd, r0, ve, rt)
            for t in range(NT):
                dve.tensor_scalar(g[:, t, :], g[:, t, :], mv[:, t, 0:1], rstd[:, t:t + 1], ALU.subtract, ALU.mult
                                  ).then_inc(x_norm, 1)
                if t >= 1:
                    lo_tile(t - 1, t - 1, x_hi, x_lo)
            lo_tile(NT - 1, NT - 1, x_hi, x_lo)
            dve.wait_ge(x_norm, NT)
            for t in range(NT):
                stats(t, g[:, t, :])
            dve.tensor_scalar(ve, mv[:, :, 1], EPS, None, ALU.add).then_inc(var_done, 1)
            dve.wait_ge(w_hi, 5)
            dve.tensor_tensor(aff1_hi[64:96, :], stage[64:96, :], aff1_hi[64:96, :].bitcast(F32), ALU.subtract
                              ).then_inc(split_done, 1)
            by_head = lambda ap: ap.rearrange("p (h d) -> p h d", h=MH)
            wide = lambda ap: ap.unsqueeze(2).to_broadcast((TP, MH, MD))
            for t in range(NT):
                src = [pS[0:TP, t % 2, :], pOJ[t % 2][0:TP, :]]
                dve.wait_ge(kv_sq, t + 1)
                for w in range(2):
                    link(dve.tensor_reduce(ms8[:, w, 1, :], by_head(kvq[:, w, :]), AX.X, ALU.add))
                dve.tensor_scalar(ms8[:, :, 1, :], ms8[:, :, 1, :], 1.0 / MD, EPS, ALU.mult, ALU.add).then_inc(kv_var, 1)
                dve.wait_ge(kv_std, t + 1)
                link(dve.reciprocal(ms8[:, :, 3, :], ms8[:, :, 2, :]))
                newton(ms8[:, :, 4, :], ms8[:, :, 3, :], ms8[:, :, 1, :], ms8[:, :, 2, :])
                if t >= 2:
                    dve.wait_ge(kv_acc, t - 1)
                link(dve.tensor_tensor(by_head(kvh[:, t % 2, 0, :]), by_head(src[0]), wide(ms8[:, 0, 4, :]), ALU.mult))
                dve.tensor_tensor(by_head(kvh[:, t % 2, 1, :]), by_head(src[1]), wide(ms8[:, 1, 4, :]), ALU.mult
                                  ).then_inc(kv_norm, 1)
            dve.wait_ge(ld_mix, 16 * 7)
            dve.wait_ge(kv_acc, NT)
            gk, bk = mrow[:, 0, :], mrow[:, 1, :]
            row = lambda ap: ap[:].rearrange("p k n -> p (k n)")
            for p in range(4):
                link(dve.tensor_scalar(pvk[:, p, :], pT[:, 0, 128 * p:128 * (p + 1)], mcol[:, 0, p:p + 1], None, ALU.mult))
            link(dve.tensor_tensor(row(pvk), row(pvk), gk, ALU.mult))
            link(dve.tensor_tensor(row(pvu), pT[:, 2, :], gk, ALU.mult))
            link(dve.scalar_tensor_tensor(out=row(pvu), in0=bk, scalar=float(N), in1=row(pvu), op0=ALU.mult, op1=ALU.add))
            link(dve.tensor_tensor(mcol[:, 2, :], pT[:, 1, 0:4], mcol[:, 0, :], ALU.mult))
            for p in range(4):
                link(dve.scalar_tensor_tensor(out=pvk[:, p, :], in0=pvu[:, p, :], scalar=mcol[:, 1, p:p + 1],
                                              in1=pvk[:, p, :], op0=ALU.mult, op1=ALU.add))
                link(dve.scalar_tensor_tensor(out=pvk[:, p, :], in0=bk[:, 128 * p:128 * (p + 1)],
                                              scalar=mcol[:, 2, p:p + 1], in1=pvk[:, p, :], op0=ALU.mult, op1=ALU.add))
            dve.tensor_tensor(pvk[:], pvk[:], hmask[:].unsqueeze(1).to_broadcast((128, 4, 128)), ALU.mult
                              ).then_inc(pv_ready, 1)
            for m in range(4):
                dve.wait_ge(we_h, m + 1)
                dve.tensor_tensor(we_lo[:, m, :], (pS[:, m, :] if m < 3 else pJ[:, :]), we_hi[:, m, :].bitcast(F32),
                                  ALU.subtract).then_inc(we_l, 1)
            for t in range(NT):
                dve.wait_ge(xr_in[t % 2], 16 * (t // 2 + 1))
                dve.wait_ge(mix_mm, t + 1)
                dve.tensor_tensor(xr[:, t % 2, :], xr[:, t % 2, :], pOJ[t % 2][0:TP, :], ALU.add).then_inc(mix_add, 1)

            def ln_stats(base, s):
                link(dve.bn_stats(st6[:, s % 2, :], g[:, s, :]))
                link(dve.bn_aggr(mv[:, s, :], st6[:, s % 2, :]))
                dve.tensor_scalar(ve[:, s:s + 1], mv[:, s, 1:2], EPS, None, ALU.add).then_inc(var_done, 1)

            def ln_finish(base, s, each=True):
                if 1 <= s <= NT:
                    t, G = s - 1, base + s - 1
                    c = slice(t, t + 1)
                    if each:
                        dve.wait_ge(pow_done, G + 1)
                        newton(rstd[:, c], r0[:, c], ve[:, c], rt[:, c])
                    if G:
                        dve.wait_ge(y_scaled, G)
                    link(dve.tensor_scalar(xh[:], g[:, t, :], mv[:, t, 0:1], rstd[:, c], ALU.subtract, ALU.mult))
                    dve.wait_ge(aff_mm, G + 1)
                    if G >= 2:
                        dve.wait_ge(y_turn, G - 1)
                    dve.scalar_tensor_tensor(out=y1[:, t % 2, :], in0=pS[0:TP, G % 2, :], scalar=1.0, in1=xh[:],
                                             op0=ALU.add, op1=ALU.mult).then_inc(y_scaled, 1)
                if s >= 2:
                    lo_tile(base + s - 2, s - 2, y_hi, y_lo)

            dve.wait_ge(pow_done, 1)
            dve.wait_ge(var_done, 1)
            newton(rstd, r0, ve, rt)
            for s in range(1, NT + 2):
                ln_finish(0, s, each=False)
            def ln_counts(t):
                dve.wait_ge(l_ln, t + 1)
                dve.scalar_tensor_tensor(out=L[:, t, :], in0=lnc[:, t % 2, :], scalar=1.0 / SCALE,
                                         in1=mask[:, t % 2, :], op0=ALU.mult, op1=ALU.add).then_inc(l_done, 1)

            for t in range(NT):
                if t % 2 == 0:
                    dve.wait_ge(tab_in[t // 2], 32)
                dve.tensor_tensor(L[:, t, :], L[:, t, :], tab2[:, t, :], ALU.add).then_inc(l_sum, 1)
                dve.wait_ge(l_sum, t + 1)
                link(dve.tensor_scalar(mask[:, t % 2, :], L[:, t, :], 0.5, MASKED, ALU.is_lt, ALU.mult))
                if t:
                    ln_counts(t - 1)
            ln_counts(NT - 1)
            dve.wait_ge(l_done, NT)
            dve.drain().then_inc(block_done, 1)
            dve.wait_ge(block_go, 1)

            with dve.Fori(0, BLOCKS) as l:
                ch = Chain(dve, lchain)
                link = ch.link
                link(dve.memset(kT_hi[:, N:NPAD].bitcast(F32), 0.0))
                link(dve.memset(kT_lo[:, N:NPAD].bitcast(F32), 0.0))
                dve.wait_ge(bias_in, 16)

                def qk_rest(h, n):
                    w, c = divmod(n, 3)
                    c0, cn = CHUNKS[c]
                    dve.wait_ge(qk_hi, 6 * h + n + 1)
                    hi, lo = ((qT_hi, qT_lo), (kT_hi, kT_lo))[w]
                    dve.scalar_tensor_tensor(out=lo[:, c0:c0 + cn], in0=pS[:, c, 0:cn],
                                             scalar=lbias[:, 4 * w + h:4 * w + h + 1],
                                             in1=hi[:, c0:c0 + cn].bitcast(F32), op0=ALU.add, op1=ALU.subtract
                                             ).then_inc(qk_lo, 1)

                def masked_max(h, i):
                    dve.wait_ge(scores, NT * h + i + 1)
                    if i >= 3:
                        dve.wait_ge(turned, 33 * h + 3 * i - 3)
                    elif i == 2:
                        dve.wait_ge(turned, 33 * h + 3)
                    elif i == 0 and h:
                        dve.wait_ge(turned, 33 * h)
                    dve.tensor_tensor_reduce(
                        out=Pb[0:TP, i % 3, 0:NPAD].rearrange("p (c n) -> p c n", c=3), in0=pS[0:TP, :, 0:SW],
                        in1=L[:, i, :].rearrange("p (c n) -> p c n", c=3), scale=1.0, scalar=2 * MASKED,
                        op0=ALU.add, op1=ALU.max, accum_out=rowmax[:, i:i + 1]).then_inc(row_max, 1)
                    dve.wait_ge(row_max, NT * h + i + 1)
                    dve.tensor_scalar(negm[:, i:i + 1], rowmax[:, i:i + 1], 0.1 * MASKED, -SCALE, ALU.max, ALU.mult
                                      ).then_inc(neg_max, 1)

                def inverse(h, i):
                    dve.wait_ge(exp_done, NT * h + i + 1)
                    link(dve.tensor_scalar(dmax[:, i:i + 1], den[:, i:i + 1], 1e-30, None, ALU.max))
                    link(dve.reciprocal(rden[:, i:i + 1], dmax[:, i:i + 1]))
                    dve.tensor_scalar(diag[:, i % 4, :], ident[0:TP, 0:TP], rden[:, i:i + 1], None, ALU.mult
                                      ).then_inc(diag_done, 1)

                def v_rest(h):
                    for j, ts in enumerate(groups_of(NT)):
                        dve.wait_ge(turn_hi, 33 * h + j + 1)
                        n = len(ts)
                        dve.tensor_tensor(v_lo[:, ts[0]:ts[0] + n, :],
                                          pT[0:TP, j, 0:128 * n].rearrange("p (t d) -> p t d", d=128),
                                          v_hi[:, ts[0]:ts[0] + n, :].bitcast(F32), ALU.subtract).then_inc(turn_lo, 1)

                def p_rest(h, i):
                    for j, bs in enumerate(groups_of(NT)):
                        dve.wait_ge(turn_hi, 33 * h + 4 + 3 * i + j)
                        n, u = len(bs), TP * (i % 2)
                        dst = (slice(None), slice(bs[0], bs[0] + n), slice(u, u + TP))
                        dve.tensor_tensor(PT_lo[dst], pT[0:TP, j, 0:TP * n].rearrange("p (b s) -> p b s", s=TP),
                                          PT_hi[dst].bitcast(F32), ALU.subtract).then_inc(turn_lo, 1)

                def o_out(h, p):
                    dve.wait_ge(rb_copied, PAIRS * h + p + 1)
                    dve.tensor_tensor(oT[:, h, 250 * p:250 * (p + 1)], pO[:, 0:250], rb[:], ALU.mult).then_inc(o_done, 1)

                for c in range(3):
                    qk_rest(0, c)
                for h in range(HEADS):
                    for c in range(3):
                        qk_rest(h, 3 + c)
                    masked_max(h, 0)
                    masked_max(h, 1)
                    v_rest(h)
                    for i in range(2, NT):
                        masked_max(h, i)
                        if i == 2:
                            inverse(h, 0)
                        inverse(h, i - 1)
                        if i >= 4 and i % 2 == 0:
                            o_out(h, i // 2 - 2)
                        p_rest(h, i - 2)
                    more = h + 1 < HEADS
                    inverse(h, 9)
                    if more:
                        qk_rest(h + 1, 0)
                    o_out(h, 3)
                    p_rest(h, 8)
                    if more:
                        qk_rest(h + 1, 1)
                    p_rest(h, 9)
                    if more:
                        qk_rest(h + 1, 2)
                    o_out(h, 4)

                def g_sum(G, s):
                    dve.wait_ge(proj, G + 1)
                    if G == 0:
                        dve.wait_ge(g_in[0], 16)
                    if G == 2:
                        dve.wait_ge(g_in[1], 16)
                    dve.tensor_tensor(g[:, s, :], g[:, s, :], pOJ[use_of[("proj", G)] % 2][0:TP, :], ALU.add
                                      ).then_inc(g_add, 1)
                    dve.wait_ge(g_add, G + 1)

                for s in range(NT + 2):
                    if s < NT:
                        g_sum(s, s)
                        ln_stats(0, s)
                    ln_finish(0, s)
                dve.wait_ge(w2_hi_done, 1)
                dve.wait_ge(y_turn, NT)
                dve.tensor_tensor(w2_lo[:], w2_raw[:], w2_hi[:].bitcast(F32), ALU.subtract).then_inc(w2_lo_done, 1)
                for kind, i in mlp_order:
                    if kind == "m1":
                        c, m = divmod(i, 4)
                        dve.wait_ge(m1_hi, i + 1)
                        dve.tensor_tensor(hT_lo[:, c % 2, m, :], fT[:, i % 2, :], hT_hi[:, c % 2, m, :].bitcast(F32),
                                          ALU.subtract).then_inc(m1_lo, 1)
                    else:
                        if i < NT:
                            g_sum(NT + i, i)
                            ln_stats(NT, i)
                        ln_finish(NT, i)
                dve.drain().then_inc(block_done, 1)
                dve.wait_ge(block_go, l + 2)

            ch = outer
            link = ch.link
            for t in range(NT):
                dve.wait_ge(f_in[t % 2], 16 * (t // 2 + 1))
                dve.tensor_tensor(g[:, t, :], g[:, t, :], xm[:, t % 2, :], ALU.add).then_inc(f_add, 1)
                dve.wait_ge(f_add, t + 1)
                stats(t, g[:, t, :])
            dve.tensor_scalar(ve, mv[:, :, 1], EPS, None, ALU.add).then_inc(f_ve, 1)
            dve.wait_ge(f_pow, 1)
            dve.wait_ge(f_ve, 1)
            newton(rstd, r0, ve, rt)
            for t in range(NT):
                if t >= 2:
                    dve.wait_ge(f_turn, t - 1)
                dve.tensor_scalar(xm[:, t % 2, :], g[:, t, :], mv[:, t, 0:1], rstd[:, t:t + 1], ALU.subtract, ALU.mult
                                  ).then_inc(f_norm, 1)
                if t >= 1:
                    lo_tile(t - 1, t - 1, f_hi, f_lo)
            lo_tile(NT - 1, NT - 1, f_hi, f_lo)
            dve.wait_ge(f_ld, 48)
            dve.wait_ge(f_logc, 3)
            link(dve.tensor_reduce(fstat[0:EXPERTS, 18:19], logT[:], AX.X, ALU.max))
            dve.tensor_scalar(fstat[0:EXPERTS, 16:17], fstat[0:EXPERTS, 18:19], -1.0, None, ALU.mult).then_inc(f_nmax, 1)
            dve.wait_ge(f_exp, 1)
            link(dve.reciprocal(fstat[0:EXPERTS, 19:20], fstat[0:EXPERTS, 17:18]))
            dve.tensor_scalar(prT[:], prT[:], fstat[0:EXPERTS, 19:20], None, ALU.mult).then_inc(f_prob, 1)
            thr, cand, kept, bit, many = [fstat[0:EXPERTS, 20 + n:21 + n] for n in range(5)]
            link(dve.memset(thr, 0.0))
            link(dve.memset(bit, 2.0 ** -63))
            with dve.Fori(0, 30) as b:
                def step(n, ins):
                    ins.then_inc(f_search, 1)
                    dve.wait_ge(f_search, 5 * b + n + 1)

                u = lambda ap: ap.bitcast(U32)
                step(0, dve.tensor_tensor(u(cand), u(thr), u(bit), ALU.bitwise_or))
                step(1, dve.tensor_scalar(u(bit), u(bit), 1, None, ALU.logical_shift_right))
                step(2, dve.tensor_scalar(junk[:], prT[:], cand, 0.0, ALU.is_ge, ALU.add, accum_out=many))
                step(3, dve.scalar_tensor_tensor(out=kept, in0=many, scalar=CAP - 0.5, in1=cand, op0=ALU.is_ge,
                                                 op1=ALU.mult))
                step(4, dve.tensor_tensor(thr, thr, kept, ALU.max))
            dve.tensor_copy(thrB[:], thr.to_broadcast((EXPERTS, TP))).then_inc(f_thr, 1)
            dve.wait_ge(f_prc, 1)
            dve.wait_ge(f_thrturn, 1)
            thr_all = pT[0:TP, 1, 0:EXPERTS].unsqueeze(1).to_broadcast((TP, NT, EXPERTS))
            link(dve.tensor_tensor(equal[:], prC[:], thr_all, ALU.is_equal))
            dve.tensor_tensor(above[:], prC[:], thr_all, ALU.is_gt).then_inc(f_above, 1)
            dve.wait_ge(f_placed, 1)
            link(dve.tensor_copy(passed[:], pT[0:TP, 0, 0:EXPERTS]))
            link(dve.tensor_tensor(place[:], pT[0:TP, 2, 0:8 * NT].rearrange("p (t e) -> p t e", e=EXPERTS),
                                   passed[:].unsqueeze(1).to_broadcast((TP, NT, EXPERTS)), ALU.add))
            link(dve.scalar_tensor_tensor(out=place[:], in0=place[:], scalar=float(CAP), in1=equal[:],
                                          op0=ALU.is_lt, op1=ALU.mult))
            dve.wait_ge(f_above, 1)
            link(dve.tensor_tensor(place[:], place[:], above[:], ALU.add))
            dve.tensor_tensor(gate[:], place[:], prC[:], ALU.mult).then_inc(f_gate, 1)
            dve.wait_ge(f_gate, 1)
            for e in range(EXPERTS):
                for t in range(NT):
                    dve.wait_ge(f_m2, NT * e + t + 1)
                    dve.scalar_tensor_tensor(out=g[:, t, :], in0=pOJ[t % 2][0:TP, :], scalar=gate[:, t, e:e + 1],
                                             in1=g[:, t, :], op0=ALU.mult, op1=ALU.add).then_inc(f_acc, 1)
                if e + 4 < EXPERTS:
                    for i in range(6):
                        hidden_rest(dve, e + 4, i)
            for t in range(NT):
                dve.wait_ge(f_b2, t + 1)
                dve.wait_ge(f_acc, NT * EXPERTS)
                dve.tensor_tensor(g[:, t, :], g[:, t, :], pOJ[t % 2][0:TP, :], ALU.add).then_inc(f_fin, 1)


def kernel(**inputs):
    import concourse.bacc as _bacc
    from concourse.bass_utils import run_bass_kernel_spmd as _run

    nc = _bacc.Bacc("TRN2", target_bir_lowering=False, num_devices=1)
    arrays, args = {}, {}
    for name, a in host_arrays({k: np.asarray(v) for k, v in inputs.items()}).items():
        arrays[f"in_{name}"] = a
        args[name] = nc.dram_tensor(f"in_{name}", a.shape, mybir.dt.from_np(a.dtype), kind="ExternalInput").ap()
    out = nc.dram_tensor("out_0", (N, D), F32, kind="ExternalOutput").ap()
    build(nc, args, out)
    r = _run(nc, [arrays], core_ids=[0])
    return r.results[0]["out_0"]
```

```python
from contextlib import ExitStack

import numpy as np

import concourse.bass as bass
from concourse import mybir

F32 = mybir.dt.float32
F32R = mybir.dt.float32r
BF16 = mybir.dt.bfloat16
I32 = mybir.dt.int32
U32 = mybir.dt.uint32
ALU = mybir.AluOpType
ACT = mybir.ActivationFunctionType
AX = mybir.AxisListType

N = 1250
D = 512
EDGES = 20000
BLOCKS = 4
HEADS = 4
DH = D // HEADS
TP = 125
NT = N // TP
TW = TP + 1
KD = D // 128
CHUNKS = [(0, 500), (500, 500), (1000, 250)]
SW = 418
NPAD = 3 * SW
PAIRS = NT // 2
ET = EDGES // TP
TABLES = 2
TABLE = N * NPAD
GE = 2 * TP
GROUPS = EDGES // GE
PARTS = [(0, 8), (8, 32), (32, GROUPS)]
COND = 16
XM_PARTS = [(0, 2), (2, 5), (5, NT)]
MH, MD = 8, 64
EXPERTS, FF, CAP = 8, 256, 512
BITS = 6
EPS = 1e-5
MASKED = -1e30
NONE = 1e-30
SCALE = float(DH) ** -0.5
TURN = 2.0 * np.pi
TURN_PARTS = [6.28125, 0.0019340515136718750, TURN - 6.28125 - 0.0019340515136718750]
ROUNDER = 1.5 * 2.0 ** 23
PI_BELOW = 3.1415925


def host_arrays(a):
    f = np.float32

    def kpn(w):
        return np.ascontiguousarray(w.reshape(KD, 128, -1).transpose(1, 0, 2).reshape(128, -1))

    g = {k[7:]: v for k, v in a.items() if k.startswith("L0_gnn_")}
    o = {"x": a["x"], "src": a["src"].reshape(80, 250), "dst": a["dst"].reshape(80, 250),
         "noise": a["node_vec1"].reshape(1, N)}
    o["ident"] = np.eye(128, dtype=f)
    freq = np.arange(1, 33, dtype=f) * f(2.0 * np.pi / 16)
    o["freq"] = np.concatenate([freq, freq]).reshape(64, 1)
    o["quarter"] = np.repeat(np.array([[0, 0], [0.25, np.pi / 2]], f), 32, axis=0)
    order = np.where(np.arange(GE)[:, None] < np.arange(GE), f(-256), f(1)).astype(f)
    o["order"] = order.reshape(2, TP, GE).transpose(1, 0, 2)
    o["before"] = np.triu(np.ones((TP, TP), f), 1)
    o["trash"] = np.tile((TABLE + np.arange(TP)).astype(f), (GROUPS, 2))
    blk = np.zeros((128, 128), f)
    blk[:64, :64] = blk[64:, 64:] = 1.0 / N
    o["headmask"] = blk
    o["f_w1"], o["f_b1"] = g["f_w1"], g["f_b1"].reshape(COND, 1)
    w2, b2 = np.zeros((COND, 96), f), np.zeros((96, 1), f)
    for r in (0, 32, 64):
        w2[:, r:r + COND], b2[r:r + COND, 0] = g["f_w2"], g["f_b2"]
        b2[r + COND] = 1.0
    o["f_w2"], o["f_b2"] = w2, b2

    def affine(cols):
        m = np.zeros((96, 3 * D), f)
        for n, (w, b) in enumerate(cols):
            for r in (0, 32, 64):
                if w is not None:
                    m[r:r + COND, n * D:(n + 1) * D] = w
                if b is not None:
                    m[r + COND, n * D:(n + 1) * D] = b
        return m

    o["aff1"] = np.stack([affine([(g["s1_w"][n % 4], g["s1_b"][n % 4]), (g["b1_w"][n % 4], g["b1_b"][n % 4]),
                                  (None, g["m_b2"][n - 1] if n else a["L0_mix_b_out"])]) for n in range(BLOCKS + 1)])
    o["aff2"] = np.stack([affine([(g["s2_w"][n], g["s2_b"][n]), (g["b2_w"][n], g["b2_b"][n]),
                                  (None, g["bo"][n])]) for n in range(BLOCKS)])
    qkv = np.stack([g["wq"], g["wk"], g["wv"]], 1).reshape(BLOCKS, 3, KD, 128, HEADS, DH)
    qkv = qkv.transpose(0, 4, 3, 1, 2, 5).reshape(BLOCKS * HEADS, 128, 3 * KD * DH)
    o["wqkv"] = np.ascontiguousarray(np.concatenate([qkv, qkv[:1]]))
    bias = np.stack([g["bq"], g["bk"], g["bv"], g["m_b1"]], 1).reshape(BLOCKS, 4, 4, 128)
    o["bias"] = np.ascontiguousarray(bias.transpose(0, 3, 1, 2).reshape(BLOCKS, 128, 16))
    o["wo"] = np.stack([kpn(w) for w in g["wo"]])
    o["w1"] = np.stack([kpn(w) for w in g["m_w1"]])
    o["w2"] = np.stack([kpn(w) for w in g["m_w2"]])
    wqkv = a["L0_mix_W_qkv"]
    o["mix_wk"], o["mix_wv"] = kpn(wqkv[D:2 * D].T), kpn(wqkv[2 * D:].T)
    o["mix_wq"] = kpn(wqkv[:D])
    o["mix_wo"] = kpn(a["L0_mix_W_out"].T)
    o["mix_gk"], o["mix_bk"] = a["L0_mix_gamma_K"].reshape(1, D), a["L0_mix_beta_K"].reshape(1, D)
    o["mix_gv"] = a["L0_mix_gamma_V"].reshape(4, 128).T
    o["mix_bv"] = a["L0_mix_beta_V"].reshape(4, 128).T
    wr = np.zeros((D, 128), f)
    wr[:, :EXPERTS] = a["L0_ffn_Wr"]
    o["ffn_wr"] = kpn(wr)
    o["ffn_w1"] = np.stack([kpn(w) for w in a["L0_ffn_W1"]])
    o["ffn_w2"] = np.ascontiguousarray(
        a["L0_ffn_W2"].reshape(EXPERTS, 2, 128, D).transpose(0, 2, 1, 3).reshape(EXPERTS, 128, 2 * D))
    o["ffn_b1"] = a["L0_ffn_b1"].reshape(EXPERTS, 2, 128).transpose(2, 0, 1).reshape(128, 16)
    b2 = np.zeros((96, D), f)
    b2[0:8] = b2[32:40] = b2[64:72] = a["L0_ffn_b2"]
    o["ffn_b2"] = b2
    return {k: np.ascontiguousarray(v) for k, v in o.items()}


def groups_of(n):
    return [range(b, min(b + 4, n)) for b in range(0, n, 4)]


def build(nc, I, out):
    ctx = ExitStack()
    uniq = [0]

    def at(name, shape, dt, addr):
        uniq[0] += 1
        with ExitStack() as s:
            if addr:
                s.enter_context(nc.sbuf_tensor(f"below{uniq[0]}", [128, addr // 4], F32))
            return s.enter_context(nc.sbuf_tensor(name, shape, dt))

    with ctx:
        names = {}

        def sem(name):
            names[name] = ctx.enter_context(nc.semaphore(name))
            return names[name]

        L = at("L", [TP, NT, NPAD], F32, 0)
        ident = at("ident_s", [128, 128], F32, 50176)
        ones = at("ones", [128, 128], F32, 50688)
        condS = at("condS", [96, N + 2], F32R, 51200)
        yT_hi = at("yT_hi", [128, KD, N], F32R, 56224)
        yT_lo = at("yT_lo", [128, KD, N], F32R, 76224)
        diag = at("diag", [TP, 4, TP], F32, 96224)
        rb = at("rb", [128, 250], F32, 98240)
        small = at("small", [128, 256], F32, 99264)
        stage = at("stage", [128, 1536], F32, 100288)
        R = 106432
        mv = small[0:TP, 0:2 * NT].rearrange("p (t s) -> p t s", s=2)
        ve = small[0:TP, 20:30]
        r0 = small[0:TP, 30:40]
        rt = small[0:TP, 40:50]
        rstd = small[0:TP, 50:60]
        st6 = small[0:TP, 60:72].rearrange("p (b s) -> p b s", b=2)
        halves = small[0:TP, 72:82]
        rowmax = small[0:TP, 82:92]
        vh = small[0:TP, 229:239]
        nmr = small[0:TP, 239:249]
        restmax = small[0:TP, 219:229]
        negm = small[0:TP, 92:102]
        den = small[0:TP, 102:112]
        rden = small[0:TP, 112:122]
        dmax = small[0:TP, 122:132]
        lbias = small[:, 132:148]
        fsmall = small[0:64, 148:152]
        fb = small[0:96, 152:154]
        wmean = small[:, 154:218]
        tiny = small[0:TP, 218:219]
        qT_hi = at("qT_hi", [128, N], F32R, R)
        qT_lo = at("qT_lo", [128, N], F32R, R + 5024)
        kT_hi = at("kT_hi", [128, NPAD], F32R, R + 10048)
        kT_lo = at("kT_lo", [128, NPAD], F32R, R + 15072)
        v_hi = at("v_hi", [TP, NT, DH], F32R, R + 20096)
        v_lo = at("v_lo", [TP, NT, DH], F32R, R + 25216)
        Pb = at("Pb", [128, 3, 1256], F32, R + 30336)
        vT = Pb[:, 2, 0:N]
        PT = at("PT", [TP, 2, NT, 250], F32R, R + 45408)
        PT_hi, PT_lo = PT[:, 0], PT[:, 1]
        oT = at("oT", [128, HEADS, N], F32, R + 65408)
        wA_hi = at("wA_hi", [128, 3, KD, DH], F32R, R + 85632)
        wA_lo = at("wA_lo", [128, 3, KD, DH], F32R, R + 91776)
        wo = at("wo_s", [128, KD, D], F32, R)
        aff2_hi = at("aff2_hi", [96, 3 * D], F32R, R + 8192)
        w1_hi = at("w1_hi", [128, KD, D], F32R, R + 20096)
        w1_lo = at("w1_lo", [128, KD, D], F32R, R + 28288)
        xh = at("xh", [TP, D], F32, R + 16384)
        y1 = at("y1", [TP, 2, D], F32, R + 36480)
        g = at("g", [TP, NT, D], F32, R + 44928)
        hT_hi = at("hT_hi", [128, 2, KD, 250], F32R, R)
        hT_lo = at("hT_lo", [128, 2, KD, 250], F32R, R + 65408)
        w2_hi = at("w2_hi", [128, KD, D], F32R, R + 73408)
        w2_lo = at("w2_lo", [128, KD, D], F32R, R + 8192)
        w2_raw = at("w2_raw", [128, KD, D], F32, R + 85632)
        fT = at("fT", [128, 2, 250], F32, R + 81600)
        aff1_hi = at("aff1_hi", [96, 3 * D], F32R, R + 97920)
        order = at("order_s", [TP, 2, GE], F32, 0)
        eqW = at("eqW", [TP, 4, 2, GE], BF16, 2048)
        zrow = at("zrow", [TP, NPAD], F32, 6432)
        trash = at("trash_s", [GROUPS, GE], F32, 11456)
        rowpick = at("rowpick", [TP, 2 * GROUPS], BF16, 12480)
        ident_r = at("ident_r", [GROUPS, GROUPS], F32R, 12800)
        keyR_hi = at("keyR_hi", [GROUPS, GE], F32R, 13120)
        keyR_lo = at("keyR_lo", [GROUPS, GE], F32R, 14144)
        wraw = at("wraw", [128, 2, KD * D], F32, 16384)
        kvs = at("kvs", [TP, 2, D], F32, 32768)
        keyR = at("keyR", [80, 250], F32, R + 97920)
        srcR = at("srcR", [80, 2, 250], I32, R + 98944)
        keyC = at("keyC", [TP, 80, 2], F32, R + 100960)
        cell = at("cell", [GROUPS, GE], F32, R + 101600)
        count = at("count", [GROUPS, GE], F32, R + 102624)
        idxU = at("idxU", [TP, ET], U32, R + 104064)
        cnt = at("cnt", [TP, ET], F32, R + 104704)
        embT = at("embT", [64, N], F32, R + 69504)
        embK = at("embK", [64, N], F32, R + 74528)
        embI = at("embI", [64, N], I32, R + 79552)
        hid = at("hid", [COND, N], F32, R + 84576)
        condF = at("condF", [96, N], F32, R + 89600)
        fw1 = at("fw1", [64, COND], F32, R + 94624)
        fw2 = at("fw2", [COND, 96], F32, R + 94688)
        tab2 = at("tab2", [TP, 3, NPAD], F32, R)
        lnc = at("lnc", [TP, 2, NPAD], F32, R + 32768)
        mask = at("mask", [TP, NPAD], F32, R + 69504)
        xh_p = at("xh_p", [TP, 2, D], F32, R + 74528)
        y1_p = at("y1_p", [TP, 2, D], F32, R + 78624)
        wk_hi = at("wk_hi", [128, KD, D], F32R, R)
        wk_lo = at("wk_lo", [128, KD, D], F32R, R + 8192)
        wv_hi = at("wv_hi", [128, KD, D], F32R, R + 16384)
        wv_lo = at("wv_lo", [128, KD, D], F32R, R + 24576)
        kvh = at("kvh", [TP, 2, 2, D], F32, R + 32768)
        kvq = at("kvq", [TP, 2, D], F32, R + 65408)
        mix_wo = at("mix_wo_s", [128, KD, D], F32, R + 69504)
        mix_wq = at("mix_wq_s", [128, KD, D], F32, R + 77696)
        hmask = at("hmask", [128, 128], F32, R + 87936)
        mrow = at("mrow", [128, 2, D], F32, R + 88448)
        mcol = at("mcol", [128, 4, 4], F32, R + 92544)
        ms8 = at("ms8", [TP, 2, 5, MH], F32, R + 92608)
        pvk = at("pvk", [128, KD, 128], F32, R)
        pvu = at("pvu", [128, KD, 128], F32, R + 2048)
        pvw = at("pvw", [128, KD, D], F32, R + 4096)
        we_hi = at("we_hi", [128, KD, D], F32R, R + 16384)
        we_lo = at("we_lo", [128, KD, D], F32R, R + 24576)
        xr = at("xr", [TP, 2, D], F32, R + 65408)
        hE2_hi = at("hE2_hi", [128, 2, 2, N], F32R, 0)
        hE2_lo = at("hE2_lo", [128, 2, 2, N], F32R, 20000)
        prC = at("prC", [TP, NT, EXPERTS], F32, 40000)
        above = at("above", [TP, NT, EXPERTS], F32, 40320)
        equal = at("equal", [TP, NT, EXPERTS], F32, 40640)
        place = at("place", [TP, NT, EXPERTS], F32, 40960)
        gate = at("gate", [TP, NT, EXPERTS], F32, 41280)
        gateT = at("gateT", [96, N], F32R, 41600)
        thrB = at("thrB", [EXPERTS, TP], F32, 46624)
        passed = at("passed", [TP, EXPERTS], F32, 47136)
        before = at("before_s", [TP, TP], F32, 47168)
        junk = at("junk", [EXPERTS, N], BF16, 41600)
        eW2_lo = at("eW2_lo", [128, 2, D], F32R, 51200)
        xm = at("xm_s", [TP, NT, D], F32, 0)
        sums = at("sums", [TP, NT, 6], F32, R + 12288)
        xn2 = at("xn2", [TP, 2, D], F32, R + 8192)
        fb2 = at("fb2", [96, D], F32, R)
        fb2_hi = at("fb2_hi", [96, D], F32R, R + 2048)
        gate3 = at("gate3", [TP, NT, 96], F32, R + 38240)
        fstat = at("fstat", [128, 32], F32, R + 6144)
        logT = at("logT", [EXPERTS, N], F32, R + 8192)
        prT = at("prT", [EXPERTS, N], F32, R + 13216)
        hE_hi = at("hE_hi", [128, 2, 2, N], F32R, R + 18240)
        wr_hi = at("wr_hi", [128, KD, 128], F32R, R + 38240)
        wr_lo = at("wr_lo", [128, KD, 128], F32R, R + 40288)
        hE_lo = at("hE_lo", [128, 2, 2, N], F32R, R + 65408)
        hF = at("hF", [128, 2, 500], F32, R + 85408)
        eW1_hi = at("eW1_hi", [128, KD, FF], F32R, R + 89408)
        eW1_lo = at("eW1_lo", [128, KD, FF], F32R, R + 93504)
        eW2_hi = at("eW2_hi", [128, 2, D], F32R, R + 97600)

        def first_weights(e):
            ap = (eW2_hi, eW2_lo) if e in (1, 3) else (eW1_hi, eW1_lo)
            return [x[:].rearrange("p a b -> p (a b)").rearrange("p (k f) -> p k f", k=KD) for x in ap]

        def second_weights(e):
            ap = (eW1_hi, eW1_lo) if e in (5, 7) else (eW2_hi, eW2_lo)
            return [x[:].rearrange("p a b -> p (a b)").rearrange("p (k d) -> p k d", k=2) for x in ap]

        def hidden(e):
            return ((hE_hi, hE_lo), (hE2_hi, hE2_lo))[e % 4 // 2][0][:, e % 2], \
                ((hE_hi, hE_lo), (hE2_hi, hE2_lo))[e % 4 // 2][1][:, e % 2]

        pS = ctx.enter_context(nc.psum_tensor("pS", [128, 3, 512], F32))
        pT = ctx.enter_context(nc.psum_tensor("pT", [128, 3, 512], F32))
        pO = ctx.enter_context(nc.psum_tensor("pO", [128, 512], F32))
        pJ = ctx.enter_context(nc.psum_tensor("pJ", [128, 512], F32))
        pOJ = [pJ, pO]

        tabs = [nc.dram_tensor(f"counts{k}", [TABLE + TP, 1], F32).ap() for k in range(TABLES)]
        keys_d = nc.dram_tensor("keys", [80, 250], F32).ap()
        g_d = nc.dram_tensor("g_spill", [N, D], F32).ap()
        xm_d = nc.dram_tensor("x_plus_mix", [N, D], F32).ap()

        ld_x, ld_edge, ld_cond, ld_ident, ld_mix = [sem(n) for n in (
            "ld_x", "ld_edge", "ld_cond", "ld_ident", "ld_mix")]
        zeroed = [sem(f"zeroed{k}") for k in range(TABLES)]
        zrow_set, key_bc, eq_done, edge_sum = [sem(n) for n in ("zrow_set", "keys_broadcast", "eq_done", "edge_sum")]
        w_in, w_cent, w_hi, w_lo = [sem(n) for n in ("weights_in", "weights_centred", "weights_hi", "weights_lo")]
        key_split, cells, cells_turn, kv_sum = [sem(n) for n in ("key_split", "cells", "cells_turned", "kv_sum")]
        aff_hi, nmr_done, xh_done = sem("affine_hi"), sem("nmr_done"), sem("xh_done")
        stage_in, split_done = sem("stage_in"), sem("split_done")
        counted = [sem(f"counted{k}") for k in range(TABLES)]
        const_set, dchain, pchain = sem("const_set"), sem("dve_chain"), sem("pool_chain")
        key_rows, key_turn, key_cols, edge_idx = [sem(n) for n in (
            "key_rows", "key_turned", "key_cols", "edge_idx")]
        emb_arg, emb_sin, hid_mm, hid_act, cond_mm, cond_act, cond_done = [sem(n) for n in (
            "emb_arg", "emb_sin", "hid_mm", "hid_act", "cond_mm", "cond_act", "cond_done")]
        x_ve, x_pow, x_norm, x_turn, x_hi, x_lo = [sem(n) for n in (
            "x_ve", "x_pow", "x_norm", "x_turned", "x_hi", "x_lo")]
        kv_mm, kv_sq, kv_var, kv_std, kv_norm, kv_acc = [sem(n) for n in (
            "kv_mm", "kv_squares", "kv_var", "kv_std", "kv_norm", "kv_acc")]
        pv_ready, pw_mm, pw_out, we_mm, we_h, we_l = [sem(n) for n in (
            "pv_ready", "pw_mm", "pw_out", "we_mm", "we_hi_done", "we_lo_done")]
        mix_mm, mix_add = sem("mix_mm"), sem("mix_add")
        xr_in = [sem(f"xr_in{k}") for k in range(2)]
        xm_out = [sem(f"xm_out{k}") for k in range(2)]
        tab_in = [sem(f"tab_in{k}") for k in range(3)]
        first_in = [sem(f"first_table_in{k}") for k in range(2)]
        l_sum, l_ln, l_done = sem("l_sum"), sem("l_ln"), sem("l_done")
        first_of_block = len(names)
        bstage_in, bsplit = sem("block_stage_in"), sem("block_split")
        bias_in, wo_in, g_out = sem("bias_in"), sem("wo_in"), sem("g_out")
        aff2_copied = sem("aff2_copied")
        w2_in, w2_hi_done, w2_lo_done = sem("w2_in"), sem("w2_hi_done"), sem("w2_lo_done")
        g_in = [sem("g_in0"), sem("g_in1")]
        qk_mm, qk_hi, qk_lo, v_mm, v_act = [sem(n) for n in ("qk_mm", "qk_hi", "qk_lo", "v_mm", "v_act")]
        scores, row_max, neg_max, exp_done, den_inv, diag_done = [sem(n) for n in (
            "scores", "row_max", "neg_max", "exp_done", "den_inverse", "diag_done")]
        turned, turn_hi, turn_lo = sem("turned"), sem("turn_hi"), sem("turn_lo")
        pv_mm, rb_copied, o_done = sem("pv_mm"), sem("rb_copied"), sem("o_done")
        proj, g_add, var_done, half_done, pow_done, aff_mm = [sem(n) for n in (
            "proj", "g_added", "var_done", "half_done", "pow_done", "affine_mm")]
        y_scaled, y_turn, y_hi, y_lo = [sem(n) for n in ("y_scaled", "y_turned", "y_hi", "y_lo")]
        m1_mm, m1_hi, m1_lo = sem("m1_mm"), sem("m1_hi"), sem("m1_lo")
        lchain = sem("dve_block_chain")
        qchain = sem("pool_block_chain")
        cleared = [s.num for s in list(names.values())[first_of_block:]]
        assert cleared == list(range(cleared[0], cleared[-1] + 1))
        cleared = range(cleared[0], cleared[-1] + 1)
        block_done, block_seen, block_go = sem("block_done"), sem("block_seen"), sem("block_go")
        f_in = [sem(f"f_in{k}") for k in range(len(XM_PARTS))]
        f_bn, f_mv = sem("f_bn"), sem("f_mv")
        f_add, f_ve, f_pow, f_norm, f_turn, f_hi, f_lo = [sem(n) for n in (
            "f_added", "f_ve", "f_pow", "f_norm", "f_turned", "f_hi", "f_lo")]
        f_ld, f_stage, f_split, f_log, f_logc, f_nmax, f_exp, f_prob = [sem(n) for n in (
            "f_ld", "f_stage_in", "f_split", "f_logits", "f_logits_out", "f_negmax", "f_exp", "f_prob")]
        f_pturn, f_prc, f_search, f_thr, f_thrturn, f_above, f_placed = [sem(n) for n in (
            "f_pturn", "f_prc", "f_search", "f_threshold", "f_threshold_turned", "f_above", "f_placed")]
        f_m1, f_h, f_hlo, f_m2, f_acc, f_gate, f_gturn, f_gt, f_gtlo, f_b2, f_biased, stored = [sem(n) for n in (
            "f_m1", "f_h", "f_hlo", "f_m2", "f_acc", "f_gate", "f_gturn", "f_gateT", "f_gateT_lo", "f_b2", "f_biased", "stored")]

        class Chain:

            def __init__(self, eng, s):
                self.eng, self.sem, self.n = eng, s, 0

            def link(self, ins):
                self.n += 1
                ins.then_inc(self.sem, 1)
                self.eng.wait_ge(self.sem, self.n)

        block = ctx.enter_context(nc.Block())

        def at_tile(ap, t):
            return ap[:, TP * t:TP * (t + 1)]

        tail_order = [("norm", s) for s in range(NT)] + [("m1", 0), ("norm", NT), ("m1", 1), ("norm", NT + 1)]
        tail_order += [("w2", 0), ("m1", 2), ("m1", 3)]
        for t in range(NT):
            first = 4 * (t // 2 + 1) + 2 * (t % 2)
            tail_order += [("m1", first + m) for m in range(2) if t // 2 + 1 < PAIRS] + [("step", t)]
        tail_order += [("step", NT), ("step", NT + 1)]
        uses = [("m1", i) if k == "m1" else ("proj", i + NT * (k == "step")) for k, i in tail_order
                if k == "m1" or k != "w2" and i < NT]
        use_of = {u: n for n, u in enumerate(uses)}
        (H1, AFF1, H2, H3, AFF2, W1A, W1B, W1C, NQ, NK, NV) = range(11)
        head_piece = {1: H1, 2: H2, 3: H3}

        def turned_tile(G):
            return pT[:, G % 3, 0:KD * TW].rearrange("p (k n) -> p k n", k=KD)[:, :, 0:TP]

        def hidden_rest(eng, e, i):
            m, c = divmod(i, 3)
            c0, cn = CHUNKS[c]
            n = 6 * e + i
            hi, lo = hidden(e)
            eng.wait_ge(f_h, n + 1)
            eng.tensor_tensor(lo[:, m, c0:c0 + cn], hF[:, n % 2, 0:cn], hi[:, m, c0:c0 + cn].bitcast(F32),
                              ALU.subtract).then_inc(f_hlo, 1)

        fpieces = [("r", 0)] + [("1", e) for e in range(4)] + [("2", 0), ("1", 4)]
        for e in range(1, EXPERTS):
            fpieces += [("2", e)] + [("1", e + 4)] * (e + 4 < EXPERTS)
        piece_of = {p: n for n, p in enumerate(fpieces)}

        @block.sync
        def _(sp):
            def stage_load(src, n, s_in, s_split):
                if n:
                    sp.wait_ge(s_split, n)
                sp.dma_start(stage[0:src.shape[0], 0:src.shape[1]], src).then_inc(s_in, 16)

            sp.dma_start(srcR[:, 0, :], I["src"]).then_inc(ld_edge, 16)
            sp.dma_start(srcR[:, 1, :], I["dst"]).then_inc(ld_edge, 16)
            sp.dma_start(ident[:], I["ident"]).then_inc(ld_ident, 16)
            sp.dma_start(order[:], I["order"]).then_inc(ld_edge, 16)
            sp.dma_start(trash[:], I["trash"]).then_inc(ld_edge, 16)

            def counts_of(k):
                return tabs[k][0:TABLE, :].rearrange("(t p c) o -> p t (c o)", t=NT, p=TP)

            def zero(k):
                sp.dma_start(counts_of(k), zrow[:].unsqueeze(1).to_broadcast((TP, NT, NPAD))).then_inc(zeroed[k], 16)
                sp.dma_start(tabs[k][TABLE:, :].rearrange("p o -> o p"), zrow[0:1, 0:TP]).then_inc(zeroed[k], 16)

            sp.wait_ge(zrow_set, 1)
            zero(0)
            sp.dma_start(embT[:], I["noise"].to_broadcast((64, N))).then_inc(ld_cond, 16)
            sp.dma_start(fsmall[:, 0:1], I["freq"]).then_inc(ld_cond, 16)
            sp.dma_start(fsmall[:, 1:3], I["quarter"]).then_inc(ld_cond, 16)
            sp.dma_start(fsmall[0:COND, 3:4], I["f_b1"]).then_inc(ld_cond, 16)
            sp.dma_start(fb[:, 0:1], I["f_b2"]).then_inc(ld_cond, 16)
            sp.dma_start(fw1[:], I["f_w1"]).then_inc(ld_cond, 16)
            sp.dma_start(fw2[:], I["f_w2"]).then_inc(ld_cond, 16)
            zero(1)
            sp.dma_start(g[:], I["x"].rearrange("(t p) d -> p t d", p=TP)).then_inc(ld_x, 16)
            sp.dma_start(wraw[:, 0, :], I["mix_wk"]).then_inc(w_in, 16)
            sp.dma_start(wraw[:, 1, :], I["mix_wv"]).then_inc(w_in, 16)
            stage_load(I["aff1"][0], 0, stage_in, split_done)
            sp.wait_ge(cond_done, 2)
            sp.dma_start(mix_wo[:].rearrange("p k n -> p (k n)"), I["mix_wo"]).then_inc(ld_mix, 16)
            sp.dma_start(mix_wq[:].rearrange("p k n -> p (k n)"), I["mix_wq"]).then_inc(ld_mix, 16)
            sp.dma_start(hmask[:], I["headmask"]).then_inc(ld_mix, 16)
            sp.dma_start(mrow[:, 0, :], I["mix_gk"].to_broadcast((128, D))).then_inc(ld_mix, 16)
            sp.dma_start(mrow[:, 1, :], I["mix_bk"].to_broadcast((128, D))).then_inc(ld_mix, 16)
            sp.dma_start(mcol[:, 0, :], I["mix_gv"]).then_inc(ld_mix, 16)
            sp.dma_start(mcol[:, 1, :], I["mix_bv"]).then_inc(ld_mix, 16)
            sp.wait_ge(x_norm, NT)
            sp.dma_start(g_d.rearrange("(t p) d -> p t d", p=TP), g[:]).then_inc(stored, 16)
            stage_load(I["wqkv"][0], 1, stage_in, split_done)
            sp.wait_ge(kv_acc, NT)
            for t in range(NT + 2):
                if t >= 2:
                    sp.wait_ge(mix_add, t - 1)
                    sp.dma_start(xm_d[TP * (t - 2):TP * (t - 1), :], xr[:, t % 2, :]).then_inc(xm_out[t % 2], 16)
                if t < NT:
                    if t >= 2:
                        sp.wait_ge(xm_out[t % 2], 16 * (t // 2))
                    sp.dma_start(xr[:, t % 2, :], I["x"][TP * t:TP * (t + 1), :]).then_inc(xr_in[t % 2], 16)
                    if t == 0:
                        sp.wait_ge(kv_sum, NT + 1)
                        for k in range(TABLES):
                            sp.wait_ge(counted[k], 16 * (ET // TABLES))
                        for k in range(2):
                            half = slice(k * NT // 2, (k + 1) * NT // 2)
                            sp.dma_start(L[:, half, :], counts_of(0)[:, half, :]).then_inc(first_in[k], 16)
                        sp.wait_ge(we_mm, 4)
                    if t >= 3:
                        sp.wait_ge(l_sum, t - 2)
                    sp.dma_start(tab2[:, t % 3, :], counts_of(1)[:, t, :]).then_inc(tab_in[t % 3], 16)
            sp.wait_ge(stored, 16)
            for k in range(2):
                sp.wait_ge(xm_out[k], 16 * (NT // 2))

            def between(n):
                sp.wait_ge(block_done, 4 * n)
                sp.sem_clear(cleared)
                sp.sem_inc(block_go, 1)

            between(1)
            with sp.Fori(0, BLOCKS) as l:
                def one(name, n=1, off=0):
                    return I[name][bass.ds(n * l + off, 1)].rearrange("a p f -> (a p) f")

                sp.dma_start(lbias[:], one("bias")).then_inc(bias_in, 16)
                stage_load(one("wqkv", HEADS, 1), H1, bstage_in, bsplit)
                stage_load(one("aff1", 1, 1), AFF1, bstage_in, bsplit)
                stage_load(one("wqkv", HEADS, 2), H2, bstage_in, bsplit)
                stage_load(one("wqkv", HEADS, 3), H3, bstage_in, bsplit)
                stage_load(one("aff2"), AFF2, bstage_in, bsplit)
                sp.wait_ge(scores, NT * HEADS)
                sp.dma_start(wo[:].rearrange("p k n -> p (k n)"), one("wo")).then_inc(wo_in, 16)
                sp.dma_start(w2_raw[:].rearrange("p k n -> p (k n)"), one("w2")).then_inc(w2_in, 16)
                stage_load(one("w1")[:, 0:683], W1A, bstage_in, bsplit)
                sp.wait_ge(pv_mm, PAIRS * HEADS)
                gv = g_d.rearrange("(t p) d -> p t d", p=TP)
                sp.dma_start(g[:, 0:2, :], gv[:, 0:2, :]).then_inc(g_in[0], 16)
                sp.dma_start(g[:, 2:NT, :], gv[:, 2:NT, :]).then_inc(g_in[1], 16)
                stage_load(one("w1")[:, 683:1366], W1B, bstage_in, bsplit)
                stage_load(one("w1")[:, 1366:], W1C, bstage_in, bsplit)
                nxt = one("wqkv", HEADS, 4)
                for t in range(NT):
                    if t in (0, 4, 6):
                        j = (0, 4, 6).index(t)
                        stage_load(nxt[:, 512 * j:512 * (j + 1)], NQ + j, bstage_in, bsplit)
                    sp.wait_ge(g_add, NT + t + 1)
                    sp.dma_start(g_d[TP * t:TP * (t + 1), :], g[:, t, :]).then_inc(g_out, 16)
                sp.wait_ge(block_done, 4 * l + 8)
                sp.sem_inc(block_seen, 1)
                sp.wait_ge(g_out, 16 * NT)
                sp.sem_clear(cleared)
                sp.sem_inc(block_go, 1)
            for k, (a, b) in enumerate(XM_PARTS):
                rows = xm_d[TP * a:TP * b, :].rearrange("(t p) d -> p t d", p=TP)
                sp.dma_start(xm[:, a:b, :], rows).then_inc(f_in[k], 16)
            sp.dma_start(fb2[:], I["ffn_b2"]).then_inc(f_ld, 16)
            sp.dma_start(fstat[:, 0:16], I["ffn_b1"]).then_inc(f_ld, 16)
            sp.dma_start(before[:], I["before"]).then_inc(f_ld, 16)
            for n, (kind, e) in enumerate(fpieces):
                stage_load(I["ffn_wr"] if kind == "r" else I["ffn_w1" if kind == "1" else "ffn_w2"][e],
                           n, f_stage, f_split)
            for t in range(NT):
                sp.wait_ge(f_acc, NT * (EXPERTS - 1) + t + 1)
                sp.dma_start(out[TP * t:TP * (t + 1), :], g[:, t, :]).then_inc(stored, 16)
            sp.wait_ge(stored, 16 * (NT + 1))

        @block.gpsimd
        def _(pool):
            ch = outer = Chain(pool, pchain)

            def split(hi, lo, n, s_in, s_done, cols, rows=128):
                pool.wait_ge(s_in, 16 * (n + 1))
                src = stage[0:rows, 0:cols]
                ch.link(pool.tensor_copy(hi, src))
                pool.tensor_tensor(lo, src, hi.bitcast(F32), ALU.subtract).then_inc(s_done, 1)

            def flat(ap, a, b):
                return ap[:].rearrange("p k n -> p (k n)")[:, a:b]

            def rsqrt(dst, src, n, s_in, n_in, s_out):
                pool.wait_ge(s_in, n_in)
                pool.tensor_tensor(dst, src, halves[:, 0:n], ALU.pow).then_inc(s_out, 1)

            def ln_pow(base, t):
                rsqrt(r0[:, t:t + 1], ve[:, t:t + 1], 1, var_done, base + t + 1, pow_done)

            def all_counted(groups):
                for k in range(TABLES):
                    pool.wait_ge(counted[k], 32 * ((groups + TABLES - 1 - k) // TABLES))

            for r in range(GROUPS):
                k = r % TABLES
                starts = [a for a, _ in PARTS]
                if r in starts:
                    pool.wait_ge(edge_idx, starts.index(r) + 1)
                if r < TABLES:
                    pool.wait_ge(zeroed[k], 32)
                else:
                    pool.wait_ge(counted[k], 32 * (r // TABLES))
                for T in (2 * r, 2 * r + 1):
                    pool.indirect_dma_start(tabs[k], bass.IndirectOffsetOnAxis(ap=idxU[:, T:T + 1], axis=0),
                                            cnt[:, T:T + 1], None, compute_op=ALU.add,
                                            bounds_check=TABLE + TP - 1).then_inc(counted[k], 16)
            all_counted(GROUPS)
            for t in range(NT):
                pool.wait_ge(first_in[2 * t // NT], 16)
                pool.wait_ge(tab_in[t % 3], 16 * (t // 3 + 1))
                pool.tensor_tensor(L[:, t, :], L[:, t, :], tab2[:, t % 3, :], ALU.add).then_inc(l_sum, 1)
                if t in (3, 5, 7):
                    j = (3, 5, 7).index(t)
                    if j == 0:
                        pool.wait_ge(stage_in, 32)
                        pool.wait_ge(we_mm, 4)
                    cols = slice(512 * j, 512 * (j + 1))
                    hi, lo = [ap[:].rearrange("p w k n -> p (w k n)")[:, cols] for ap in (wA_hi, wA_lo)]
                    ch.link(pool.tensor_copy(hi, stage[:, cols]))
                    ch.link(pool.tensor_tensor(lo, stage[:, cols], hi.bitcast(F32), ALU.subtract))
            wA = lambda ap, a, b: ap[:].rearrange("p w k n -> p (w k n)")[:, a:b]
            pool.drain().then_inc(block_done, 1)
            pool.wait_ge(block_go, 1)
            with pool.Fori(0, BLOCKS) as l:
                ch = Chain(pool, qchain)

                def third(hi, lo, n, j, rows=128):
                    if j == 0:
                        pool.wait_ge(bstage_in, 16 * (n + 1))
                    cols = slice(512 * j, 512 * (j + 1))
                    ch.link(pool.tensor_copy(hi[:, cols], stage[0:rows, cols]))
                    if rows == 128:
                        ins = pool.tensor_tensor(lo[:, cols], stage[:, cols], hi[:, cols].bitcast(F32), ALU.subtract)
                    else:
                        low = hi[64:96, cols]
                        ins = pool.tensor_tensor(low, stage[64:96, cols], low.bitcast(F32), ALU.subtract)
                    if j == 2:
                        ins.then_inc(bsplit, 1)
                        pool.wait_ge(bsplit, n + 1)
                    else:
                        ch.link(ins)

                def diagonals(h, p):
                    q = PAIRS * h + p
                    pool.wait_ge(den_inv, q + 1)
                    if q >= 2:
                        pool.wait_ge(pv_mm, q - 1)
                    for i in (2 * p, 2 * p + 1):
                        pool.tensor_scalar(diag[:, i % 4, :], ident[0:TP, 0:TP], rden[:, i:i + 1], None, ALU.mult
                                           ).then_inc(diag_done, 1)

                for h in range(HEADS):
                    for i in range(NT):
                        if h < 3 and i < 3:
                            if i == 0:
                                pool.wait_ge(v_mm, 3 * (h + 1))
                            third(wA(wA_hi, 0, 1536), wA(wA_lo, 0, 1536), head_piece[h + 1], i)
                        elif h == 0 and 6 <= i < 9:
                            third(aff1_hi, None, AFF1, i - 6, 96)
                        if i % 2:
                            diagonals(h, i // 2)
                pool.wait_ge(pv_mm, PAIRS * HEADS)
                split(flat(w1_hi, 0, 683), flat(w1_lo, 0, 683), W1A, bstage_in, bsplit, 683)
                for t in range(NT):
                    ln_pow(0, t)
                    if t in (3, 6):
                        n, a = (W1B, 683) if t == 3 else (W1C, 1366)
                        b = min(a + 683, 2048)
                        split(flat(w1_hi, a, b), flat(w1_lo, a, b), n, bstage_in, bsplit, b - a)
                for t in range(NT):
                    ln_pow(NT, t)
                    if t in (3, 5, 7):
                        j = (3, 5, 7).index(t)
                        split(wA(wA_hi, 512 * j, 512 * (j + 1)), wA(wA_lo, 512 * j, 512 * (j + 1)),
                              NQ + j, bstage_in, bsplit, 512)
                pool.drain().then_inc(block_done, 1)
                pool.wait_ge(block_go, l + 2)
            ch = outer
            rsqrt(r0, ve, NT, f_ve, 1, f_pow)
            split(wr_hi[:].rearrange("p k n -> p (k n)"), wr_lo[:].rearrange("p k n -> p (k n)"),
                  0, f_stage, f_split, 512)

            def split_expert(w, e, place):
                hi, lo = [ap.rearrange("p k n -> p (k n)") for ap in place]
                split(hi, lo, piece_of[(w, e)], f_stage, f_split, 1024)

            for e in range(4):
                if e >= 2:
                    pool.wait_ge(f_m1, 6 * (e - 1))
                split_expert("1", e, first_weights(e))
                if e:
                    for i in range(6):
                        hidden_rest(pool, e - 1, i)
            for i in range(6):
                hidden_rest(pool, 3, i)
            pool.wait_ge(f_m1, 24)
            split_expert("2", 0, second_weights(0))
            split_expert("1", 4, first_weights(4))
            for e in range(1, EXPERTS):
                if e <= 4:
                    pool.wait_ge(f_m2, NT * e)
                elif e == 5:
                    pool.wait_ge(f_m1, 6 * EXPERTS)
                else:
                    pool.wait_ge(f_m2, NT * (e - 1))
                split_expert("2", e, second_weights(e))
                if e + 4 < EXPERTS:
                    pool.wait_ge(f_m1, 6 * (e + 4))
                    split_expert("1", e + 4, first_weights(e + 4))

        @block.tensor
        def _(pe):
            def mm3(dst, lhs, rhs, first, last):
                (lh, ll), (rh, rl) = lhs, rhs
                pe.matmul(dst, lh, rh, start=first, stop=False)
                pe.matmul(dst, lh, rl, start=False, stop=False)
                return pe.matmul(dst, ll, rh, start=False, stop=last)

            def turn(dst, src):
                for k in range(KD):
                    mm = pe.transpose(dst[:, TW * k:TW * k + TP], src[:, 128 * k:128 * (k + 1)], ident[0:TP, 0:TP])
                return mm

            def y_tile(k, t):
                return at_tile(yT_hi[:, k, :], t), at_tile(yT_lo[:, k, :], t)

            def affine(aff, G, t):
                if G >= 2:
                    pe.wait_ge(y_scaled, G - 1)
                pe.matmul(pS[0:TP, G % 2, :], at_tile(condS, t), aff[:, 0:D], start=True, stop=True
                          ).then_inc(aff_mm, 1)

            def ln_turn(aff, G, t, src=y1):
                pe.wait_ge(y_scaled, G + 1)
                if G >= 3:
                    pe.wait_ge(y_lo, G - 2)
                for k in range(KD):
                    cols = slice(128 * k, 128 * (k + 1))
                    pe.transpose(pT[:, G % 3, TW * k:TW * k + TP], src[:, t % 2, cols], ident[0:TP, 0:TP])
                    mm = pe.matmul(pT[:, G % 3, TW * k:TW * (k + 1)], aff[:, D + 128 * k:D + 128 * (k + 1)],
                                   condS[:, TP * t:TP * t + TW], start=False, stop=True, skip_group_check=True)
                mm.then_inc(y_turn, 1)

            pe.wait_ge(ld_ident, 16)
            pe.wait_ge(key_rows, 1)
            for b in range(2):
                pe.transpose(pOJ[b][0:TP, 0:80], keyR[:, TP * b:TP * (b + 1)], ident[0:80, 0:80]).then_inc(key_turn, 1)
            pe.wait_ge(key_cols, 2)
            pe.wait_ge(key_split, 2)

            def edge_groups(lo, hi):
                for r in range(lo, hi + 2):
                    if r < hi:
                        if r >= 3:
                            pe.wait_ge(eq_done, r - 2)
                        pick = ident_r[:, r:r + 1].to_broadcast((GROUPS, TP))
                        pe.matmul(pS[0:TP, r % 3, 0:GE], pick, keyR_hi[:], start=True, stop=False)
                        pe.matmul(pS[0:TP, r % 3, 0:GE], pick, keyR_lo[:], start=False, stop=True).then_inc(key_bc, 1)
                    if r - 2 >= lo:
                        q = r - 2
                        pe.wait_ge(eq_done, q + 1)
                        for b in range(2):
                            mm = pe.matmul(pO[0:GROUPS, 0:GE], rowpick[:, GROUPS - q:2 * GROUPS - q], eqW[:, q % 4, b, :],
                                           start=(q == lo and b == 0), stop=(q == hi - 1 and b == 1))
                        mm.then_inc(edge_sum, 1)
                pe.wait_ge(cells, [a for a, _ in PARTS].index(lo) + 1)
                for n, rows in enumerate((cell, count)):
                    for b in range(2):
                        mm = pe.transpose(pJ[0:TP, GROUPS * (2 * n + b):GROUPS * (2 * n + b + 1)],
                                          rows[:, TP * b:TP * (b + 1)], ident[0:GROUPS, 0:GROUPS])
                mm.then_inc(cells_turn, 1)

            edge_groups(*PARTS[0])
            pe.wait_ge(ld_cond, 16 * 7)
            pe.wait_ge(emb_sin, 1)
            for c, (c0, cn) in enumerate(CHUNKS):
                pe.matmul(pT[0:COND, c, 0:cn], fw1[:], embT[:, c0:c0 + cn], start=True, stop=True).then_inc(hid_mm, 1)
            edge_groups(*PARTS[1])
            for c, (c0, cn) in enumerate(CHUNKS):
                pe.wait_ge(hid_act, c + 1)
                pe.matmul(pT[0:96, c, 0:cn], fw2[:], hid[:, c0:c0 + cn], start=True, stop=True).then_inc(cond_mm, 1)
            edge_groups(*PARTS[2])
            pe.wait_ge(cond_act, 3)
            for t in range(NT):
                pe.wait_ge(x_norm, t + 1)
                if t >= 3:
                    pe.wait_ge(x_lo, t - 2)
                turn(pT[:, t % 3, :], g[:, t, :]).then_inc(x_turn, 1)
            pe.wait_ge(w_lo, 2)
            pe.wait_ge(edge_idx, len(PARTS))

            def kv_products(t):
                pe.wait_ge(kv_norm, t + 1)
                k, v = kvh[:, t % 2, 0, :], kvh[:, t % 2, 1, :]
                for p in range(4):
                    cols = slice(128 * p, 128 * (p + 1))
                    mm = pe.matmul(pT[:, 0, cols], v[:, cols], k[:, cols], start=(t == 0 and p == 0),
                                   stop=(t == NT - 1), skip_group_check=True)
                mm.then_inc(kv_acc, 1)

            for t in range(NT):
                pe.wait_ge(x_lo, t + 1)
                if t >= 2:
                    pe.wait_ge(kv_norm, t - 1)
                for k in range(KD):
                    mm3(pS[0:TP, t % 2, :], y_tile(k, t), (wk_hi[:, k, :], wk_lo[:, k, :]), k == 0, k == KD - 1)
                for k in range(KD):
                    mm = mm3(pOJ[t % 2][0:TP, :], y_tile(k, t), (wv_hi[:, k, :], wv_lo[:, k, :]), k == 0, k == KD - 1)
                mm.then_inc(kv_mm, 1)
                if t == 0:
                    pe.wait_ge(x_lo, NT)
                if t:
                    kv_products(t - 1)
            kv_products(NT - 1)
            pe.wait_ge(kv_sum, NT)
            pe.matmul(pT[:, 2, :], ones[0:TP, :], kvs[:, 0, :], start=True, stop=True)
            for p in range(4):
                mm = pe.matmul(pT[:, 1, p:p + 1], kvs[:, 1, 128 * p:128 * (p + 1)], ones[0:TP, 0:1],
                               start=True, stop=True)
            mm.then_inc(kv_sum, 1)
            banks4 = [pS[:, 0, :], pS[:, 1, :], pS[:, 2, :], pJ[:, :]]
            pe.wait_ge(ld_mix, 16 * 7)
            pe.wait_ge(pv_ready, 1)
            for p in range(4):
                pe.matmul(banks4[p], pvk[:, p, :], mix_wo[:, p, :], start=True, stop=True).then_inc(pw_mm, 1)
            for m in range(4):
                pe.wait_ge(pw_out, 4)
                for p in range(4):
                    mm = pe.matmul(banks4[m], mix_wq[:, p, 128 * m:128 * (m + 1)], pvw[:, p, :],
                                   start=(p == 0), stop=(p == 3))
                mm.then_inc(we_mm, 1)
            pe.wait_ge(we_l, 4)
            pe.wait_ge(cond_done, 2)
            pe.wait_ge(split_done, 1)
            for s in range(NT + 2):
                if s < NT:
                    if s >= 2:
                        pe.wait_ge(mix_add, s - 1)
                    dst = pOJ[s % 2][0:TP, :]
                    pe.matmul(dst, at_tile(condS, s), aff1_hi[:, 2 * D:], start=True, stop=False)
                    for k in range(KD):
                        mm = mm3(dst, y_tile(k, s), (we_hi[:, k, :], we_lo[:, k, :]), False, k == KD - 1)
                    mm.then_inc(mix_mm, 1)
                if 1 <= s <= NT:
                    affine(aff1_hi, s - 1, s - 1)
                if s >= 2:
                    ln_turn(aff1_hi, s - 2, s - 2, y1_p)
            pe.drain().then_inc(block_done, 1)
            pe.wait_ge(block_go, 1)

            with pe.Fori(0, BLOCKS) as l:
                def qk_group(h, n):
                    w, c = divmod(n, 3)
                    c0, cn = CHUNKS[c]
                    if w == 1:
                        pe.wait_ge(qk_lo, 6 * h + c + 1)
                    elif h and c == 0:
                        pe.wait_ge(bsplit, head_piece[h] + 1)
                        pe.wait_ge(row_max, 2 * NT * h)
                    for k in range(KD):
                        mm = mm3(pS[:, c, 0:cn], (wA_hi[:, w, k, :], wA_lo[:, w, k, :]),
                                 (yT_hi[:, k, c0:c0 + cn], yT_lo[:, k, c0:c0 + cn]), k == 0, k == KD - 1)
                    mm.then_inc(qk_mm, 1)

                def v_group(h, c):
                    c0, cn = CHUNKS[c]
                    if c < 2 and h:
                        last = max(q for q in range(PAIRS * h) if q % 2 == c)
                        pe.wait_ge(o_done, last + 1)
                    if c == 2 or h:
                        pe.wait_ge(v_act, 3 * h + (1 if c == 2 else 0))
                    for k in range(KD):
                        mm = mm3(pOJ[c % 2][:, 0:cn], (wA_hi[:, 2, k, :], wA_lo[:, 2, k, :]),
                                 (yT_hi[:, k, c0:c0 + cn], yT_lo[:, k, c0:c0 + cn]), k == 0, k == KD - 1)
                    mm.then_inc(v_mm, 1)

                def score(h, i):
                    if i == 0:
                        pe.wait_ge(qk_lo, 6 * h + 6)
                    for c in range(3):
                        if i and c < 2:
                            pe.wait_ge(row_max, 2 * (NT * h + i) - 1 + c)
                        cols = slice(SW * c, SW * (c + 1))
                        mm = mm3(pS[0:TP, c, 0:SW], (at_tile(qT_hi, i), at_tile(qT_lo, i)),
                                 (kT_hi[:, cols], kT_lo[:, cols]), True, True)
                    mm.then_inc(scores, 1)

                def turn_v(h):
                    pe.wait_ge(v_act, 3 * h + 3)
                    for j, ts in enumerate(groups_of(NT)):
                        if h:
                            pe.wait_ge(turn_lo, 33 * h + j - 2)
                        for t in ts:
                            mm = pe.transpose(pT[0:TP, j, 128 * (t % 4):128 * (t % 4 + 1)],
                                              at_tile(vT, t), ident[:, :])
                        mm.then_inc(turned, 1)

                def turn_p(h, i):
                    pe.wait_ge(exp_done, NT * h + i + 1)
                    for j, bs in enumerate(groups_of(NT)):
                        G = 33 * h + 3 + 3 * i + j
                        pe.wait_ge(turn_lo, G - 2)
                        for b in bs:
                            mm = pe.transpose(pT[0:TP, j, TP * (b % 4):TP * (b % 4 + 1)],
                                              at_tile(Pb[0:TP, i % 3, :], b), ident[0:TP, 0:TP])
                        mm.then_inc(turned, 1)

                def pv(h, p):
                    q = PAIRS * h + p
                    bank_q = pOJ[q % 2]
                    if q >= 2:
                        pe.wait_ge(o_done, q - 1)
                    if p == 0:
                        pe.wait_ge(v_act, 3 * h + 3)
                    for b in range(NT):
                        if b % 4 == 0:
                            pe.wait_ge(turn_lo, 33 * h + 7 + 6 * p + b // 4)
                        mm3(bank_q[:, 0:250], (v_hi[:, b, :], v_lo[:, b, :]), (PT_hi[:, b, :], PT_lo[:, b, :]),
                            b == 0, b == NT - 1)
                    pe.wait_ge(diag_done, NT * h + 2 * p + 2)
                    for u in range(2):
                        mm = pe.matmul(bank_q[:, 250 + TP * u:250 + TP * (u + 1)], ones[0:TP, :],
                                       diag[:, (2 * p + u) % 4, :], start=True, stop=True)
                    mm.then_inc(pv_mm, 1)

                for c in range(3):
                    qk_group(0, c)
                for h in range(HEADS):
                    for c in range(3):
                        qk_group(h, 3 + c)
                    v_group(h, 0)
                    score(h, 0)
                    v_group(h, 1)
                    v_group(h, 2)
                    score(h, 1)
                    turn_v(h)
                    for i in range(2, NT):
                        score(h, i)
                        if i >= 4 and i % 2 == 0:
                            pv(h, i // 2 - 2)
                        turn_p(h, i - 2)
                    nxt = [lambda c=c: qk_group(h + 1, c) for c in range(3)] if h + 1 < HEADS else [lambda: None] * 3
                    nxt[0]()
                    pv(h, 3)
                    turn_p(h, 8)
                    nxt[1]()
                    turn_p(h, 9)
                    nxt[2]()
                    pv(h, 4)

                def bank(use):
                    n = use_of[use]
                    if n >= 2:
                        kind, i = uses[n - 2]
                        pe.wait_ge(m1_hi if kind == "m1" else g_add, i + 1)
                    return pOJ[n % 2]

                def out_proj(t):
                    if t == 0:
                        pe.wait_ge(o_done, PAIRS * HEADS)
                        pe.wait_ge(wo_in, 16)
                        pe.wait_ge(bsplit, AFF2 + 1)
                    dst = bank(("proj", t))[0:TP, :]
                    pe.matmul(dst, at_tile(condS, t), aff2_hi[:, 2 * D:], start=True, stop=False)
                    for k in range(KD):
                        mm = pe.matmul(dst, at_tile(oT[:, k, :], t), wo[:, k, :], start=False, stop=(k == KD - 1))
                    mm.then_inc(proj, 1)

                def mlp_out(t):
                    c, u = divmod(t, 2)
                    if t == 0:
                        pe.wait_ge(w2_lo_done, 1)
                    pe.wait_ge(m1_lo, 4 * (c + 1))
                    dst = bank(("proj", NT + t))[0:TP, :]
                    pe.matmul(dst, at_tile(condS, t), aff1_hi[:, 2 * D:], start=True, stop=False)
                    for k in range(KD):
                        mm = mm3(dst, (at_tile(hT_hi[:, c % 2, k, :], u), at_tile(hT_lo[:, c % 2, k, :], u)),
                                 (w2_hi[:, k, :], w2_lo[:, k, :]), False, k == KD - 1)
                    mm.then_inc(proj, 1)

                def mlp_in(i):
                    c, m = divmod(i, 4)
                    if i == 0:
                        pe.wait_ge(bsplit, W1C + 1)
                    pe.wait_ge(y_lo, 2 * c + 2)
                    dst = bank(("m1", i))[:, 0:250]
                    cols, nodes = slice(128 * m, 128 * (m + 1)), slice(250 * c, 250 * (c + 1))
                    for k in range(KD):
                        mm = mm3(dst, (w1_hi[:, k, cols], w1_lo[:, k, cols]),
                                 (yT_hi[:, k, nodes], yT_lo[:, k, nodes]), k == 0, k == KD - 1)
                    mm.then_inc(m1_mm, 1)

                for kind, i in tail_order:
                    if kind == "m1":
                        mlp_in(i)
                    elif kind in ("norm", "step"):
                        base, aff = (0, aff2_hi) if kind == "norm" else (NT, aff1_hi)
                        if i < NT:
                            (out_proj if kind == "norm" else mlp_out)(i)
                        if 1 <= i <= NT:
                            affine(aff, base + i - 1, i - 1)
                        if i >= 2:
                            ln_turn(aff, base + i - 2, i - 2)
                pe.drain().then_inc(block_done, 1)
                pe.wait_ge(block_go, l + 2)

            for t in range(NT):
                pe.wait_ge(f_norm, t + 1)
                if t >= 3:
                    pe.wait_ge(f_lo, t - 2)
                turn(pT[:, t % 3, :], xn2[:, t % 2, :]).then_inc(f_turn, 1)
            pe.wait_ge(f_split, 1)
            pe.wait_ge(f_lo, NT)
            for c, (c0, cn) in enumerate(CHUNKS):
                for k in range(KD):
                    mm = mm3(pS[:, c, 0:cn], (wr_hi[:, k, :], wr_lo[:, k, :]),
                             (yT_hi[:, k, c0:c0 + cn], yT_lo[:, k, c0:c0 + cn]), k == 0, k == KD - 1)
                mm.then_inc(f_log, 1)

            def expert_in(e):
                pe.wait_ge(f_split, piece_of[("1", e)] + 1)
                w_hi_e, w_lo_e = first_weights(e)
                for i in range(6):
                    m, c = divmod(i, 3)
                    c0, cn = CHUNKS[c]
                    n = 6 * e + i
                    if n < 3:
                        pe.wait_ge(f_logc, c + 1)
                    else:
                        pe.wait_ge(f_h, n - 2)
                    cols = slice(128 * m, 128 * (m + 1))
                    for k in range(KD):
                        mm = mm3(pS[:, c, 0:cn], (w_hi_e[:, k, cols], w_lo_e[:, k, cols]),
                                 (yT_hi[:, k, c0:c0 + cn], yT_lo[:, k, c0:c0 + cn]), k == 0, k == KD - 1)
                    mm.then_inc(f_m1, 1)

            def expert_out(e):
                pe.wait_ge(f_hlo, 6 * e + 6)
                pe.wait_ge(f_split, piece_of[("2", e)] + 1)
                hi, lo = hidden(e)
                w_hi_e, w_lo_e = second_weights(e)
                for t in range(NT):
                    n = NT * e + t
                    if n >= 2:
                        pe.wait_ge(f_acc, n - 1)
                    for k in range(2):
                        mm = mm3(pOJ[t % 2][0:TP, :],
                                 (at_tile(hi[:, k, :], t), at_tile(lo[:, k, :], t)),
                                 (w_hi_e[:, k, :], w_lo_e[:, k, :]), k == 0, k == 1)
                    mm.then_inc(f_m2, 1)

            expert_in(0)
            pe.wait_ge(f_prob, 1)
            for t in range(NT):
                mm = pe.transpose(pT[0:TP, 0, 8 * t:8 * (t + 1)], at_tile(prT, t), ident[0:8, 0:8])
            mm.then_inc(f_pturn, 1)
            for e in (1, 2, 3):
                expert_in(e)
            pe.wait_ge(f_thr, 1)
            pe.transpose(pT[0:TP, 1, 0:EXPERTS], thrB[:], ident[0:EXPERTS, 0:EXPERTS]).then_inc(f_thrturn, 1)
            pe.wait_ge(f_above, 1)
            pe.wait_ge(f_ld, 48)
            total = pT[0:TP, 0, 0:EXPERTS]
            for t in range(NT):
                pe.matmul(total, ones[0:TP, 0:TP], above[:, t, :], start=(t == 0), stop=(t == NT - 1))
            pe.matmul(pT[0:TP, 2, 0:8 * NT], before[:], equal[:].rearrange("p t e -> p (t e)"), start=True, stop=False,
                      skip_group_check=True)
            for t in range(NT - 1):
                mm = pe.matmul(pT[0:TP, 2, 8 * (t + 1):8 * NT], ones[0:TP, 0:TP],
                               equal[:, t, :].unsqueeze(1).to_broadcast((TP, NT - 1 - t, EXPERTS)),
                               start=False, stop=(t == NT - 2), skip_group_check=True)
            mm.then_inc(f_placed, 1)
            expert_out(0)
            expert_in(4)
            pe.wait_ge(f_gate, 4)
            for t in range(NT):
                mm = pe.transpose(pT[0:96, t // 4, TP * (t % 4):TP * (t % 4 + 1)], gate3[:, t, :], ident[0:TP, 0:TP])
            mm.then_inc(f_gturn, 1)
            expert_out(1)
            pe.wait_ge(f_gtlo, 2)
            pe.wait_ge(f_acc, 2 * NT)
            for t in range(NT):
                if t >= 2:
                    pe.wait_ge(f_biased, t - 1)
                pe.matmul(pOJ[t % 2][0:TP, :], at_tile(gateT, t), fb2_hi[:], start=True, stop=True).then_inc(f_b2, 1)
            expert_in(5)
            pe.wait_ge(f_biased, NT)
            for e in range(2, EXPERTS):
                expert_out(e)
                if e + 4 < EXPERTS:
                    expert_in(e + 4)

        @block.scalar
        def _(act):
            A = nc.scalar.activation
            act.wait_ge(emb_arg, 1)
            A(embT[:], embT[:], ACT.Sin).then_inc(emb_sin, 1)
            for c, (c0, cn) in enumerate(CHUNKS):
                act.wait_ge(hid_mm, c + 1)
                A(hid[:, c0:c0 + cn], pT[0:COND, c, 0:cn], ACT.Silu, bias=fsmall[0:COND, 3:4]).then_inc(hid_act, 1)
            for c, (c0, cn) in enumerate(CHUNKS):
                act.wait_ge(cond_mm, c + 1)
                A(condF[:, c0:c0 + cn], pT[0:96, c, 0:cn], ACT.Identity, bias=fb[:, 0:1]).then_inc(cond_act, 1)

            def hi_tile(G, t, s_in, s_out):
                act.wait_ge(s_in, G + 1)
                A(yT_hi[:, :, TP * t:TP * (t + 1)], turned_tile(G), ACT.Copy).then_inc(s_out, 1)

            act.wait_ge(x_ve, 1)
            A(rt, ve, ACT.Sqrt).then_inc(x_pow, 1)
            for n, hi in enumerate((wk_hi, wv_hi)):
                act.wait_ge(w_cent, n + 1)
                A(hi[:].rearrange("p k n -> p (k n)"), wraw[:, n, :], ACT.Copy).then_inc(w_hi, 1)
            for t in range(NT):
                hi_tile(t, t, x_turn, x_hi)
            act.wait_ge(stage_in, 16)
            act.wait_ge(edge_idx, len(PARTS))
            A(aff1_hi[:], stage[0:96, :], ACT.Copy).then_inc(aff_hi, 1)
            act.wait_ge(var_done, 1)
            A(rt, ve, ACT.Sqrt).then_inc(pow_done, 1)
            for t in range(NT):
                act.wait_ge(kv_mm, t + 1)
                if t:
                    act.wait_ge(kv_var, t)
                A(kvq[:, 0, :], pS[0:TP, t % 2, :], ACT.Square)
                A(kvq[:, 1, :], pOJ[t % 2][0:TP, :], ACT.Square).then_inc(kv_sq, 1)
                act.wait_ge(kv_var, t + 1)
                A(ms8[:, :, 2, :], ms8[:, :, 1, :], ACT.Sqrt).then_inc(kv_std, 1)
            for p in range(4):
                act.wait_ge(pw_mm, p + 1)
                A(pvw[:, p, :], (pS[:, p, :] if p < 3 else pJ[:, :]), ACT.Copy).then_inc(pw_out, 1)
            for m in range(4):
                act.wait_ge(we_mm, m + 1)
                A(we_hi[:, m, :], (pS[:, m, :] if m < 3 else pJ[:, :]), ACT.Copy).then_inc(we_h, 1)

            for s in range(NT + 2):
                if s >= 2:
                    hi_tile(s - 2, s - 2, y_turn, y_hi)
                if s < NT:
                    if s == 0:
                        act.wait_ge(we_mm, 4)
                        act.wait_ge(nmr_done, 1)
                    if s >= 2:
                        act.wait_ge(y_scaled, s - 1)
                    A(xh_p[:, s % 2, :], g[:, s, :], ACT.Identity, bias=nmr[:, s:s + 1], scale=rstd[:, s:s + 1]
                      ).then_inc(xh_done, 1)
                    act.wait_ge(l_sum, s + 1)
                    if s >= 2:
                        act.wait_ge(l_done, s - 1)
                    A(lnc[:, s % 2, :], L[:, s, :], ACT.Ln, bias=tiny).then_inc(l_ln, 1)
            act.drain().then_inc(block_done, 1)
            act.wait_ge(block_go, 1)

            with act.Fori(0, BLOCKS) as l:
                act.wait_ge(bias_in, 16)

                def qk_out(h, n):
                    w, c = divmod(n, 3)
                    c0, cn = CHUNKS[c]
                    act.wait_ge(qk_mm, 6 * h + n + 1)
                    dst = (qT_hi, kT_hi)[w][:, c0:c0 + cn]
                    A(dst, pS[:, c, 0:cn], ACT.Identity, bias=lbias[:, 4 * w + h:4 * w + h + 1]).then_inc(qk_hi, 1)

                def v_out(h, c):
                    c0, cn = CHUNKS[c]
                    act.wait_ge(v_mm, 3 * h + c + 1)
                    A(vT[:, c0:c0 + cn], pOJ[c % 2][:, 0:cn], ACT.Identity, bias=lbias[:, 8 + h:9 + h]).then_inc(v_act, 1)

                def exp(h, i):
                    act.wait_ge(neg_max, NT * h + i + 1)
                    p = Pb[0:TP, i % 3, 0:N]
                    A(p, p, ACT.Exp, bias=negm[:, i:i + 1], scale=SCALE, accum_out=den[:, i:i + 1]).then_inc(exp_done, 1)

                def v_turned(h):
                    for j, ts in enumerate(groups_of(NT)):
                        act.wait_ge(turned, 33 * h + j + 1)
                        n = len(ts)
                        A(v_hi[:, ts[0]:ts[0] + n, :], pT[0:TP, j, 0:128 * n].rearrange("p (t d) -> p t d", d=128),
                          ACT.Copy).then_inc(turn_hi, 1)

                def p_turned(h, i):
                    for j, bs in enumerate(groups_of(NT)):
                        act.wait_ge(turned, 33 * h + 4 + 3 * i + j)
                        n, u = len(bs), TP * (i % 2)
                        A(PT_hi[:, bs[0]:bs[0] + n, u:u + TP],
                          pT[0:TP, j, 0:TP * n].rearrange("p (b s) -> p b s", s=TP), ACT.Copy).then_inc(turn_hi, 1)

                def rden_out(h, p):
                    act.wait_ge(pv_mm, PAIRS * h + p + 1)
                    if h or p:
                        act.wait_ge(o_done, PAIRS * h + p)
                    A(rb[:], pOJ[(PAIRS * h + p) % 2][:, 250:500], ACT.Copy).then_inc(rb_copied, 1)

                for c in range(3):
                    qk_out(0, c)
                for h in range(HEADS):
                    for c in range(3):
                        qk_out(h, 3 + c)
                    for c in range(3):
                        v_out(h, c)
                    exp(h, 0)
                    v_turned(h)
                    exp(h, 1)
                    for i in range(2, NT):
                        if i >= 4 and i % 2 == 0:
                            exp(h, i)
                            rden_out(h, i // 2 - 2)
                            p_turned(h, i - 2)
                        else:
                            p_turned(h, i - 2)
                            exp(h, i)
                    more = h + 1 < HEADS
                    if more:
                        qk_out(h + 1, 0)
                    rden_out(h, 3)
                    p_turned(h, 8)
                    if more:
                        qk_out(h + 1, 1)
                    p_turned(h, 9)
                    if more:
                        qk_out(h + 1, 2)
                    else:
                        act.wait_ge(bstage_in, 16 * (AFF2 + 1))
                        act.wait_ge(scores, NT * HEADS)
                        A(aff2_hi[:], stage[0:96, :], ACT.Copy).then_inc(aff2_copied, 1)
                    rden_out(h, 4)
                for kind, i in tail_order:
                    if kind == "w2":
                        act.wait_ge(w2_in, 16)
                        act.wait_ge(proj, NT)
                        A(w2_hi[:], w2_raw[:], ACT.Copy).then_inc(w2_hi_done, 1)
                    elif kind == "norm":
                        if i >= 2:
                            hi_tile(i - 2, i - 2, y_turn, y_hi)
                    elif kind == "m1":
                        c, m = divmod(i, 4)
                        src = pOJ[use_of[("m1", i)] % 2][:, 0:250]
                        act.wait_ge(m1_mm, i + 1)
                        if i >= 2:
                            act.wait_ge(m1_lo, i - 1)
                        if c >= 2 and m == 0:
                            act.wait_ge(proj, NT + 2 * (c - 1))
                        A(fT[:, i % 2, :], src, ACT.Relu, bias=lbias[:, 12 + m:13 + m])
                        A(hT_hi[:, c % 2, m, :], src, ACT.Relu, bias=lbias[:, 12 + m:13 + m]).then_inc(m1_hi, 1)
                    elif i >= 2:
                        hi_tile(NT + i - 2, i - 2, y_turn, y_hi)
                act.drain().then_inc(block_done, 1)
                act.wait_ge(block_go, l + 2)

            for t in range(NT):
                hi_tile(t, t, f_turn, f_hi)
            for c, (c0, cn) in enumerate(CHUNKS):
                act.wait_ge(f_log, c + 1)
                A(logT[:, c0:c0 + cn], pS[0:EXPERTS, c, 0:cn], ACT.Copy).then_inc(f_logc, 1)
            act.wait_ge(f_nmax, 1)
            A(prT[:], logT[:], ACT.Exp, bias=fstat[0:EXPERTS, 16:17], accum_out=fstat[0:EXPERTS, 17:18]).then_inc(f_exp, 1)
            act.wait_ge(f_ld, 48)

            def expert_act(e):
                for i in range(6):
                    m, c = divmod(i, 3)
                    c0, cn = CHUNKS[c]
                    n = 6 * e + i
                    act.wait_ge(f_m1, n + 1)
                    if n >= 2:
                        act.wait_ge(f_hlo, n - 1)
                    if i == 0 and e >= 4:
                        act.wait_ge(f_m2, NT * (e - 3))
                    b = fstat[:, 2 * e + m:2 * e + m + 1]
                    A(hF[:, n % 2, 0:cn], pS[:, c, 0:cn], ACT.Gelu, bias=b)
                    A(hidden(e)[0][:, m, c0:c0 + cn], pS[:, c, 0:cn], ACT.Gelu, bias=b).then_inc(f_h, 1)

            expert_act(0)
            act.wait_ge(f_pturn, 1)
            A(prC[:].rearrange("p t e -> p (t e)"), pT[0:TP, 0, 0:8 * NT], ACT.Copy).then_inc(f_prc, 1)
            for e in range(1, EXPERTS):
                expert_act(e)
                if e == 4:
                    act.wait_ge(f_gturn, 1)
                    A(fb2_hi[:], fb2[:], ACT.Copy)
                    for c, (c0, cn) in enumerate(CHUNKS):
                        ins = A(gateT[:, c0:c0 + cn], pT[0:96, c, 0:cn], ACT.Copy)
                    ins.then_inc(f_gt, 1)

        @block.vector
        def _(dve):
            ch = outer = Chain(dve, dchain)
            link = ch.link

            def newton(r, r_in, v, tmp):
                link(dve.tensor_tensor(tmp, r_in, r_in, ALU.mult))
                link(dve.tensor_tensor(tmp, tmp, v, ALU.mult))
                link(dve.tensor_scalar(tmp, tmp, -0.5, 1.5, ALU.mult, ALU.add))
                link(dve.tensor_tensor(r, r_in, tmp, ALU.mult))

            def lo_tile(G, t, s_in, s_out):
                dve.wait_ge(s_in, G + 1)
                cols = slice(TP * t, TP * (t + 1))
                dve.tensor_tensor(yT_lo[:, :, cols], turned_tile(G), yT_hi[:, :, cols].bitcast(F32), ALU.subtract).then_inc(s_out, 1)

            dve.memset(zrow[:], 0.0).then_inc(zrow_set, 1)
            dve.memset(halves, -0.5).then_inc(const_set, 1)
            dve.memset(ones[:], 1.0).then_inc(const_set, 1)
            dve.memset(tiny, NONE).then_inc(const_set, 1)
            link(dve.memset(rowpick[:], 0.0))
            link(dve.memset(rowpick[:, GROUPS:GROUPS + 1], 1.0))
            dve.wait_ge(ld_ident, 16)
            link(dve.tensor_copy(ident_r[:], ident[0:GROUPS, 0:GROUPS]))
            dve.wait_ge(ld_edge, 64)
            dve.scalar_tensor_tensor(out=keyR[:], in0=srcR[:, 0, :], scalar=float(NPAD), in1=srcR[:, 1, :],
                                     op0=ALU.mult, op1=ALU.add).then_inc(key_rows, 1)
            dve.wait_ge(key_rows, 1)
            dve.tensor_copy(keyR_hi[:], keyR[:]).then_inc(key_split, 1)
            dve.wait_ge(key_split, 1)
            dve.tensor_tensor(keyR_lo[:], keyR[:], keyR_hi[:].bitcast(F32), ALU.subtract).then_inc(key_split, 1)
            for b in range(2):
                dve.wait_ge(key_turn, b + 1)
                dve.tensor_copy(keyC[:, :, b], pOJ[b][0:TP, 0:80]).then_inc(key_cols, 1)
            dve.wait_ge(key_cols, 2)
            def edge_groups(lo, hi):
                for r in range(lo, hi):
                    dve.wait_ge(key_bc, r + 1)
                    if r >= 4:
                        dve.wait_ge(edge_sum, r - 3)
                    for b in range(2):
                        ins = dve.scalar_tensor_tensor(out=eqW[:, r % 4, b, :], in0=pS[0:TP, r % 3, 0:GE],
                                                       scalar=keyC[:, r, b:b + 1], in1=order[:, b, :],
                                                       op0=ALU.is_equal, op1=ALU.mult)
                    ins.then_inc(eq_done, 1)
                n = [a for a, _ in PARTS].index(lo) + 1
                dve.wait_ge(edge_sum, hi)
                link(dve.tensor_scalar(cell[:], pO[0:GROUPS, 0:GE], 0.0, None, ALU.is_gt))
                link(dve.tensor_tensor(count[:], keyR[:], trash[:], ALU.subtract))
                link(dve.tensor_tensor(cell[:], cell[:], count[:], ALU.mult))
                link(dve.tensor_tensor(cell[:], cell[:], trash[:], ALU.add))
                dve.tensor_copy(count[:], pO[0:GROUPS, 0:GE]).then_inc(cells, 1)
                dve.wait_ge(cells_turn, n)
                turned = pJ[0:TP, 0:4 * GROUPS].rearrange("p (n b r) -> p n r b", n=2, b=2)
                link(dve.tensor_copy(cnt[:, 2 * lo:2 * hi].rearrange("p (r b) -> p r b", b=2), turned[:, 1, lo:hi, :]))
                dve.tensor_copy(idxU[:, 2 * lo:2 * hi].rearrange("p (r b) -> p r b", b=2), turned[:, 0, lo:hi, :]
                                ).then_inc(edge_idx, 1)

            edge_groups(*PARTS[0])
            dve.wait_ge(ld_cond, 16 * 7)
            link(dve.tensor_scalar(embT[:], embT[:], fsmall[:, 0:1], None, ALU.mult))
            link(dve.tensor_scalar(embK[:], embT[:], 1.0 / TURN, fsmall[:, 1:2], ALU.mult, ALU.add))
            link(dve.tensor_scalar(embK[:], embK[:], ROUNDER, None, ALU.add))
            link(dve.tensor_scalar(embK[:], embK[:], -ROUNDER, None, ALU.add))
            for part in TURN_PARTS:
                link(dve.scalar_tensor_tensor(out=embT[:], in0=embK[:], scalar=-part, in1=embT[:],
                                              op0=ALU.mult, op1=ALU.add))
            link(dve.tensor_scalar(embT[:], embT[:], fsmall[:, 2:3], PI_BELOW, ALU.add, ALU.min))
            dve.tensor_scalar(embT[:], embT[:], -PI_BELOW, None, ALU.max).then_inc(emb_arg, 1)
            edge_groups(*PARTS[1])
            dve.wait_ge(ld_x, 16)

            def stats(t, src):
                link(dve.bn_stats(st6[:, t % 2, :], src))
                link(dve.bn_aggr(mv[:, t, :], st6[:, t % 2, :]))

            for t in range(NT):
                stats(t, g[:, t, :])
            dve.tensor_scalar(ve, mv[:, :, 1], EPS, None, ALU.add).then_inc(x_ve, 1)
            dve.wait_ge(cond_act, 3)
            link(dve.memset(condS[:, N:].bitcast(F32), 0.0))
            dve.tensor_copy(condS[:, 0:N], condF[:]).then_inc(cond_done, 1)
            dve.wait_ge(cond_done, 1)
            dve.tensor_tensor(condS[32:64, 0:N], condF[32:64, :], condS[32:64, 0:N].bitcast(F32), ALU.subtract
                              ).then_inc(cond_done, 1)
            edge_groups(*PARTS[2])
            dve.wait_ge(w_in, 32)
            for n in range(2):
                part = wraw[:, n, :].rearrange("p (h d) -> p h d", d=MD)
                mean = wmean[:, 32 * n:32 * (n + 1)]
                link(dve.tensor_reduce(mean, part, AX.X, ALU.add))
                link(dve.tensor_scalar(mean, mean, 1.0 / MD, None, ALU.mult))
                dve.tensor_tensor(part, part, mean.unsqueeze(2).to_broadcast((128, 32, MD)), ALU.subtract
                                  ).then_inc(w_cent, 1)
            for n, (hi, lo) in enumerate(((wk_hi, wk_lo), (wv_hi, wv_lo))):
                dve.wait_ge(w_hi, n + 1)
                dve.tensor_tensor(lo[:].rearrange("p k n -> p (k n)"), wraw[:, n, :],
                                  hi[:].rearrange("p k n -> p (k n)").bitcast(F32), ALU.subtract).then_inc(w_lo, 1)
            dve.wait_ge(x_pow, 1)
            link(dve.reciprocal(r0, rt))
            newton(rstd, r0, ve, rt)
            for t in range(NT):
                dve.tensor_scalar(g[:, t, :], g[:, t, :], mv[:, t, 0:1], rstd[:, t:t + 1], ALU.subtract, ALU.mult
                                  ).then_inc(x_norm, 1)
                if t >= 1:
                    lo_tile(t - 1, t - 1, x_hi, x_lo)
            lo_tile(NT - 1, NT - 1, x_hi, x_lo)
            dve.wait_ge(x_norm, NT)
            for t in range(NT):
                stats(t, g[:, t, :])
            dve.tensor_scalar(ve, mv[:, :, 1], EPS, None, ALU.add).then_inc(var_done, 1)
            dve.wait_ge(aff_hi, 1)
            dve.tensor_tensor(aff1_hi[64:96, :], stage[64:96, :], aff1_hi[64:96, :].bitcast(F32), ALU.subtract
                              ).then_inc(split_done, 1)
            by_head = lambda ap: ap.rearrange("p (h d) -> p h d", h=MH)
            wide = lambda ap: ap.unsqueeze(2).to_broadcast((TP, MH, MD))
            for t in range(NT):
                src = [pS[0:TP, t % 2, :], pOJ[t % 2][0:TP, :]]
                dve.wait_ge(kv_sq, t + 1)
                for w in range(2):
                    link(dve.tensor_reduce(ms8[:, w, 1, :], by_head(kvq[:, w, :]), AX.X, ALU.add))
                dve.tensor_scalar(ms8[:, :, 1, :], ms8[:, :, 1, :], 1.0 / MD, EPS, ALU.mult, ALU.add).then_inc(kv_var, 1)
                dve.wait_ge(kv_std, t + 1)
                link(dve.reciprocal(ms8[:, :, 3, :], ms8[:, :, 2, :]))
                newton(ms8[:, :, 4, :], ms8[:, :, 3, :], ms8[:, :, 1, :], ms8[:, :, 2, :])
                if t >= 2:
                    dve.wait_ge(kv_acc, t - 1)
                link(dve.tensor_tensor(by_head(kvh[:, t % 2, 0, :]), by_head(src[0]), wide(ms8[:, 0, 4, :]), ALU.mult))
                dve.tensor_tensor(by_head(kvh[:, t % 2, 1, :]), by_head(src[1]), wide(ms8[:, 1, 4, :]), ALU.mult
                                  ).then_inc(kv_norm, 1)
                dve.wait_ge(kv_norm, t + 1)
                if t == 0:
                    dve.tensor_copy(kvs[:], kvh[:, 0]).then_inc(kv_sum, 1)
                else:
                    dve.wait_ge(kv_sum, t)
                    dve.tensor_tensor(kvs[:], kvs[:], kvh[:, t % 2], ALU.add).then_inc(kv_sum, 1)
            dve.wait_ge(ld_mix, 16 * 7)
            dve.wait_ge(kv_acc, NT)
            dve.wait_ge(kv_sum, NT + 1)
            gk, bk = mrow[:, 0, :], mrow[:, 1, :]
            row = lambda ap: ap[:].rearrange("p k n -> p (k n)")
            for p in range(4):
                link(dve.tensor_scalar(pvk[:, p, :], pT[:, 0, 128 * p:128 * (p + 1)], mcol[:, 0, p:p + 1], None, ALU.mult))
            link(dve.tensor_tensor(row(pvk), row(pvk), gk, ALU.mult))
            link(dve.tensor_tensor(row(pvu), pT[:, 2, :], gk, ALU.mult))
            link(dve.scalar_tensor_tensor(out=row(pvu), in0=bk, scalar=float(N), in1=row(pvu), op0=ALU.mult, op1=ALU.add))
            link(dve.tensor_tensor(mcol[:, 2, :], pT[:, 1, 0:4], mcol[:, 0, :], ALU.mult))
            for p in range(4):
                link(dve.scalar_tensor_tensor(out=pvk[:, p, :], in0=pvu[:, p, :], scalar=mcol[:, 1, p:p + 1],
                                              in1=pvk[:, p, :], op0=ALU.mult, op1=ALU.add))
                link(dve.scalar_tensor_tensor(out=pvk[:, p, :], in0=bk[:, 128 * p:128 * (p + 1)],
                                              scalar=mcol[:, 2, p:p + 1], in1=pvk[:, p, :], op0=ALU.mult, op1=ALU.add))
            dve.tensor_tensor(pvk[:], pvk[:], hmask[:].unsqueeze(1).to_broadcast((128, 4, 128)), ALU.mult
                              ).then_inc(pv_ready, 1)
            for m in range(4):
                dve.wait_ge(we_h, m + 1)
                dve.tensor_tensor(we_lo[:, m, :], (pS[:, m, :] if m < 3 else pJ[:, :]), we_hi[:, m, :].bitcast(F32),
                                  ALU.subtract).then_inc(we_l, 1)

            def ln_stats(base, s):
                link(dve.bn_stats(st6[:, s % 2, :], g[:, s, :]))
                link(dve.bn_aggr(mv[:, s, :], st6[:, s % 2, :]))
                dve.tensor_scalar(ve[:, s:s + 1], mv[:, s, 1:2], EPS, None, ALU.add).then_inc(var_done, 1)
                dve.tensor_scalar(vh[:, s:s + 1], mv[:, s, 1:2], EPS, -0.5, ALU.add, ALU.mult).then_inc(half_done, 1)

            def scale_tile(G, t, src, dst):
                dve.wait_ge(aff_mm, G + 1)
                if G >= 2:
                    dve.wait_ge(y_turn, G - 1)
                dve.scalar_tensor_tensor(out=dst[:, t % 2, :], in0=pS[0:TP, G % 2, :], scalar=1.0, in1=src,
                                         op0=ALU.add, op1=ALU.mult).then_inc(y_scaled, 1)

            def ln_finish(base, s):
                if 1 <= s <= NT:
                    t, G = s - 1, base + s - 1
                    c = slice(t, t + 1)
                    dve.wait_ge(pow_done, G + 1)
                    dve.wait_ge(half_done, G + 1)
                    link(dve.scalar_tensor_tensor(out=rt[:, c], in0=r0[:, c], scalar=vh[:, c], in1=r0[:, c],
                                                  op0=ALU.mult, op1=ALU.mult))
                    link(dve.scalar_tensor_tensor(out=rstd[:, c], in0=rt[:, c], scalar=1.5, in1=r0[:, c],
                                                  op0=ALU.add, op1=ALU.mult))
                    if G:
                        dve.wait_ge(y_scaled, G)
                    link(dve.tensor_scalar(xh[:], g[:, t, :], mv[:, t, 0:1], rstd[:, c], ALU.subtract, ALU.mult))
                    scale_tile(G, t, xh[:], y1)
                if s >= 2:
                    lo_tile(base + s - 2, s - 2, y_hi, y_lo)

            dve.wait_ge(pow_done, 1)
            link(dve.reciprocal(r0, rt))
            dve.wait_ge(var_done, 1)
            newton(rstd, r0, ve, rt)
            dve.scalar_tensor_tensor(out=nmr, in0=mv[:, :, 0], scalar=-1.0, in1=rstd, op0=ALU.mult, op1=ALU.mult
                                     ).then_inc(nmr_done, 1)
            for t in range(NT + 2):
                if t < NT:
                    dve.wait_ge(xr_in[t % 2], 16 * (t // 2 + 1))
                    dve.wait_ge(mix_mm, t + 1)
                    dve.tensor_tensor(xr[:, t % 2, :], xr[:, t % 2, :], pOJ[t % 2][0:TP, :], ALU.add).then_inc(mix_add, 1)
                if 1 <= t <= NT:
                    dve.wait_ge(xh_done, t)
                    scale_tile(t - 1, t - 1, xh_p[:, (t - 1) % 2, :], y1_p)
                if t >= 2:
                    lo_tile(t - 2, t - 2, y_hi, y_lo)
                if t < NT:
                    dve.wait_ge(l_ln, t + 1)
                    if t:
                        dve.wait_ge(l_done, t)
                    link(dve.tensor_scalar(mask[:], lnc[:, t % 2, :], 0.0, MASKED / float(np.log(NONE)), ALU.min, ALU.mult))
                    dve.scalar_tensor_tensor(out=L[:, t, :], in0=lnc[:, t % 2, :], scalar=1.0 / SCALE, in1=mask[:],
                                             op0=ALU.mult, op1=ALU.add).then_inc(l_done, 1)
            dve.wait_ge(l_done, NT)
            dve.drain().then_inc(block_done, 1)
            dve.wait_ge(block_go, 1)

            with dve.Fori(0, BLOCKS) as l:
                ch = Chain(dve, lchain)
                link = ch.link
                link(dve.memset(kT_hi[:, N:NPAD].bitcast(F32), 0.0))
                link(dve.memset(kT_lo[:, N:NPAD].bitcast(F32), 0.0))
                dve.wait_ge(bias_in, 16)

                def qk_rest(h, n):
                    w, c = divmod(n, 3)
                    c0, cn = CHUNKS[c]
                    dve.wait_ge(qk_hi, 6 * h + n + 1)
                    hi, lo = ((qT_hi, qT_lo), (kT_hi, kT_lo))[w]
                    dve.scalar_tensor_tensor(out=lo[:, c0:c0 + cn], in0=pS[:, c, 0:cn],
                                             scalar=lbias[:, 4 * w + h:4 * w + h + 1],
                                             in1=hi[:, c0:c0 + cn].bitcast(F32), op0=ALU.add, op1=ALU.subtract
                                             ).then_inc(qk_lo, 1)

                def masked_max(h, i):
                    dve.wait_ge(scores, NT * h + i + 1)
                    if i >= 3:
                        dve.wait_ge(turned, 33 * h + 3 * i - 3)
                    elif i == 2:
                        dve.wait_ge(turned, 33 * h + 3)
                    elif i == 0 and h:
                        dve.wait_ge(turned, 33 * h)
                    for banks, most in ((slice(0, 1), rowmax), (slice(1, 3), restmax)):
                        dve.tensor_tensor_reduce(
                            out=Pb[0:TP, i % 3, 0:NPAD].rearrange("p (c n) -> p c n", c=3)[:, banks, :],
                            in0=pS[0:TP, banks, 0:SW], in1=L[:, i, :].rearrange("p (c n) -> p c n", c=3)[:, banks, :],
                            scale=1.0, scalar=0.1 * MASKED, op0=ALU.add, op1=ALU.max, accum_out=most[:, i:i + 1]
                            ).then_inc(row_max, 1)
                    dve.wait_ge(row_max, 2 * (NT * h + i + 1))
                    dve.tensor_scalar(negm[:, i:i + 1], rowmax[:, i:i + 1], restmax[:, i:i + 1], -SCALE, ALU.max, ALU.mult
                                      ).then_inc(neg_max, 1)

                def inverses(h, p):
                    both = slice(2 * p, 2 * p + 2)
                    dve.wait_ge(exp_done, NT * h + 2 * p + 2)
                    if p < 2 and h:
                        dve.wait_ge(diag_done, NT * h)
                    link(dve.tensor_scalar(dmax[:, both], den[:, both], 1e-30, None, ALU.max))
                    dve.reciprocal(rden[:, both], dmax[:, both]).then_inc(den_inv, 1)

                def v_rest(h):
                    for j, ts in enumerate(groups_of(NT)):
                        dve.wait_ge(turn_hi, 33 * h + j + 1)
                        n = len(ts)
                        dve.tensor_tensor(v_lo[:, ts[0]:ts[0] + n, :],
                                          pT[0:TP, j, 0:128 * n].rearrange("p (t d) -> p t d", d=128),
                                          v_hi[:, ts[0]:ts[0] + n, :].bitcast(F32), ALU.subtract).then_inc(turn_lo, 1)

                def p_rest(h, i):
                    for j, bs in enumerate(groups_of(NT)):
                        dve.wait_ge(turn_hi, 33 * h + 4 + 3 * i + j)
                        n, u = len(bs), TP * (i % 2)
                        dst = (slice(None), slice(bs[0], bs[0] + n), slice(u, u + TP))
                        dve.tensor_tensor(PT_lo[dst], pT[0:TP, j, 0:TP * n].rearrange("p (b s) -> p b s", s=TP),
                                          PT_hi[dst].bitcast(F32), ALU.subtract).then_inc(turn_lo, 1)

                def o_out(h, p):
                    dve.wait_ge(rb_copied, PAIRS * h + p + 1)
                    dve.tensor_tensor(oT[:, h, 250 * p:250 * (p + 1)], pOJ[(PAIRS * h + p) % 2][:, 0:250], rb[:],
                                      ALU.mult).then_inc(o_done, 1)

                for c in range(3):
                    qk_rest(0, c)
                for h in range(HEADS):
                    for c in range(3):
                        qk_rest(h, 3 + c)
                    masked_max(h, 0)
                    masked_max(h, 1)
                    v_rest(h)
                    for i in range(2, NT):
                        masked_max(h, i)
                        if i >= 4 and i % 2 == 0:
                            o_out(h, i // 2 - 2)
                        p_rest(h, i - 2)
                        if i % 2 == 0:
                            inverses(h, i // 2 - 1)
                    more = h + 1 < HEADS
                    if more:
                        qk_rest(h + 1, 0)
                    o_out(h, 3)
                    p_rest(h, 8)
                    inverses(h, 4)
                    if more:
                        qk_rest(h + 1, 1)
                    p_rest(h, 9)
                    if more:
                        qk_rest(h + 1, 2)
                    else:
                        dve.wait_ge(aff2_copied, 1)
                        dve.tensor_tensor(aff2_hi[64:96, :], stage[64:96, :], aff2_hi[64:96, :].bitcast(F32),
                                          ALU.subtract).then_inc(bsplit, 1)
                    o_out(h, 4)

                def g_sum(G, s):
                    dve.wait_ge(proj, G + 1)
                    if G == 0:
                        dve.wait_ge(g_in[0], 16)
                    if G == 2:
                        dve.wait_ge(g_in[1], 16)
                    dve.tensor_tensor(g[:, s, :], g[:, s, :], pOJ[use_of[("proj", G)] % 2][0:TP, :], ALU.add
                                      ).then_inc(g_add, 1)
                    dve.wait_ge(g_add, G + 1)

                for kind, i in tail_order:
                    if kind == "w2":
                        dve.wait_ge(w2_hi_done, 1)
                        dve.wait_ge(y_turn, NT)
                        dve.tensor_tensor(w2_lo[:], w2_raw[:], w2_hi[:].bitcast(F32), ALU.subtract
                                          ).then_inc(w2_lo_done, 1)
                    elif kind == "m1":
                        c, m = divmod(i, 4)
                        dve.wait_ge(m1_hi, i + 1)
                        dve.tensor_tensor(hT_lo[:, c % 2, m, :], fT[:, i % 2, :], hT_hi[:, c % 2, m, :].bitcast(F32),
                                          ALU.subtract).then_inc(m1_lo, 1)
                    else:
                        base = 0 if kind == "norm" else NT
                        if i < NT:
                            g_sum(base + i, i)
                            ln_stats(base, i)
                        ln_finish(base, i)
                dve.drain().then_inc(block_done, 1)
                dve.wait_ge(block_go, l + 2)

            ch = outer
            link = ch.link
            for s in range(NT + 2):
                if s < NT:
                    part = [a <= s < b for a, b in XM_PARTS].index(True)
                    dve.wait_ge(f_in[part], 16)
                    dve.tensor_tensor(g[:, s, :], g[:, s, :], xm[:, s, :], ALU.add).then_inc(f_add, 1)
                if 1 <= s <= NT:
                    dve.wait_ge(f_add, s)
                    dve.bn_stats(sums[:, s - 1, :], g[:, s - 1, :]).then_inc(f_bn, 1)
                if s >= 2:
                    dve.wait_ge(f_bn, s - 1)
                    dve.bn_aggr(mv[:, s - 2, :], sums[:, s - 2, :]).then_inc(f_mv, 1)
            dve.wait_ge(f_mv, NT)
            dve.tensor_scalar(ve, mv[:, :, 1], EPS, None, ALU.add).then_inc(f_ve, 1)
            dve.wait_ge(f_pow, 1)
            dve.wait_ge(f_ve, 1)
            newton(rstd, r0, ve, rt)
            for t in range(NT):
                if t >= 2:
                    dve.wait_ge(f_turn, t - 1)
                dve.tensor_scalar(xn2[:, t % 2, :], g[:, t, :], mv[:, t, 0:1], rstd[:, t:t + 1], ALU.subtract, ALU.mult
                                  ).then_inc(f_norm, 1)
                if t >= 1:
                    lo_tile(t - 1, t - 1, f_hi, f_lo)
            lo_tile(NT - 1, NT - 1, f_hi, f_lo)
            dve.wait_ge(f_ld, 48)
            dve.wait_ge(f_logc, 3)
            link(dve.tensor_reduce(fstat[0:EXPERTS, 18:19], logT[:], AX.X, ALU.max))
            dve.tensor_scalar(fstat[0:EXPERTS, 16:17], fstat[0:EXPERTS, 18:19], -1.0, None, ALU.mult).then_inc(f_nmax, 1)
            dve.wait_ge(f_exp, 1)
            link(dve.reciprocal(fstat[0:EXPERTS, 19:20], fstat[0:EXPERTS, 17:18]))
            dve.tensor_scalar(prT[:], prT[:], fstat[0:EXPERTS, 19:20], None, ALU.mult).then_inc(f_prob, 1)
            thr, cand, kept, bit, many = [fstat[0:EXPERTS, 20 + n:21 + n] for n in range(5)]
            link(dve.memset(thr, 0.0))
            link(dve.memset(bit, 2.0 ** -63))
            with dve.Fori(0, 30 // BITS) as b:
                def step(n, ins):
                    ins.then_inc(f_search, 1)
                    dve.wait_ge(f_search, (4 * BITS + 1) * b + n + 1)

                u = lambda ap: ap.bitcast(U32)
                for j in range(BITS):
                    step(4 * j, dve.scalar_tensor_tensor(out=u(cand), in0=u(bit), scalar=j, in1=u(thr),
                                                         op0=ALU.logical_shift_right, op1=ALU.bitwise_or))
                    step(4 * j + 1, dve.tensor_scalar(junk[:], prT[:], cand, 0.0, ALU.is_ge, ALU.add, accum_out=many))
                    step(4 * j + 2, dve.scalar_tensor_tensor(out=kept, in0=many, scalar=CAP - 0.5, in1=cand,
                                                             op0=ALU.is_ge, op1=ALU.mult))
                    step(4 * j + 3, dve.tensor_tensor(thr, thr, kept, ALU.max))
                step(4 * BITS, dve.tensor_scalar(u(bit), u(bit), BITS, None, ALU.logical_shift_right))
            dve.tensor_copy(thrB[:], thr.to_broadcast((EXPERTS, TP))).then_inc(f_thr, 1)
            dve.wait_ge(f_prc, 1)
            dve.wait_ge(f_thrturn, 1)
            thr_all = pT[0:TP, 1, 0:EXPERTS].unsqueeze(1).to_broadcast((TP, NT, EXPERTS))
            link(dve.tensor_tensor(equal[:], prC[:], thr_all, ALU.is_equal))
            dve.tensor_tensor(above[:], prC[:], thr_all, ALU.is_gt).then_inc(f_above, 1)
            dve.wait_ge(f_placed, 1)
            link(dve.tensor_copy(passed[:], pT[0:TP, 0, 0:EXPERTS]))
            link(dve.tensor_tensor(place[:], pT[0:TP, 2, 0:8 * NT].rearrange("p (t e) -> p t e", e=EXPERTS),
                                   passed[:].unsqueeze(1).to_broadcast((TP, NT, EXPERTS)), ALU.add))
            link(dve.scalar_tensor_tensor(out=place[:], in0=place[:], scalar=float(CAP), in1=equal[:],
                                          op0=ALU.is_lt, op1=ALU.mult))
            dve.wait_ge(f_above, 1)
            link(dve.tensor_tensor(place[:], place[:], above[:], ALU.add))
            dve.tensor_tensor(gate[:], place[:], prC[:], ALU.mult).then_inc(f_gate, 1)
            dve.wait_ge(f_gate, 1)
            dve.wait_ge(f_log, 3)
            link(dve.memset(gate3[:], 0.0))
            for r in (0, 32, 64):
                dve.tensor_copy(gate3[:, :, r:r + EXPERTS], gate[:]).then_inc(f_gate, 1)
            for e in range(EXPERTS):
                for t in range(NT):
                    dve.wait_ge(f_m2, NT * e + t + 1)
                    dve.scalar_tensor_tensor(out=g[:, t, :], in0=pOJ[t % 2][0:TP, :], scalar=gate[:, t, e:e + 1],
                                             in1=g[:, t, :], op0=ALU.mult, op1=ALU.add).then_inc(f_acc, 1)
                if e == 1:
                    dve.wait_ge(f_gt, 1)
                    for c, (c0, cn) in enumerate(CHUNKS):
                        low = gateT[32:64, c0:c0 + cn]
                        ins = dve.tensor_tensor(low, pT[32:64, c, 0:cn], low.bitcast(F32), ALU.subtract)
                    ins.then_inc(f_gtlo, 1)
                    dve.tensor_tensor(fb2_hi[64:96, :], fb2[64:96, :], fb2_hi[64:96, :].bitcast(F32), ALU.subtract
                                      ).then_inc(f_gtlo, 1)
                    for t in range(NT):
                        dve.wait_ge(f_b2, t + 1)
                        dve.tensor_tensor(g[:, t, :], g[:, t, :], pOJ[t % 2][0:TP, :], ALU.add).then_inc(f_biased, 1)
                if e + 4 < EXPERTS:
                    for i in range(6):
                        hidden_rest(dve, e + 4, i)


def kernel(**inputs):
    import concourse.bacc as _bacc
    from concourse.bass_utils import run_bass_kernel_spmd as _run

    nc = _bacc.Bacc("TRN2", target_bir_lowering=False, num_devices=1)
    arrays, args = {}, {}
    for name, a in host_arrays({k: np.asarray(v) for k, v in inputs.items()}).items():
        arrays[f"in_{name}"] = a
        args[name] = nc.dram_tensor(f"in_{name}", a.shape, mybir.dt.from_np(a.dtype), kind="ExternalInput").ap()
    out = nc.dram_tensor("out_0", (N, D), F32, kind="ExternalOutput").ap()
    build(nc, args, out)
    r = _run(nc, [arrays], core_ids=[0])
    return r.results[0]["out_0"]
```
